# Optimizing a Trainium2 kernel written in Bass

```python
import numpy as np
import jax
import jax.numpy as jnp

def _softmax(x, axis=-1):
    return jax.nn.softmax(x, axis=axis)

def _gelu(x):
    return jax.nn.gelu(x, approximate=True)

def _silu(x):
    return jax.nn.silu(x)

def _sigmoid(x):
    return jax.nn.sigmoid(x)

def _layernorm(x, axis=-1, eps=1e-05):
    m = jnp.mean(x, axis=axis, keepdims=True)
    v = jnp.var(x, axis=axis, keepdims=True)
    return (x - m) / jnp.sqrt(v + eps)

def _scatter_add(tgt, idx, src, axis=0):
    return tgt.at[idx].add(src)

def _segment_sum(src, seg, n):
    return jax.ops.segment_sum(src, seg, n)
kernel_name = 'mk_audio_tower_d1_tok_audfeat768_r4_790319'

def setup_inputs(seed: int=0):
    np.random.seed(seed)
    _w = jnp.asarray

    def _rec_inputs():
        import jax
        import jax.numpy as jnp
        _rk = jax.random.key(seed)
        x = -4.65018e-05 + 0.999886 * jax.random.normal(jax.random.fold_in(_rk, 1), (64, 125, 192), jnp.float32)
        return x
    x = _rec_inputs()

    def _L0_tok_setup():
        import jax, jax.numpy as jnp
        import numpy as np
        key = jax.random.key(seed)
        ks = jax.random.split(key, 8)
        B, S, TD, DM = (16, 1024, 192, 192)
        s = 0.02
        return {'text_embeddings': jax.random.normal(ks[0], (B, S, TD), jnp.float32), 'W_w': jax.random.normal(ks[1], (DM, TD), jnp.float32) * s, 'W_b': jax.random.normal(ks[2], (DM,), jnp.float32) * s, 'b': jnp.zeros((DM,), jnp.float32), 'V_w': jax.random.normal(ks[3], (1, DM), jnp.float32) * s, 'V_b': jax.random.normal(ks[4], (1,), jnp.float32) * s, 'P_w': jax.random.normal(ks[5], (DM, TD), jnp.float32) * s, 'P_b': jax.random.normal(ks[6], (DM,), jnp.float32) * s, 'patch_len': 4, 'stride': 2}
    _L0_tok_all = _L0_tok_setup()
    _L0_tok_in = {k: v for k, v in _L0_tok_all.items() if k in ('W_w', 'W_b', 'b', 'V_w', 'V_b', 'P_w', 'P_b')}
    del _L0_tok_all

    def _L0_attn_setup():
        import jax, jax.numpy as jnp
        import numpy as np
        MAX_DIST = 100

        def _pos_bias(rel_emb, length):
            emb_sum = rel_emb[..., 0].sum(axis=-1)
            pos = jnp.arange(length)
            rel = pos[None, :] - pos[:, None]
            idx = jnp.clip(rel, -(MAX_DIST - 1), MAX_DIST - 1) + MAX_DIST - 1
            return emb_sum[:, idx]
        key = jax.random.key(seed)
        ks = jax.random.split(key, 6)
        b, s, e, h, d = (4, 512, 192, 8, 96)
        return {'x': jax.random.normal(ks[0], (b, s, e), dtype=jnp.float32), 'w_q': jax.random.normal(ks[1], (h, e, d), dtype=jnp.float32) * 0.02, 'w_k': jax.random.normal(ks[2], (h, e, d), dtype=jnp.float32) * 0.02, 'w_v': jax.random.normal(ks[3], (h, e, d), dtype=jnp.float32) * 0.02, 'w_o': jax.random.normal(ks[4], (h, d, e), dtype=jnp.float32) * 0.02, 'rel_emb': jax.random.normal(ks[5], (h, 2 * MAX_DIST - 1, d, 1), dtype=jnp.float32) * 0.02}
    _L0_attn_all = _L0_attn_setup()
    _L0_attn_in = {k: v for k, v in _L0_attn_all.items() if k in ('w_q', 'w_k', 'w_v', 'w_o', 'rel_emb')}
    del _L0_attn_all

    def _L0_ffn_setup():
        import jax, jax.numpy as jnp
        import numpy as np
        from jax import lax
        DIM = 192
        INTER = 128
        E = 8
        G = 4
        TOPK_G = 2
        TOPK = 2
        ROUTE_SCALE = 1.0

        def _gate(x2, gate_weight, gate_bias):
            T = x2.shape[0]
            scores = jax.nn.sigmoid(x2 @ gate_weight.T)
            s = scores + gate_bias
            sv = s.reshape(T, G, E // G)
            top2, _ = lax.top_k(sv, 2)
            group_scores = top2.sum(-1)
            _, gidx = lax.top_k(group_scores, TOPK_G)
            gmask = jnp.zeros((T, G), bool).at[jnp.arange(T)[:, None], gidx].set(True)
            masked = jnp.where(gmask[:, :, None], sv, -jnp.inf).reshape(T, E)
            _, idx = lax.top_k(masked, TOPK)
            w = jnp.take_along_axis(scores, idx, axis=1)
            w = w / (w.sum(-1, keepdims=True) + 1e-06) * ROUTE_SCALE
            return (w, idx)
        key = jax.random.key(seed)
        ks = jax.random.split(key, 9)
        s = 1.0 / np.sqrt(DIM)
        si = 1.0 / np.sqrt(INTER)
        return {'x': jax.random.normal(ks[0], (4, 1024, DIM), jnp.float32), 'gate_weight': jax.random.uniform(ks[1], (E, DIM), jnp.float32, -s, s), 'gate_bias': jnp.zeros((E,), jnp.float32), 'w1': jax.random.uniform(ks[2], (E, INTER, DIM), jnp.float32, -s, s), 'w2': jax.random.uniform(ks[3], (E, DIM, INTER), jnp.float32, -si, si), 'w3': jax.random.uniform(ks[4], (E, INTER, DIM), jnp.float32, -s, s), 'sw1': jax.random.uniform(ks[5], (INTER, DIM), jnp.float32, -s, s), 'sw2': jax.random.uniform(ks[6], (DIM, INTER), jnp.float32, -si, si), 'sw3': jax.random.uniform(ks[7], (INTER, DIM), jnp.float32, -s, s)}
    _L0_ffn_all = _L0_ffn_setup()
    _L0_ffn_in = {k: v for k, v in _L0_ffn_all.items() if k in ('gate_weight', 'gate_bias', 'w1', 'w2', 'w3', 'sw1', 'sw2', 'sw3')}
    del _L0_ffn_all
    return {'x': x, 'L0_tok_W_w': _L0_tok_in['W_w'], 'L0_tok_W_b': _L0_tok_in['W_b'], 'L0_tok_b': _L0_tok_in['b'], 'L0_tok_V_w': _L0_tok_in['V_w'], 'L0_tok_V_b': _L0_tok_in['V_b'], 'L0_tok_P_w': _L0_tok_in['P_w'], 'L0_tok_P_b': _L0_tok_in['P_b'], 'L0_attn_w_q': _L0_attn_in['w_q'], 'L0_attn_w_k': _L0_attn_in['w_k'], 'L0_attn_w_v': _L0_attn_in['w_v'], 'L0_attn_w_o': _L0_attn_in['w_o'], 'L0_attn_rel_emb': _L0_attn_in['rel_emb'], 'L0_ffn_gate_weight': _L0_ffn_in['gate_weight'], 'L0_ffn_gate_bias': _L0_ffn_in['gate_bias'], 'L0_ffn_w1': _L0_ffn_in['w1'], 'L0_ffn_w2': _L0_ffn_in['w2'], 'L0_ffn_w3': _L0_ffn_in['w3'], 'L0_ffn_sw1': _L0_ffn_in['sw1'], 'L0_ffn_sw2': _L0_ffn_in['sw2'], 'L0_ffn_sw3': _L0_ffn_in['sw3']}

def reference(x, L0_tok_W_w, L0_tok_W_b, L0_tok_b, L0_tok_V_w, L0_tok_V_b, L0_tok_P_w, L0_tok_P_b, L0_attn_w_q, L0_attn_w_k, L0_attn_w_v, L0_attn_w_o, L0_attn_rel_emb, L0_ffn_gate_weight, L0_ffn_gate_bias, L0_ffn_w1, L0_ffn_w2, L0_ffn_w3, L0_ffn_sw1, L0_ffn_sw2, L0_ffn_sw3):
    import jax
    import jax.numpy as jnp

    def _L0_tok_ref(text_embeddings, W_w, W_b, b, V_w, V_b, P_w, P_b, patch_len, stride):
        import jax, jax.numpy as jnp
        import numpy as np
        B, S, TD = text_embeddings.shape
        A = jnp.tanh(jnp.einsum('bst,dt->bsd', text_embeddings, W_w) + W_b + b)
        scores = jnp.einsum('bsd,od->bso', A, V_w)[..., 0] + V_b[0]
        starts = jnp.arange(0, S - patch_len + 1, stride)
        idx = starts[:, None] + jnp.arange(patch_len)
        sw = scores[:, idx]
        w = jax.nn.softmax(sw, axis=-1)
        xw = text_embeddings[:, idx]
        attended = jnp.einsum('bpl,bplt->bpt', w, xw)
        return jnp.einsum('bpt,dt->bpd', attended, P_w) + P_b

    def _L0_attn_ref(x, w_q, w_k, w_v, w_o, rel_emb):
        import jax, jax.numpy as jnp
        import numpy as np
        MAX_DIST = 100

        def _pos_bias(rel_emb, length):
            emb_sum = rel_emb[..., 0].sum(axis=-1)
            pos = jnp.arange(length)
            rel = pos[None, :] - pos[:, None]
            idx = jnp.clip(rel, -(MAX_DIST - 1), MAX_DIST - 1) + MAX_DIST - 1
            return emb_sum[:, idx]
        b, s, e = x.shape
        d = w_q.shape[-1]
        q = jnp.einsum('bse,hed->bhsd', x, w_q)
        k = jnp.einsum('bse,hed->bhsd', x, w_k)
        v = jnp.einsum('bse,hed->bhsd', x, w_v)
        scale = d ** (-0.5)
        logits = jnp.einsum('bhqd,bhkd->bhqk', q, k) * scale
        logits = logits + _pos_bias(rel_emb, s)[None]
        attn = jax.nn.softmax(logits, axis=-1)
        ctx = jnp.einsum('bhqk,bhkd->bhqd', attn, v)
        return jnp.einsum('bhsd,hde->bse', ctx, w_o)

    def _L0_ffn_ref(x, gate_weight, gate_bias, w1, w2, w3, sw1, sw2, sw3):
        import jax, jax.numpy as jnp
        import numpy as np
        from jax import lax
        DIM = 192
        INTER = 128
        E = 8
        G = 4
        TOPK_G = 2
        TOPK = 2
        ROUTE_SCALE = 1.0

        def _gate(x2, gate_weight, gate_bias):
            T = x2.shape[0]
            scores = jax.nn.sigmoid(x2 @ gate_weight.T)
            s = scores + gate_bias
            sv = s.reshape(T, G, E // G)
            top2, _ = lax.top_k(sv, 2)
            group_scores = top2.sum(-1)
            _, gidx = lax.top_k(group_scores, TOPK_G)
            gmask = jnp.zeros((T, G), bool).at[jnp.arange(T)[:, None], gidx].set(True)
            masked = jnp.where(gmask[:, :, None], sv, -jnp.inf).reshape(T, E)
            _, idx = lax.top_k(masked, TOPK)
            w = jnp.take_along_axis(scores, idx, axis=1)
            w = w / (w.sum(-1, keepdims=True) + 1e-06) * ROUTE_SCALE
            return (w, idx)
        B, S, D = x.shape
        x2 = x.reshape(-1, D)
        T = x2.shape[0]
        weights, indices = _gate(x2, gate_weight, gate_bias)
        cw = jnp.zeros((T, E), x.dtype).at[jnp.arange(T)[:, None], indices].add(weights)
        h1 = jnp.einsum('td,eid->tei', x2, w1)
        h3 = jnp.einsum('td,eid->tei', x2, w3)
        h = jax.nn.silu(h1) * h3
        y = jnp.einsum('tei,edi,te->td', h, w2, cw)
        z = jax.nn.silu(x2 @ sw1.T) * (x2 @ sw3.T) @ sw2.T
        return (y + z).reshape(B, S, D)
    h = _L0_tok_ref(x, L0_tok_W_w, L0_tok_W_b, L0_tok_b, L0_tok_V_w, L0_tok_V_b, L0_tok_P_w, L0_tok_P_b, 4, 2)
    h = h + _L0_attn_ref(_layernorm(h, axis=-1), L0_attn_w_q, L0_attn_w_k, L0_attn_w_v, L0_attn_w_o, L0_attn_rel_emb)
    h = h + _L0_ffn_ref(_layernorm(h, axis=-1), L0_ffn_gate_weight, L0_ffn_gate_bias, L0_ffn_w1, L0_ffn_w2, L0_ffn_w3, L0_ffn_sw1, L0_ffn_sw2, L0_ffn_sw3)
    return h

_drawn_inputs = setup_inputs


def setup_inputs(seed=0):
    import zlib

    import numpy as np

    out = dict(_drawn_inputs(seed))
    spreads = {'L0_tok_b': (0.0, 0.494), 'L0_ffn_gate_bias': (0.0, 0.1)}
    factors = {'L0_tok_W_b': 6.144}
    for name, (base, spread) in spreads.items():
        noise = np.random.default_rng([zlib.crc32(name.encode()), seed]).standard_normal(out[name].shape)
        drawn = base * np.exp(spread * noise) if base else spread * noise
        out[name] = jnp.asarray(drawn.astype(out[name].dtype))
    for name, factor in factors.items():
        out[name] = (out[name] * factor).astype(out[name].dtype)
    return out
```

```python
import concourse.bass as bass
from concourse import mybir
from contextlib import ExitStack

FP32 = mybir.dt.float32
F32R = mybir.dt.float32r
ALU = mybir.AluOpType
ACT = mybir.ActivationFunctionType
AX = mybir.AxisListType.X

B, S, D = 64, 125, 192
NP = (S - 4) // 2 + 1
H, DH = 8, 96
E, INTER = 8, 128
GB = 4
NG = B // GB
PAIRS = GB // 2
TT = 2 * NP
GT = GB * NP
DA, DB = 128, D - 128
LO = 64
KS = LO + NP
HP = H // 2
LN_EPS = 1e-5
BIG = 1.5e38


class Signal:

    def __init__(self, sem, per_group):
        self.sem, self.n = sem, per_group

    def at(self, g, k):
        return self.sem, g * self.n + k


def split_product(pe, out, xa_hi, xa_lo, xb2, xb_lo, wa_hi, wa_lo, wb):
    pe.matmul(out, xa_hi, wa_hi, start=True, stop=False)
    pe.matmul(out, xa_lo, wa_hi, start=False, stop=False)
    pe.matmul(out, xa_hi, wa_lo, start=False, stop=False)
    pe.matmul(out, xb2, wb, start=False, stop=False)
    return pe.matmul(out, xb_lo, wb[0:DB], start=False, stop=True)


def audio_tower_kernel(nc, x, xT, tok_wT, tok_bias, tok_v, tok_vb, tok_pT, tok_pb, wqT, wkT, wvT, wo, rel, gate_w,
                       gate_b, w1T, w3T, w2T, sw1T, sw3T, sw2T, c_ident, c_band, c_diag, c_flip, c_pick, c_lt4,
                       c_lt8, out):
    scratch = nc.dram_tensor("bias_sums", [H, 2 * NP], FP32, kind="Internal")

    ctx = ExitStack()
    with ctx:
        def sb(name, shape, dt=FP32, where=ctx):
            return where.enter_context(nc.sbuf_tensor(name, shape, dt))

        def sem(name):
            return ctx.enter_context(nc.semaphore(name))

        def signal(name, per_group):
            return Signal(sem(name), per_group)

        qk_a = [sb(f"qk_a{n}", [DA, HP, 3, 128], F32R) for n in range(2)]
        qk_b = sb("qk_b", [2 * DB, HP, 3, 128], F32R)
        vo_a = [sb(f"vo_a{n}", [DA, H, D], F32R) for n in range(2)]
        vo_b = [sb(f"vo_b{n}", [2 * DB, HP, D], F32R) for n in range(2)]
        up_a = [sb(f"up_a{n}", [DA, E + 1, 2, INTER], F32R) for n in range(2)]
        up_b = sb("up_b", [2 * DB, E + 1, 2, INTER], F32R)
        down = [sb(f"down{n}", [INTER, E + 1, D], F32R) for n in range(2)]
        gw_a = [sb(f"gw_a{n}", [DA, E], F32R) for n in range(2)]
        gw_b = sb("gw_b", [2 * DB, E], F32R)
        bias = sb("bias", [KS, H, NP], F32R)
        tw_a, tw_b = sb("tw_a", [DA, D]), sb("tw_b", [DB + 2, D])
        tp_a, tp_b = sb("tp_a", [DA, D]), sb("tp_b", [DB, D])
        v_row, vb_col = sb("v_row", [S, D]), sb("vb_col", [S, 1])
        pb_row, gb_row = sb("pb_row", [TT, D]), sb("gb_row", [TT, E])
        ident = sb("ident", [128, 128])
        ident_r = sb("ident_r", [S, S], F32R)
        band_raw, band_mask = sb("band_raw", [S, GB * NP]), sb("band_mask", [S, GB * NP], F32R)
        diag_mask = sb("diag_mask", [GB, GB, NP])
        flip_raw, flip = sb("flip_raw", [KS, NP]), sb("flip", [KS, NP], F32R)
        pick_raw, pick = sb("pick_raw", [40, E, 128]), sb("pick", [40, E, 128], F32R)
        lt4, lt8 = sb("lt4", [TT, 16]), sb("lt8", [TT, 64])
        ones = sb("ones", [128, 128])
        minus_half = sb("minus_half", [TT, PAIRS])
        wait_cell = sb("wait_cell", [TT, 1])
        xin_a, xin_b = sb("xin_a", [DA, GB * S]), sb("xin_b", [DB + 2, GB * S])
        xin = sb("xin", [S, GB, D])
        tanh_sb = sb("tanh_sb", [S, GB, D])
        score_raw, score = sb("score_raw", [S, GB]), sb("score", [S, GB])
        neg_max, max_diag = sb("neg_max", [GB, NP]), sb("max_diag", [GB, GB, NP])
        band = sb("band", [S, GB, NP])
        mix_a, mix_b = sb("mix_a", [DA, GT]), sb("mix_b", [DB, GT])
        band_rden = sb("band_rden", [TT, PAIRS])
        h1, h1_res = sb("h1", [TT, PAIRS, D]), sb("h1_res", [TT, PAIRS, D])
        st1, mv1, ve1, rs1 = (sb("st1", [TT, PAIRS, 6]), sb("mv1", [TT, PAIRS, 2]), sb("ve1", [TT, PAIRS]),
                              sb("rs1", [TT, PAIRS]))
        xn1 = sb("xn1", [TT, PAIRS, D])
        xn_half = [sb(f"xn_half{n}", [TT, PAIRS, D], F32R) for n in range(2)]
        xc_hi = sb("xc_hi", [KS, GB, D], F32R)
        xc_lo = sb("xc_lo", [NP, GB, D], F32R)
        x1_a = [sb(f"x1_a{n}", [DA, GT], F32R) for n in range(2)]
        x1_b2, x1_blo = sb("x1_b2", [2 * DB, GT], F32R), sb("x1_blo", [DB, GT], F32R)
        prob = [sb(f"prob{n}", [NP, H, NP]) for n in range(2)]
        row_max, row_sum, row_rec = (sb("row_max", [NP, H]), sb("row_sum", [NP, H]), sb("row_rec", [NP, H]))
        probT = sb("probT", [KS, H * NP], F32R)
        h2, h2_res = sb("h2", [TT, PAIRS, D]), sb("h2_res", [TT, PAIRS, D])
        st2, mv2, ve2, rs2 = (sb("st2", [TT, PAIRS, 6]), sb("mv2", [TT, PAIRS, 2]), sb("ve2", [TT, PAIRS]),
                              sb("rs2", [TT, PAIRS]))
        xn2 = sb("xn2", [TT, PAIRS, D])
        x2_a = [sb(f"x2_a{n}", [DA, GT], F32R) for n in range(2)]
        x2_b2, x2_blo = sb("x2_b2", [2 * DB, GT], F32R), sb("x2_blo", [DB, GT], F32R)
        g_tanh, g_sig, g_sb = (sb("g_tanh", [TT, PAIRS * E]), sb("g_sig", [TT, PAIRS, E]), sb("g_sb", [TT, PAIRS, E]))
        g_grp, g_rank4, g_sel4 = (sb("g_grp", [TT, PAIRS, 4]), sb("g_rank4", [TT, PAIRS, 4]), sb("g_sel4", [TT, PAIRS, 4]))
        g_cmp4, g_eq4 = sb("g_cmp4", [TT, PAIRS, 16]), sb("g_eq4", [TT, PAIRS, 16])
        g_msk = sb("g_msk", [TT, PAIRS, E])
        g_cmp8, g_eq8 = sb("g_cmp8", [TT, PAIRS, 64]), sb("g_eq8", [TT, PAIRS, 64])
        g_rank8, g_w = sb("g_rank8", [TT, PAIRS, E]), sb("g_w", [TT, PAIRS, E])
        g_sum, g_rec = sb("g_sum", [TT, PAIRS]), sb("g_rec", [TT, PAIRS])
        g_cw = sb("g_cw", [TT, PAIRS, E])
        cwT = sb("cwT", [40, GT], F32R)
        act = [sb(f"act{n}", [INTER, 2, GT]) for n in range(2)]
        cw_sb = sb("cw_sb", [INTER, 2, GT])
        out_sb = sb("out_sb", [TT, PAIRS, D])

        raw = ExitStack()
        rq, rk, rv, ro = (sb(f"raw_{n}", [DH, H, D], FP32, raw) for n in "qkvo")
        r_up_a, r_up_b = (sb(f"raw_up{n}", [p, E + 1, 2, INTER], FP32, raw) for n, p in (("a", DA), ("b", DB)))
        r_down = sb("raw_down", [INTER, E + 1, D], FP32, raw)
        raw.close()
        z_a = [sb(f"z_a{n}", [DA, GB, H, NP], F32R) for n in range(2)]
        z_b = sb("z_b", [2 * DB, GB, H, NP], F32R)
        c_a = [sb(f"c_a{n}", [DA, H, 2, NP], F32R) for n in range(2)]
        c_b = [sb(f"c_b{n}", [2 * DB, HP, 2, NP], F32R) for n in range(2)]
        hid = [sb(f"hid{n}", [INTER, E + 1, GT], F32R) for n in range(2)]
        rel_raw = tanh_sb[0:2 * NP - 1, :, :].rearrange("p b d -> p (b d)").rearrange("p (h e) -> p h e", h=H)
        rel_sum, rel_sumT = sb("rel_sum", [2 * NP - 1, H]), sb("rel_sumT", [H, 2 * NP])
        bias_raw = sb("bias_raw", [NP, H, NP])
        gw_raw_a, gw_raw_b = sb("gw_raw_a", [DA, E]), sb("gw_raw_b", [DB, E])

        bank = {n: ctx.enter_context(nc.psum_tensor(f"bank_{n}", [128, 512], FP32))
                for n in ("logit", "probT", "ca", "cb", "up", "gate_up", "s0", "s1")}

        d_tok, d_small, d_qk, d_vo, d_up, d_down, d_rel, d_bias = (
            sem(n) for n in ("d_tok", "d_small", "d_qk", "d_vo", "d_up", "d_down", "d_rel", "d_bias"))
        p_fill, p_const, p_mm, p_hi, p_lo, p_rel, p_relT, p_relc, d_relw = (
            sem(n) for n in ("p_fill", "p_const", "p_mm", "p_hi", "p_lo", "p_rel", "p_relT", "p_relc", "d_relw"))

        x_loaded = signal("x_loaded", 48)
        a_mm, a_tanh = signal("a_mm", 2), signal("a_tanh", 2)
        av, sc_raw, sc, scT = signal("av", 1), signal("sc_raw", 1), signal("sc", 1), signal("scT", 1)
        nm, nmd, band_mm, band_in, band_e = (signal(n, 1) for n in ("nm", "nmd", "band_mm", "band_in", "band_e"))
        mix_mm, mix_sb, rden, p_mm2, h1_ok = (signal("mix_mm", 1), signal("mix_sb", 2), signal("rden", 1),
                                              signal("proj_mm", 1), signal("h1_ok", 2))
        st1_ok, mv1_ok, ve1_ok, rs1_ok, xn1_ok = (signal("st1_ok", 2), signal("mv1_ok", 2), signal("ve1_ok", 1),
                                                  signal("rs1_ok", 1), signal("xn1_ok", 2))
        xn_hi_ok, xn_lo_ok, xc_moved, h1_kept = (signal("xn_hi_ok", 1), signal("xn_lo_ok", 1), signal("xc_moved", 96),
                                                 signal("h1_kept", 1))
        x1_mm, x1_hi, x1_lo = signal("x1_mm", 1), signal("x1_hi", 3), signal("x1_lo", 2)
        z_mm, z_hi, z_lo = signal("z_mm", 6), signal("z_hi", 8), signal("z_lo", 8)
        l_mm, mx_ok, sub_ok, exp_ok, sum_ok, rec_ok, pn_ok = (
            signal(n, GB) for n in ("l_mm", "mx_ok", "sub_ok", "exp_ok", "sum_ok", "rec_ok", "pn_ok"))
        pt_mm, pt_hi, pt_lo, ca_mm, ca_hi, ca_lo, cb_mm = (
            signal(n, GB) for n in ("pt_mm", "pt_hi", "pt_lo", "ca_mm", "ca_hi", "ca_lo", "cb_mm"))
        cb_hi, cb_lo = signal("cb_hi", 2 * GB), signal("cb_lo", 2 * GB)
        o_mm, h2_ok, st2_ok, mv2_ok, ve2_ok, rs2_ok, xn2_ok, h2_kept = (
            signal("o_mm", 2), signal("h2_ok", 2), signal("st2_ok", 2), signal("mv2_ok", 2), signal("ve2_ok", 1),
            signal("rs2_ok", 1), signal("xn2_ok", 2), signal("h2_kept", 1))
        x2_mm, x2_hi, x2_lo = signal("x2_mm", 1), signal("x2_hi", 3), signal("x2_lo", 2)
        g_mm, g_th = signal("g_mm", 1), signal("g_th", 1)
        GATE_STEPS = 22
        g_step = signal("g_step", GATE_STEPS)
        cwt_mm, cwt_hi, cwt_lo = signal("cwt_mm", 1), signal("cwt_hi", 1), signal("cwt_lo", 1)
        cw_mm, cw_ok, w_ok = signal("cw_mm", HP), signal("cw_ok", HP), signal("w_ok", HP)
        up_mm, tanh_ok, u_ok, v_ok, hid_hi, hid_lo = (
            signal(n, HP + 1) for n in ("up_mm", "tanh_ok", "u_ok", "v_ok", "hid_hi", "hid_lo"))
        y_mm, out_ok, out_sent = signal("y_mm", 2), signal("out_ok", 2), signal("out_sent", 16)

        class Section:
            def __init__(self, i, first, last):
                self.i, self.a, self.f, self.t = i, first >= 0 and last < NG, first >= 1, last < NG - 1
                self.key = first

            @property
            def tg(self):
                return self.i + 1

            @property
            def ag(self):
                return self.i

            @property
            def fg(self):
                return self.i - 1

        LOOP = (2, NG - 1)

        def sections(eng, body):
            for i in (-1, 0, 1):
                body(Section(i, i, i))
            with eng.Fori(LOOP[0], LOOP[1]) as i:
                body(Section(i, LOOP[0], LOOP[1] - 1))
            for i in (NG - 1, NG):
                body(Section(i, i, i))

        USES = {}
        for j in range(GB):
            USES["logit", j] = ("logit", "a", sub_ok, j + 1)
            USES["probT", j] = ("probT", "a", pt_lo, j + 1)
            USES["ca", j] = ("ca", "a", ca_lo, j + 1)
            USES["cb", j] = ("cb", "a", cb_lo, 2 * (j + 1))
            USES["up", j] = ("up", "f", u_ok, j + 1)
            USES["gate_up", j] = ("gate_up", "f", v_ok, j + 1)
        USES["up", HP] = ("up", "f", v_ok, HP + 1)
        for n, (b, k) in enumerate([("logit", 1), ("probT", 2), ("gate_up", 4), ("up", 5), ("ca", 6), ("cb", 8)]):
            USES["z", n] = (b, "t", z_lo, k)
        for name, b, stage, sig, k in [
                (("score", 0), "s0", "t", a_tanh, 1), (("cwT", 0), "s1", "f", cwt_lo, 1),
                (("score", 1), "s0", "t", a_tanh, 2), (("cw", 0), "s1", "f", cw_ok, 1),
                (("cw", 1), "s1", "f", cw_ok, 2), (("scT", 0), "s0", "t", nm, 1), (("cw", 2), "s1", "f", cw_ok, 3),
                (("o", 0), "s1", "a", h2_ok, 1), (("band", 0), "s0", "t", band_in, 1),
                (("cw", 3), "s1", "f", cw_ok, 4), (("mix", 0), "s0", "t", rden, 1), (("proj", 0), "s1", "t", h1_ok, 2),
                (("y", 0), "s0", "f", out_ok, 1), (("o", 1), "s1", "a", h2_ok, 2), (("x1", 0), "s0", "t", x1_lo, 2),
                (("y", 1), "s1", "f", out_ok, 2), (("x2", 0), "s0", "a", x2_lo, 2), (("gate", 0), "s1", "a", g_th, 1)]:
            USES[name] = (b, stage, sig, k)

        def free(pe, sec, name):
            b = USES[name][0]
            order = [u for u in USES if USES[u][0] == b]
            stage_on = lambda s, u: {"a": s.a, "f": s.f, "t": s.t}[USES[u][1]]
            n = order.index(name)
            for u in reversed(order[:n]):
                if stage_on(sec, u):
                    _, stage, sig, k = USES[u]
                    pe.wait_ge(*sig.at({"a": sec.ag, "f": sec.fg, "t": sec.tg}[stage], k))
                    return
            if sec.key < 0:
                return
            before = Section(sec.i - 1, sec.key - 1, sec.key - 1)
            for u in reversed(order):
                if stage_on(before, u):
                    _, stage, sig, k = USES[u]
                    pe.wait_ge(*sig.at({"a": before.ag, "f": before.fg, "t": before.tg}[stage], k))
                    return

        UP_CHUNKS = 3
        SMALL_LOADS = 13
        block = ctx.enter_context(nc.Block())

        @block.sync
        def _(sp):
            def load_x(g):
                sp.dma_start(xin_a[:, :], xT[0:DA, bass.ds(g * (GB * S), GB * S)]).then_inc(x_loaded.sem, 16)
                sp.dma_start(xin_b[0:DB, :], xT[DA:D, bass.ds(g * (GB * S), GB * S)]).then_inc(x_loaded.sem, 16)
                sp.dma_start(xin[:, :, :], x[bass.ds(g * GB, GB), :, :].rearrange("b s d -> s b d"))\
                    .then_inc(x_loaded.sem, 16)

            load_x(0)
            sp.dma_start(tw_a[:, :], tok_wT[0:DA, :]).then_inc(d_tok, 16)
            sp.dma_start(tw_b[0:DB, :], tok_wT[DA:D, :]).then_inc(d_tok, 16)
            sp.dma_start(tw_b[DB:DB + 2, :], tok_bias).then_inc(d_tok, 16)
            sp.dma_start(tp_a[:, :], tok_pT[0:DA, :]).then_inc(d_tok, 16)
            sp.dma_start(tp_b[:, :], tok_pT[DA:D, :]).then_inc(d_tok, 16)
            sp.dma_start(r_up_a[:, 0:E, 0, :], w1T[0:DA]).then_inc(d_up, 16)
            sp.dma_start(r_up_a[:, 0:E, 1, :], w3T[0:DA]).then_inc(d_up, 16)
            sp.dma_start(r_up_a[:, E, 0, :], sw1T[0:DA]).then_inc(d_up, 16)
            sp.dma_start(r_up_a[:, E, 1, :], sw3T[0:DA]).then_inc(d_up, 16)
            sp.dma_start(r_up_b[:, 0:E, 0, :], w1T[DA:D]).then_inc(d_up, 16)
            sp.dma_start(r_up_b[:, 0:E, 1, :], w3T[DA:D]).then_inc(d_up, 16)
            sp.dma_start(r_up_b[:, E, 0, :], sw1T[DA:D]).then_inc(d_up, 16)
            sp.dma_start(r_up_b[:, E, 1, :], sw3T[DA:D]).then_inc(d_up, 16)
            sp.wait_ge(p_relc, 1)
            sp.dma_start(scratch[:, 0:2 * NP - 1], rel_sumT[:, 0:2 * NP - 1]).then_inc(d_relw, 16)
            sp.wait_ge(d_relw, 16)
            sp.dma_start(bias_raw[:, :, :], bass.AP(scratch, 0, [[1, NP], [2 * NP, H], [1, NP]])).then_inc(d_bias, 16)

            def body(s):
                if s.t:
                    sp.wait_ge(*xn_hi_ok.at(s.tg, 1))
                    sp.wait_ge(*xn_lo_ok.at(s.tg, 1))
                    if s.a:
                        sp.wait_ge(*cb_mm.at(s.ag, GB))
                    else:
                        sp.wait_ge(p_fill, 6)
                    for par in range(2):
                        src = slice(par * NP, (par + 1) * NP)
                        sp.dma_start(xc_hi[0:NP, par::2, :].bitcast(FP32), xn_half[0][src, :, :].bitcast(FP32)).then_inc(xc_moved.sem, 16)
                        sp.dma_start(xc_hi[LO:KS, par::2, :].bitcast(FP32), xn_half[0][src, :, :].bitcast(FP32)).then_inc(xc_moved.sem, 16)
                        sp.dma_start(xc_lo[:, par::2, :].bitcast(FP32), xn_half[1][src, :, :].bitcast(FP32)).then_inc(xc_moved.sem, 16)
                if s.f:
                    sp.wait_ge(*out_ok.at(s.fg, 2))
                    dst = out[bass.ds(s.fg * GB, GB), :, :].rearrange("(t b) p d -> (b p) t d", b=2)
                    sp.dma_start(dst, out_sb[:, :, :]).then_inc(out_sent.sem, 16)

            def load_next(s, has_next):
                if s.t and has_next:
                    sp.wait_ge(*mix_mm.at(s.tg, 1))
                    load_x(s.tg + 1)

            def step(s):
                load_next(s, s.key < NG - 2 and not s.key == NG - 2)
                body(s)

            for i in (-1, 0, 1):
                step(Section(i, i, i))
            with sp.Fori(LOOP[0], NG - 2) as i:
                step(Section(i, LOOP[0], LOOP[1] - 1))
            for i in (NG - 2, NG - 1, NG):
                step(Section(i, i, i))
            sp.wait_ge(out_sent.sem, 16 * NG)

        @block.tensor
        def _(pe):
            mm = nc.tensor.matmul

            pe.wait_ge(p_rel, 1)
            pe.wait_ge(d_small, 16 * SMALL_LOADS)
            nc.tensor.transpose(bank["s0"][0:H, 0:2 * NP - 1], rel_sum[:, :], ident[0:2 * NP - 1, 0:2 * NP - 1])\
                .then_inc(p_relT, 1)
            order = ["logit", "probT", "ca", "cb", "up", "gate_up"]
            n = 0
            for k, (left, right, loaded) in enumerate(((rk, rq, d_qk), (rv, ro, d_vo))):
                pe.wait_ge(loaded, 32)
                for hp in range(HP):
                    for c0, cn in ((0, DA), (DA, DB)):
                        dst = bank[order[n % 6]]
                        if n >= 6:
                            pe.wait_ge(p_lo, n - 5)
                        for par in range(2):
                            last = mm(dst[0:cn, par * D:(par + 1) * D], left[:, 2 * hp + par, c0:c0 + cn],
                                      right[:, 2 * hp + par, :], start=True, stop=True)
                        last.then_inc(p_mm, 1)
                        n += 1

            def up(s, j, n, b_up, b_gate):
                for kind, dst in enumerate((b_up, b_gate)):
                    for e in range(n):
                        ex = 2 * j + e
                        o = dst[:, e * GT:(e + 1) * GT]
                        wa, wl, wb = (w[:, ex, kind, :] for w in (up_a[0], up_a[1], up_b))
                        mm(o, wa, x2_a[0][:, :], start=True, stop=False)
                        mm(o, wl, x2_a[0][:, :], start=False, stop=False)
                        mm(o, wa, x2_a[1][:, :], start=False, stop=False)
                        mm(o, wb, x2_b2[:, :], start=False, stop=False)
                        last = mm(o, wb[0:DB], x2_blo[:, :], start=False, stop=True)
                return last

            def out_proj(s, t):
                free(pe, s, ("o", t))
                pe.wait_ge(*ca_lo.at(s.ag, 2 * t + 2))
                pe.wait_ge(*cb_lo.at(s.ag, 4 * t + 4))
                o = bank["s1"][0:TT, 0:D]
                for hh in range(H):
                    ch, cl = (c[:, hh, :, :].rearrange("p b q -> p (b q)") for c in c_a)
                    mm(o, ch, vo_a[0][:, hh, :], start=hh == 0, stop=False)
                    mm(o, cl, vo_a[0][:, hh, :], start=False, stop=False)
                    mm(o, ch, vo_a[1][:, hh, :], start=False, stop=False)
                for hp in range(HP):
                    ch, cl = (c[:, hp, :, :].rearrange("p b q -> p (b q)") for c in c_b)
                    mm(o, ch, vo_b[0][:, hp, :], start=False, stop=False)
                    mm(o, cl, vo_b[0][:, hp, :], start=False, stop=False)
                    last = mm(o, ch, vo_b[1][:, hp, :], start=False, stop=hp == HP - 1)
                last.then_inc(o_mm.sem, 1)

            def logits(s, j):
                free(pe, s, ("logit", j))
                if j == 0:
                    pe.wait_ge(*z_lo.at(s.ag, 8))
                q = slice(j * NP, (j + 1) * NP)
                o = bank["logit"][0:NP, 0:H * NP]
                mm(o, flip[:, :], bias[:, :, :].rearrange("p h k -> p (h k)"), start=True, stop=False)
                zh, zl, zb = (z[:, j, :, :].rearrange("p h k -> p (h k)") for z in (z_a[0], z_a[1], z_b))
                mm(o, x1_a[0][:, q], zh, start=False, stop=False)
                mm(o, x1_a[1][:, q], zh, start=False, stop=False)
                mm(o, x1_a[0][:, q], zl, start=False, stop=False)
                mm(o, x1_b2[:, q], zb, start=False, stop=False)
                mm(o, x1_blo[:, q], zb[0:DB], start=False, stop=True).then_inc(l_mm.sem, 1)

            def prob_transpose(s, j):
                free(pe, s, ("probT", j))
                pe.wait_ge(*pn_ok.at(s.ag, j + 1))
                mm(bank["probT"][0:NP, 0:2], flip[:, :], ident_r[:, 0:2], start=True, stop=True)
                for hh in range(H):
                    last = nc.tensor.transpose(bank["probT"][0:NP, hh * NP:(hh + 1) * NP], prob[j % 2][:, hh, :],
                                               ident[0:NP, 0:NP])
                last.then_inc(pt_mm.sem, 1)

            def context(s, j):
                if j == 0:
                    pe.wait_ge(*xc_moved.at(s.ag, 96))
                pe.wait_ge(*pt_lo.at(s.ag, j + 1))
                for name, sig, c0, cn in (("ca", ca_mm, 0, DA), ("cb", cb_mm, DA, DB)):
                    free(pe, s, (name, j))
                    o = bank[name][0:cn, 0:H * NP]
                    mm(o, xc_hi[:, j, c0:c0 + cn], probT[:, :], start=True, stop=False)
                    mm(o, xc_lo[:, j, c0:c0 + cn], probT[0:NP, :], start=False, stop=True).then_inc(sig.sem, 1)

            def token_scores(s, m):
                free(pe, s, ("score", m))
                if m == 0:
                    pe.wait_ge(*x_loaded.at(s.tg, 48))
                    if s.key < 0:
                        pe.wait_ge(d_tok, 80)
                        pe.wait_ge(p_fill, 6)
                for e in range(2):
                    o = bank["s0"][0:S, e * D:(e + 1) * D]
                    p = slice((2 * m + e) * S, (2 * m + e + 1) * S)
                    mm(o, xin_a[:, p], tw_a[:, :], start=True, stop=False)
                    last = mm(o, xin_b[:, p], tw_b[:, :], start=False, stop=True)
                last.then_inc(a_mm.sem, 1)

            def experts(s, j):
                if j == 0:
                    pe.wait_ge(*x2_lo.at(s.fg, 2))
                free(pe, s, ("up", j))
                free(pe, s, ("gate_up", j))
                up(s, j, 2, bank["up"], bank["gate_up"]).then_inc(up_mm.sem, 1)

            def spread_weights(s, j):
                free(pe, s, ("cw", j))
                if j == 0:
                    pe.wait_ge(*cwt_lo.at(s.fg, 1))
                for e in range(2):
                    last = mm(bank["s1"][:, e * GT:(e + 1) * GT], pick[:, 2 * j + e, :], cwT[:, :], start=True, stop=True)
                last.then_inc(cw_mm.sem, 1)

            def down_proj(s, t):
                free(pe, s, ("y", t))
                if t == 0:
                    pe.wait_ge(*hid_lo.at(s.fg, HP + 1))
                o = bank[USES["y", t][0]][0:TT, 0:D]
                q = slice(t * TT, (t + 1) * TT)
                for e in range(E + 1):
                    mm(o, hid[0][:, e, q], down[0][:, e, :], start=e == 0, stop=False)
                    mm(o, hid[1][:, e, q], down[0][:, e, :], start=False, stop=False)
                    last = mm(o, hid[0][:, e, q], down[1][:, e, :], start=False, stop=e == E)
                last.then_inc(y_mm.sem, 1)

            def x_transpose(s, name, src, sig, g, ready):
                free(pe, s, (name, 0))
                pe.wait_ge(*ready.at(g, 2))
                o = bank["s0"]
                for t in range(PAIRS):
                    nc.tensor.transpose(o[0:DA, t * TT:(t + 1) * TT], src[:, t, 0:DA], ident[0:TT, 0:TT])
                for t in range(PAIRS):
                    last = nc.tensor.transpose(o[0:DB, GT + t * TT:GT + (t + 1) * TT], src[:, t, DA:D],
                                               ident[0:TT, 0:TT])
                last.then_inc(sig.sem, 1)

            def z_tiles(s, n):
                if n == 0:
                    pe.wait_ge(*x1_lo.at(s.tg, 2))
                    if s.key < 0:
                        pe.wait_ge(p_lo, 27)
                free(pe, s, ("z", n))
                dst = bank[USES["z", n][0]]
                half, kind = n // 3, n % 3
                for e in range(2):
                    hp, tile = (2 * half + kind, e) if kind < 2 else (2 * half + e, 2)
                    w = [q[:, hp, tile, :] for q in (qk_a[0], qk_a[1], qk_b)]
                    o = dst[:, e * GT:(e + 1) * GT]
                    mm(o, w[0], x1_a[0][:, :], start=True, stop=False)
                    mm(o, w[1], x1_a[0][:, :], start=False, stop=False)
                    mm(o, w[0], x1_a[1][:, :], start=False, stop=False)
                    mm(o, w[2], x1_b2[:, :], start=False, stop=False)
                    last = mm(o, w[2][0:DB], x1_blo[:, :], start=False, stop=True)
                last.then_inc(z_mm.sem, 1)

            def body(s):
                for j in range(GB):
                    if s.a:
                        logits(s, j)
                        if j:
                            prob_transpose(s, j - 1)
                        if j == 3:
                            out_proj(s, 0)
                    if s.f:
                        experts(s, j)
                    if s.a and j:
                        context(s, j - 1)
                    if s.t and j == 0:
                        token_scores(s, 0)
                    if s.f and j == 0:
                        free(pe, s, ("cwT", 0))
                        pe.wait_ge(*g_step.at(s.fg, GATE_STEPS))
                        for t in range(PAIRS):
                            last = nc.tensor.transpose(bank["s1"][0:E, t * TT:(t + 1) * TT], g_cw[:, t, :],
                                                       ident[0:TT, 0:TT])
                        last.then_inc(cwt_mm.sem, 1)
                    if s.t and j == 0:
                        token_scores(s, 1)
                    if s.t and j == 2:
                        free(pe, s, ("scT", 0))
                        pe.wait_ge(*sc.at(s.tg, 1))
                        nc.tensor.transpose(bank["s0"][0:GB, 0:S], score[:, :], ident[0:S, 0:S]).then_inc(scT.sem, 1)
                    if s.t and j == 3:
                        free(pe, s, ("band", 0))
                        pe.wait_ge(*nmd.at(s.tg, 1))
                        o = bank["s0"][0:S, 0:GT]
                        mm(o, ident_r[:, :], band_mask[:, :], start=True, stop=False)
                        mm(o, ones[0:GB, 0:S], max_diag[:, :, :].rearrange("p b q -> p (b q)"), start=False, stop=True)\
                            .then_inc(band_mm.sem, 1)
                    if s.f:
                        spread_weights(s, j)
                if s.a:
                    prob_transpose(s, GB - 1)
                if s.t:
                    free(pe, s, ("mix", 0))
                    pe.wait_ge(*band_e.at(s.tg, 1))
                    for c0, cn, o0 in ((0, DA, 0), (DA, DB, GT)):
                        for b in range(GB):
                            mm(bank["s0"][0:cn, o0 + b * NP:o0 + (b + 1) * NP], xin[:, b, c0:c0 + cn], band[:, b, :],
                               start=True, stop=True)
                    for t in range(PAIRS):
                        last = mm(bank["s0"][0:TT, 2 * GT + t:2 * GT + t + 1],
                                  band[:, 2 * t:2 * t + 2, :].rearrange("p b q -> p (b q)"), ones[0:S, 0:1],
                                  start=True, stop=True)
                    last.then_inc(mix_mm.sem, 1)
                if s.f:
                    free(pe, s, ("up", HP))
                    b = bank["up"]
                    up(s, HP, 1, b[:, 0:GT], b[:, GT:2 * GT]).then_inc(up_mm.sem, 1)
                if s.a:
                    context(s, GB - 1)
                if s.t:
                    free(pe, s, ("proj", 0))
                    pe.wait_ge(*mix_sb.at(s.tg, 2))
                    for t in range(PAIRS):
                        o, q = bank["s1"][0:TT, t * D:(t + 1) * D], slice(t * TT, (t + 1) * TT)
                        mm(o, mix_a[:, q], tp_a[:, :], start=True, stop=False)
                        last = mm(o, mix_b[:, q], tp_b[:, :], start=False, stop=True)
                    last.then_inc(p_mm2.sem, 1)
                if s.f:
                    down_proj(s, 0)
                if s.a:
                    out_proj(s, 1)
                if s.t:
                    x_transpose(s, "x1", xn1, x1_mm, s.tg, xn1_ok)
                if s.f:
                    down_proj(s, 1)
                if s.t:
                    for n in range(3):
                        z_tiles(s, n)
                if s.a:
                    x_transpose(s, "x2", xn2, x2_mm, s.ag, xn2_ok)
                if s.t:
                    for n in range(3, 6):
                        z_tiles(s, n)
                if s.a:
                    free(pe, s, ("gate", 0))
                    pe.wait_ge(*x2_lo.at(s.ag, 2))
                    for t in range(PAIRS):
                        q = slice(t * TT, (t + 1) * TT)
                        o = bank["s1"][0:TT, t * E:(t + 1) * E]
                        last = split_product(nc.tensor, o, x2_a[0][:, q], x2_a[1][:, q], x2_b2[:, q], x2_blo[:, q],
                                             gw_a[0][:, :], gw_a[1][:, :], gw_b[:, :])
                    last.then_inc(g_mm.sem, 1)

            sections(pe, body)

        @block.scalar
        def _(ac):
            def copy(out_, in_, scale=1.0):
                return nc.scalar.activation(out_, in_, ACT.Copy, scale=scale)

            ac.dma_start(rk[:, :, :], wkT).then_inc(d_qk, 16)
            ac.dma_start(rq[:, :, :], wqT).then_inc(d_qk, 16)
            ac.dma_start(rv[:, :, :], wvT).then_inc(d_vo, 16)
            ac.dma_start(ro[:, :, :], wo).then_inc(d_vo, 16)
            ac.dma_start(r_down[:, 0:E, :], w2T).then_inc(d_down, 16)
            ac.dma_start(r_down[:, E, :], sw2T).then_inc(d_down, 16)
            ac.wait_ge(p_relT, 1)
            copy(rel_sumT[:, 0:2 * NP - 1], bank["s0"][0:H, 0:2 * NP - 1]).then_inc(p_relc, 1)
            order = ["logit", "probT", "ca", "cb", "up", "gate_up"]
            n = 0
            for k in range(2):
                for hp in range(HP):
                    for c0, cn in ((0, DA), (DA, DB)):
                        src = bank[order[n % 6]][0:cn, 0:2 * D].rearrange("p (h e) -> p h e", h=2)
                        ac.wait_ge(p_mm, n + 1)
                        hs = slice(2 * hp, 2 * hp + 2)
                        if k == 0:
                            dst = (qk_a[0][:, hp] if c0 == 0 else qk_b[0:DB, hp])
                            copy(dst[:, 0:2, :], src[:, :, 0:DA], DH ** -0.5)
                            copy(dst[:, 2, :].rearrange("p (h e) -> p h e", h=2), src[:, :, DA:D], DH ** -0.5)\
                                .then_inc(p_hi, 1)
                        elif c0 == 0:
                            copy(vo_a[0][:, hs, :], src).then_inc(p_hi, 1)
                        else:
                            copy(vo_b[0][0:DB, hp, :], src[:, 0, :])
                            copy(vo_b[0][DB:2 * DB, hp, :], src[:, 1, :]).then_inc(p_hi, 1)
                        n += 1
            ac.wait_ge(d_small, 16 * SMALL_LOADS)
            copy(gw_a[0][:, :], gw_raw_a[:, :])
            copy(gw_b[0:DB, :], gw_raw_b[:, :]).then_inc(p_hi, 1)
            ac.wait_ge(d_up, 128)
            for c in range(UP_CHUNKS):
                es = slice(3 * c, 3 * c + 3)
                copy(up_a[0][:, es], r_up_a[:, es]).then_inc(p_hi, 1)
                copy(up_b[0:DB, es], r_up_b[:, es]).then_inc(p_hi, 1)
            ac.wait_ge(d_down, 32)
            for c in range(UP_CHUNKS):
                es = slice(3 * c, 3 * c + 3)
                copy(down[0][:, es], r_down[:, es]).then_inc(p_hi, 1)
            ac.wait_ge(d_bias, 16)
            copy(bias[0:NP, :, :], bias_raw[:, :, :]).then_inc(p_hi, 1)

            def prob_hi(s, j):
                ac.wait_ge(*pt_mm.at(s.ag, j + 1))
                if j:
                    ac.wait_ge(*cb_mm.at(s.ag, j))
                elif s.key > 0:
                    ac.wait_ge(*cb_mm.at(s.ag - 1, GB))
                else:
                    ac.wait_ge(p_fill, 6)
                copy(probT[0:NP, :], bank["probT"][0:NP, 0:H * NP]).then_inc(pt_hi.sem, 1)

            def context_hi(s, j):
                pb = j % 2
                if pb == 0:
                    if j:
                        ac.wait_ge(*o_mm.at(s.ag, j // 2))
                    elif s.key > 0:
                        ac.wait_ge(*o_mm.at(s.ag - 1, 2))
                ac.wait_ge(*ca_mm.at(s.ag, j + 1))
                copy(c_a[0][:, :, pb, :], bank["ca"][:, 0:H * NP].rearrange("p (h q) -> p h q", h=H))\
                    .then_inc(ca_hi.sem, 1)
                ac.wait_ge(*cb_mm.at(s.ag, j + 1))
                src = bank["cb"][0:DB, 0:H * NP].rearrange("p (h two q) -> p h two q", h=HP, two=2)
                for par in range(2):
                    copy(c_b[0][par * DB:(par + 1) * DB, :, pb, :], src[:, :, par, :]).then_inc(cb_hi.sem, 1)

            def hidden_hi(s, j):
                n = 2 if j < HP else 1
                if j < HP:
                    ac.wait_ge(*w_ok.at(s.fg, j + 1))
                else:
                    ac.wait_ge(*v_ok.at(s.fg, HP + 1))
                copy(hid[0][:, 2 * j:2 * j + n, :], act[j % 2][:, 0:n, :]).then_inc(hid_hi.sem, 1)

            def gate_tanh(s, j, n):
                ac.wait_ge(*up_mm.at(s.fg, j + 1))
                if j >= 2:
                    ac.wait_ge(*hid_lo.at(s.fg, j - 1))
                elif s.key > 1:
                    ac.wait_ge(*hid_lo.at(s.fg - 1, HP + 1 if j == 0 else HP))
                nc.scalar.activation(act[j % 2][:, 0:n, :], bank["up"][:, 0:n * GT].rearrange("p (e t) -> p e t", e=n),
                                     ACT.Tanh, scale=0.5).then_inc(tanh_ok.sem, 1)

            def score_tanh(s, m):
                ac.wait_ge(*a_mm.at(s.tg, m + 1))
                if s.key < 0:
                    ac.wait_ge(p_rel, 1)
                elif m == 0:
                    ac.wait_ge(*sc_raw.at(s.tg - 1, 1))
                nc.scalar.activation(tanh_sb[:, 2 * m:2 * m + 2, :],
                                     bank["s0"][0:S, 0:2 * D].rearrange("p (e d) -> p e d", e=2), ACT.Tanh)\
                    .then_inc(a_tanh.sem, 1)

            def x_hi(s, sig_mm, sig, g, xa, xb2):
                ac.wait_ge(*sig_mm.at(g, 1))
                copy(xa[0][:, :], bank["s0"][:, 0:GT]).then_inc(sig.sem, 1)
                copy(xb2[0:DB, :], bank["s0"][0:DB, GT:2 * GT]).then_inc(sig.sem, 1)
                copy(xb2[DB:2 * DB, :], bank["s0"][0:DB, GT:2 * GT]).then_inc(sig.sem, 1)

            def z_high(s, n):
                half, kind = n // 3, n % 3
                ac.wait_ge(*z_mm.at(s.tg, n + 1))
                src = bank[USES["z", n][0]]
                if kind < 2:
                    h0 = 4 * half + 2 * kind
                    copy(z_a[0][:, :, h0:h0 + 2, :].rearrange("p b h k -> p h b k"),
                         src[:, 0:2 * GT].rearrange("p (h b k) -> p h b k", h=2, b=GB)).then_inc(z_hi.sem, 1)
                else:
                    for par in range(2):
                        copy(z_b[0:DB, :, 4 * half + par:4 * half + 4:2, :].rearrange("p b h k -> p h b k"),
                             src[par * DB:(par + 1) * DB, 0:2 * GT].rearrange("p (h b k) -> p h b k", h=2, b=GB))\
                            .then_inc(z_hi.sem, 1)

            def body(s):
                for j in range(GB):
                    if s.a:
                        if j:
                            prob_hi(s, j - 1)
                        ac.wait_ge(*sub_ok.at(s.ag, j + 1))
                        nc.scalar.activation(prob[j % 2][:, :, :], prob[j % 2][:, :, :], ACT.Exp).then_inc(exp_ok.sem, 1)
                    if s.f:
                        gate_tanh(s, j, 2)
                    if s.a and j:
                        context_hi(s, j - 1)
                    if s.t and j == 0:
                        score_tanh(s, 0)
                    if s.f and j == 0:
                        ac.wait_ge(*cwt_mm.at(s.fg, 1))
                        if s.key > 1:
                            ac.wait_ge(*cw_mm.at(s.fg - 1, HP))
                        else:
                            ac.wait_ge(p_fill, 6)
                        copy(cwT[0:E, :], bank["s1"][0:E, 0:GT]).then_inc(cwt_hi.sem, 1)
                    if s.t and j == 0:
                        score_tanh(s, 1)
                    if s.f:
                        ac.wait_ge(*cw_mm.at(s.fg, j + 1))
                        if j:
                            ac.wait_ge(*w_ok.at(s.fg, j))
                        elif s.key > 1:
                            ac.wait_ge(*w_ok.at(s.fg - 1, HP))
                        copy(cw_sb[:, :, :], bank["s1"][:, 0:2 * GT].rearrange("p (e t) -> p e t", e=2))\
                            .then_inc(cw_ok.sem, 1)
                        hidden_hi(s, j)
                    if s.t and j == 3:
                        ac.wait_ge(*band_in.at(s.tg, 1))
                        nc.scalar.activation(band[:, :, :], band[:, :, :], ACT.Exp).then_inc(band_e.sem, 1)
                if s.a:
                    prob_hi(s, GB - 1)
                if s.t:
                    ac.wait_ge(*mix_mm.at(s.tg, 1))
                    if s.key >= 0:
                        ac.wait_ge(*p_mm2.at(s.tg - 1, 1))
                    copy(mix_a[:, :], bank["s0"][:, 0:GT]).then_inc(mix_sb.sem, 1)
                    copy(mix_b[:, :], bank["s0"][0:DB, GT:2 * GT]).then_inc(mix_sb.sem, 1)
                if s.f:
                    gate_tanh(s, HP, 1)
                if s.a:
                    context_hi(s, GB - 1)
                if s.f:
                    hidden_hi(s, HP)
                if s.t:
                    ac.wait_ge(*xn1_ok.at(s.tg, 2))
                    if s.key >= 0:
                        ac.wait_ge(*xc_moved.at(s.tg - 1, 96))
                    copy(xn_half[0][:, :, :], xn1[:, :, :]).then_inc(xn_hi_ok.sem, 1)
                    x_hi(s, x1_mm, x1_hi, s.tg, x1_a, x1_b2)
                    if s.key < 0:
                        ac.wait_ge(p_lo, 27)
                    for n in range(3):
                        z_high(s, n)
                if s.a:
                    x_hi(s, x2_mm, x2_hi, s.ag, x2_a, x2_b2)
                if s.t:
                    for n in range(3, 6):
                        z_high(s, n)
                    if s.a:
                        ac.wait_ge(*h2_ok.at(s.ag, 2))
                    else:
                        ac.wait_ge(*h1_ok.at(s.tg, 2))
                    copy(h1_res[:, :, :], h1[:, :, :]).then_inc(h1_kept.sem, 1)
                if s.a:
                    if s.f:
                        ac.wait_ge(*out_ok.at(s.fg, 2))
                    else:
                        ac.wait_ge(*h2_ok.at(s.ag, 2))
                    copy(h2_res[:, :, :], h2[:, :, :]).then_inc(h2_kept.sem, 1)
                    ac.wait_ge(*g_mm.at(s.ag, 1))
                    nc.scalar.activation(g_tanh[:, :], bank["s1"][0:TT, 0:PAIRS * E], ACT.Tanh, scale=0.5)\
                        .then_inc(g_th.sem, 1)

            sections(ac, body)

        @block.vector
        def _(ve):
            v = nc.vector

            def low(out_, src, hi):
                return v.tensor_tensor(out_, src, hi.bitcast(FP32), ALU.subtract)

            v.memset(ones[:, :], 1.0).then_inc(p_fill, 1)
            v.memset(minus_half[:, :], -0.5).then_inc(p_fill, 1)
            v.memset(xin_b[DB:DB + 2, :], 1.0).then_inc(p_fill, 1)
            v.memset(probT[32:LO, :].bitcast(FP32), 0.0).then_inc(p_fill, 1)
            v.memset(xc_hi[32:LO, :, :].bitcast(FP32), 0.0)
            v.memset(bias[32:LO, :, :].bitcast(FP32), 0.0).then_inc(p_fill, 1)
            v.memset(cwT[:, :].bitcast(FP32), 0.0).then_inc(p_fill, 1)
            ve.wait_ge(d_rel, 16)
            v.tensor_reduce(rel_sum[:, :], rel_raw, axis=AX, op=ALU.add).then_inc(p_rel, 1)
            ve.wait_ge(d_small, 16 * SMALL_LOADS)
            v.tensor_copy(ident_r[:, :], ident[0:S, 0:S])
            v.tensor_copy(band_mask[:, :], band_raw[:, :])
            v.tensor_copy(flip[:, :], flip_raw[:, :])
            v.tensor_copy(pick[:, :, :], pick_raw[:, :, :]).then_inc(p_const, 1)
            order = ["logit", "probT", "ca", "cb", "up", "gate_up"]
            n = 0
            for k in range(2):
                for hp in range(HP):
                    for c0, cn in ((0, DA), (DA, DB)):
                        src = bank[order[n % 6]][0:cn, 0:2 * D].rearrange("p (h e) -> p h e", h=2)
                        ve.wait_ge(p_hi, n + 1)
                        hs = slice(2 * hp, 2 * hp + 2)
                        if k == 0:
                            hi, lo = ((qk_a[0][:, hp], qk_a[1][:, hp]) if c0 == 0 else
                                      (qk_b[0:DB, hp], qk_b[DB:2 * DB, hp]))
                            for o_, i_, h_ in ((lo[:, 0:2, :], src[:, :, 0:DA], hi[:, 0:2, :]),
                                               (lo[:, 2, :].rearrange("p (h e) -> p h e", h=2), src[:, :, DA:D],
                                                hi[:, 2, :].rearrange("p (h e) -> p h e", h=2))):
                                last = v.scalar_tensor_tensor(out=o_, in0=i_, scalar=DH ** -0.5, in1=h_.bitcast(FP32),
                                                              op0=ALU.mult, op1=ALU.subtract)
                            last.then_inc(p_lo, 1)
                        elif c0 == 0:
                            low(vo_a[1][:, hs, :], src, vo_a[0][:, hs, :]).then_inc(p_lo, 1)
                        else:
                            low(vo_b[1][0:DB, hp, :], src[:, 0, :], vo_b[0][0:DB, hp, :])
                            low(vo_b[1][DB:2 * DB, hp, :], src[:, 1, :], vo_b[0][DB:2 * DB, hp, :]).then_inc(p_lo, 1)
                        n += 1
            ve.wait_ge(p_hi, 17)
            low(gw_a[1][:, :], gw_raw_a[:, :], gw_a[0][:, :])
            low(gw_b[DB:2 * DB, :], gw_raw_b[:, :], gw_b[0:DB, :]).then_inc(p_lo, 1)
            for c in range(UP_CHUNKS):
                es = slice(3 * c, 3 * c + 3)
                ve.wait_ge(p_hi, 18 + 2 * c)
                low(up_a[1][:, es], r_up_a[:, es], up_a[0][:, es]).then_inc(p_lo, 1)
                ve.wait_ge(p_hi, 19 + 2 * c)
                low(up_b[DB:2 * DB, es], r_up_b[:, es], up_b[0:DB, es]).then_inc(p_lo, 1)
            for c in range(UP_CHUNKS):
                es = slice(3 * c, 3 * c + 3)
                ve.wait_ge(p_hi, 24 + c)
                low(down[1][:, es], r_down[:, es], down[0][:, es]).then_inc(p_lo, 1)
            ve.wait_ge(p_hi, 27)
            ve.wait_ge(p_fill, 6)
            low(bias[LO:KS, :, :], bias_raw[:, :, :], bias[0:NP, :, :]).then_inc(p_lo, 1)

            def norm_stats(s, g, t, src, st, mv, src_ok, st_ok, mv_ok):
                ve.wait_ge(*src_ok.at(g, t + 1))
                v.bn_stats(st[:, t, :], src[:, t, :]).then_inc(st_ok.sem, 1)
                ve.wait_ge(*st_ok.at(g, t + 1))
                v.memset(wait_cell[:, :], 0.0)
                v.bn_aggr(mv[:, t, :], st[:, t, :]).then_inc(mv_ok.sem, 1)

            def norm_eps(s, g, mv, veps, mv_ok, ve_ok):
                ve.wait_ge(*mv_ok.at(g, 2))
                v.tensor_scalar(veps[:, :], mv[:, :, 1], LN_EPS, None, ALU.add).then_inc(ve_ok.sem, 1)

            def norm_apply(s, g, src, mv, rs, dst, rs_ok, ok):
                ve.wait_ge(*rs_ok.at(g, 1))
                for t in range(PAIRS):
                    v.tensor_scalar(dst[:, t, :], src[:, t, :], mv[:, t, 0:1], rs[:, t:t + 1], ALU.subtract, ALU.mult)\
                        .then_inc(ok.sem, 1)

            def prob_lo(s, j):
                ve.wait_ge(*pt_hi.at(s.ag, j + 1))
                low(probT[LO:KS, :], bank["probT"][0:NP, 0:H * NP], probT[0:NP, :]).then_inc(pt_lo.sem, 1)

            def context_lo(s, j):
                pb = j % 2
                ve.wait_ge(*ca_hi.at(s.ag, j + 1))
                low(c_a[1][:, :, pb, :], bank["ca"][:, 0:H * NP].rearrange("p (h q) -> p h q", h=H),
                    c_a[0][:, :, pb, :]).then_inc(ca_lo.sem, 1)
                ve.wait_ge(*cb_hi.at(s.ag, 2 * j + 2))
                src = bank["cb"][0:DB, 0:H * NP].rearrange("p (h two q) -> p h two q", h=HP, two=2)
                for par in range(2):
                    p = slice(par * DB, (par + 1) * DB)
                    low(c_b[1][p, :, pb, :], src[:, :, par, :], c_b[0][p, :, pb, :]).then_inc(cb_lo.sem, 1)

            def gate_product(s, j, n):
                a = act[j % 2][:, 0:n, :].rearrange("p e t -> p (e t)")
                ve.wait_ge(*tanh_ok.at(s.fg, j + 1))
                v.scalar_tensor_tensor(out=a, in0=a, scalar=1.0, in1=bank["up"][:, 0:n * GT], op0=ALU.add,
                                       op1=ALU.mult).then_inc(u_ok.sem, 1)
                ve.wait_ge(*u_ok.at(s.fg, j + 1))
                other = bank["gate_up"][:, 0:n * GT] if n == 2 else bank["up"][:, GT:2 * GT]
                v.scalar_tensor_tensor(out=a, in0=a, scalar=0.5, in1=other, op0=ALU.mult, op1=ALU.mult)\
                    .then_inc(v_ok.sem, 1)

            def residual(s, t):
                ve.wait_ge(*o_mm.at(s.ag, t + 1))
                if t == 0:
                    ve.wait_ge(*h1_kept.at(s.ag, 1))
                    if s.key > 0:
                        ve.wait_ge(*h2_kept.at(s.ag - 1, 1))
                v.tensor_tensor(h2[:, t, :], bank["s1"][0:TT, 0:D], h1_res[:, t, :], ALU.add).then_inc(h2_ok.sem, 1)
                norm_stats(s, s.ag, t, h2, st2, mv2, h2_ok, st2_ok, mv2_ok)

            def emit(s, t):
                ve.wait_ge(*y_mm.at(s.fg, t + 1))
                if t == 0:
                    ve.wait_ge(*h2_kept.at(s.fg, 1))
                    if s.key > 1:
                        ve.wait_ge(*out_sent.at(s.fg - 1, 16))
                v.tensor_tensor(out_sb[:, t, :], bank[USES["y", t][0]][0:TT, 0:D], h2_res[:, t, :], ALU.add)\
                    .then_inc(out_ok.sem, 1)

            def x_low(s, sig_hi, sig, g, xa, xb2, xblo):
                ve.wait_ge(*sig_hi.at(g, 3))
                low(xa[1][:, :], bank["s0"][:, 0:GT], xa[0][:, :]).then_inc(sig.sem, 1)
                low(xblo[:, :], bank["s0"][0:DB, GT:2 * GT], xb2[0:DB, :]).then_inc(sig.sem, 1)

            def z_low(s, n):
                half, kind = n // 3, n % 3
                src = bank[USES["z", n][0]]
                done = 4 * half + (kind + 1 if kind < 2 else 4)
                ve.wait_ge(*z_hi.at(s.tg, done))
                if kind < 2:
                    h0 = 4 * half + 2 * kind
                    low(z_a[1][:, :, h0:h0 + 2, :].rearrange("p b h k -> p h b k"),
                        src[:, 0:2 * GT].rearrange("p (h b k) -> p h b k", h=2, b=GB),
                        z_a[0][:, :, h0:h0 + 2, :].rearrange("p b h k -> p h b k")).then_inc(z_lo.sem, 1)
                else:
                    for par in range(2):
                        hs = slice(4 * half + par, 4 * half + 4, 2)
                        low(z_b[DB:2 * DB, :, hs, :].rearrange("p b h k -> p h b k"),
                            src[par * DB:(par + 1) * DB, 0:2 * GT].rearrange("p (h b k) -> p h b k", h=2, b=GB),
                            z_b[0:DB, :, hs, :].rearrange("p b h k -> p h b k")).then_inc(z_lo.sem, 1)

            def choose(s):
                g, n = s.ag, [0]

                def then(ins):
                    n[0] += 1
                    ins.then_inc(g_step.sem, 1)
                    ve.wait_ge(*g_step.at(g, n[0]))

                def rank(val, cmp, eq, below, res, m):
                    vj = val[:, :, :].unsqueeze(2).to_broadcast([TT, PAIRS, m, m])
                    vi = val[:, :, :].unsqueeze(3).to_broadcast([TT, PAIRS, m, m])
                    c4, e4 = (q[:, :, :].rearrange("p t (i j) -> p t i j", i=m) for q in (cmp, eq))
                    lo = below[:, :].unsqueeze(1).to_broadcast([TT, PAIRS, m * m])
                    then(v.tensor_tensor(c4, vj, vi, ALU.is_gt))
                    then(v.tensor_tensor(e4, vj, vi, ALU.is_equal))
                    then(v.tensor_tensor(eq[:, :, :], eq[:, :, :], lo, ALU.mult))
                    then(v.tensor_tensor(cmp[:, :, :], cmp[:, :, :], eq[:, :, :], ALU.add))
                    then(v.tensor_reduce(res[:, :, :], c4, axis=AX, op=ALU.add))

                ve.wait_ge(*g_th.at(g, 1))
                if s.key > 0:
                    ve.wait_ge(*cwt_mm.at(g - 1, 1))
                sig = g_sig[:, :, :].rearrange("p t e -> p (t e)")
                then(v.tensor_scalar(sig, g_tanh[:, :], 0.5, 0.5, ALU.mult, ALU.add))
                then(v.tensor_tensor(g_sb[:, :, :], g_sig[:, :, :], gb_row[:, :].unsqueeze(1).to_broadcast([TT, PAIRS, E]),
                                     ALU.add))
                pairs = g_sb[:, :, :].rearrange("p t (g two) -> p t g two", two=2)
                then(v.tensor_tensor(g_grp[:, :, :], pairs[:, :, :, 0], pairs[:, :, :, 1], ALU.add))
                rank(g_grp, g_cmp4, g_eq4, lt4, g_rank4, 4)
                then(v.tensor_scalar(g_sel4[:, :, :], g_rank4[:, :, :], 2.0, 2 * BIG, ALU.is_lt, ALU.mult))
                then(v.tensor_scalar(g_sel4[:, :, :], g_sel4[:, :, :], BIG, None, ALU.subtract))
                then(v.tensor_tensor(g_msk[:, :, :].rearrange("p t (g two) -> p t g two", two=2), pairs,
                                     g_sel4[:, :, :].unsqueeze(3).to_broadcast([TT, PAIRS, 4, 2]), ALU.min))
                rank(g_msk, g_cmp8, g_eq8, lt8, g_rank8, 8)
                then(v.scalar_tensor_tensor(out=g_w[:, :, :], in0=g_rank8[:, :, :], scalar=2.0, in1=g_sig[:, :, :],
                                            op0=ALU.is_lt, op1=ALU.mult))
                then(v.tensor_reduce(g_sum[:, :], g_w[:, :, :], axis=AX, op=ALU.add))
                then(v.tensor_scalar(g_sum[:, :], g_sum[:, :], 1e-6, None, ALU.add))
                then(v.reciprocal(g_rec[:, :], g_sum[:, :]))
                then(v.tensor_tensor(g_cw[:, :, :], g_w[:, :, :], g_rec[:, :].unsqueeze(2).to_broadcast([TT, PAIRS, E]),
                                     ALU.mult))
                while n[0] < GATE_STEPS:
                    then(v.tensor_scalar(g_sum[:, :], g_sum[:, :], 1.0, None, ALU.mult))

            def body(s):
                for j in range(GB):
                    if s.a:
                        p = prob[j % 2]
                        ve.wait_ge(*l_mm.at(s.ag, j + 1))
                        lg = bank["logit"][0:NP, 0:H * NP].rearrange("p (h k) -> p h k", h=H)
                        v.tensor_reduce(row_max[:, :], lg, axis=AX, op=ALU.max).then_inc(mx_ok.sem, 1)
                        ve.wait_ge(*mx_ok.at(s.ag, j + 1))
                        if j >= 2:
                            ve.wait_ge(*pt_mm.at(s.ag, j - 1))
                        elif s.key > 0:
                            ve.wait_ge(*pt_mm.at(s.ag - 1, j + 3))
                        v.tensor_tensor(p[:, :, :], lg, row_max[:, :].unsqueeze(2).to_broadcast([NP, H, NP]),
                                        ALU.subtract).then_inc(sub_ok.sem, 1)
                        if j:
                            prob_lo(s, j - 1)
                        ve.wait_ge(*exp_ok.at(s.ag, j + 1))
                        v.tensor_reduce(row_sum[:, :], p[:, :, :], axis=AX, op=ALU.add).then_inc(sum_ok.sem, 1)
                        ve.wait_ge(*sum_ok.at(s.ag, j + 1))
                        if j:
                            ve.wait_ge(*pn_ok.at(s.ag, j))
                        elif s.key > 0:
                            ve.wait_ge(*pn_ok.at(s.ag - 1, GB))
                        v.reciprocal(row_rec[:, :], row_sum[:, :]).then_inc(rec_ok.sem, 1)
                        if j == 3:
                            residual(s, 0)
                    if s.f:
                        gate_product(s, j, 2)
                    if s.a and j:
                        context_lo(s, j - 1)
                    if s.f and j == 0:
                        ve.wait_ge(*cwt_hi.at(s.fg, 1))
                        low(cwT[32:32 + E, :], bank["s1"][0:E, 0:GT], cwT[0:E, :]).then_inc(cwt_lo.sem, 1)
                    if s.t and j == 1:
                        ve.wait_ge(*av.at(s.tg, 1))
                        v.tensor_reduce(score_raw[:, :], tanh_sb[:, :, :], axis=AX, op=ALU.add).then_inc(sc_raw.sem, 1)
                        ve.wait_ge(*sc_raw.at(s.tg, 1))
                        v.tensor_scalar(score[:, :], score_raw[:, :], vb_col[:, 0:1], None, ALU.add)\
                            .then_inc(sc.sem, 1)
                    if s.t and j == 2:
                        ve.wait_ge(*scT.at(s.tg, 1))
                        win = bass.AP(bank["s0"], 0, [[512, GB], [2, NP], [1, 4]])
                        v.tensor_reduce(neg_max[:, :], win, axis=AX, op=ALU.max, negate=True).then_inc(nm.sem, 1)
                        ve.wait_ge(*nm.at(s.tg, 1))
                        v.tensor_tensor(max_diag[:, :, :], diag_mask[:, :, :],
                                        neg_max[:, :].unsqueeze(1).to_broadcast([GB, GB, NP]), ALU.mult)\
                            .then_inc(nmd.sem, 1)
                    if s.t and j == 3:
                        ve.wait_ge(*band_mm.at(s.tg, 1))
                        v.tensor_tensor(band[:, :, :], bank["s0"][0:S, 0:GT].rearrange("p (b q) -> p b q", b=GB),
                                        score[:, :].unsqueeze(2).to_broadcast([S, GB, NP]), ALU.add)\
                            .then_inc(band_in.sem, 1)
                if s.a:
                    prob_lo(s, GB - 1)
                if s.t:
                    ve.wait_ge(*mix_sb.at(s.tg, 2))
                    v.reciprocal(band_rden[:, :], bank["s0"][0:TT, 2 * GT:2 * GT + PAIRS]).then_inc(rden.sem, 1)
                if s.f:
                    gate_product(s, HP, 1)
                if s.a:
                    context_lo(s, GB - 1)
                if s.t:
                    ve.wait_ge(*p_mm2.at(s.tg, 1))
                    ve.wait_ge(*rden.at(s.tg, 1))
                    if s.key >= 0:
                        ve.wait_ge(*h1_kept.at(s.tg - 1, 1))
                    for t in range(PAIRS):
                        v.scalar_tensor_tensor(out=h1[:, t, :], in0=bank["s1"][0:TT, t * D:(t + 1) * D],
                                               scalar=band_rden[:, t:t + 1], in1=pb_row[:, :], op0=ALU.mult,
                                               op1=ALU.add).then_inc(h1_ok.sem, 1)
                    for t in range(PAIRS):
                        norm_stats(s, s.tg, t, h1, st1, mv1, h1_ok, st1_ok, mv1_ok)
                    norm_eps(s, s.tg, mv1, ve1, mv1_ok, ve1_ok)
                if s.f:
                    emit(s, 0)
                if s.t:
                    if s.key >= 0:
                        ve.wait_ge(*xn_lo_ok.at(s.tg - 1, 1))
                        ve.wait_ge(*xn_hi_ok.at(s.tg - 1, 1))
                    norm_apply(s, s.tg, h1, mv1, rs1, xn1, rs1_ok, xn1_ok)
                if s.a:
                    residual(s, 1)
                    norm_eps(s, s.ag, mv2, ve2, mv2_ok, ve2_ok)
                if s.t:
                    x_low(s, x1_hi, x1_lo, s.tg, x1_a, x1_b2, x1_blo)
                if s.a:
                    norm_apply(s, s.ag, h2, mv2, rs2, xn2, rs2_ok, xn2_ok)
                if s.f:
                    emit(s, 1)
                if s.t:
                    for n in range(3):
                        z_low(s, n)
                if s.a:
                    x_low(s, x2_hi, x2_lo, s.ag, x2_a, x2_b2, x2_blo)
                if s.t:
                    for n in range(3, 6):
                        z_low(s, n)
                if s.a:
                    choose(s)

            sections(ve, body)

        @block.gpsimd
        def _(po):
            p = nc.gpsimd
            po.dma_start(rel_raw, rel).then_inc(d_rel, 16)
            for dst, src in ((ident[:, :], c_ident), (band_raw[:, :], c_band), (diag_mask[:, :, :], c_diag),
                             (flip_raw[:, :], c_flip), (pick_raw[:, :, :], c_pick),
                             (lt4[:, :], c_lt4.partition_broadcast(TT)), (lt8[:, :], c_lt8.partition_broadcast(TT)),
                             (v_row[:, :], tok_v.partition_broadcast(S)), (vb_col[:, :], tok_vb.partition_broadcast(S)),
                             (pb_row[:, :], tok_pb.partition_broadcast(TT)),
                             (gb_row[:, :], gate_b.partition_broadcast(TT)),
                             (gw_raw_a[:, :], gate_w[0:DA, :]), (gw_raw_b[:, :], gate_w[DA:D, :])):
                po.dma_start(dst, src).then_inc(d_small, 16)
            po.wait_ge(d_small, 16 * SMALL_LOADS)

            def inv_sqrt(g, ve_ok, veps, rs, ok):
                po.wait_ge(*ve_ok.at(g, 1))
                p.tensor_tensor(rs[:, :], veps[:, :], minus_half[:, :], ALU.pow).then_inc(ok.sem, 1)

            def hidden_lo(s, j):
                n = 2 if j < HP else 1
                po.wait_ge(*hid_hi.at(s.fg, j + 1))
                p.tensor_tensor(hid[1][:, 2 * j:2 * j + n, :], act[j % 2][:, 0:n, :],
                                hid[0][:, 2 * j:2 * j + n, :].bitcast(FP32), ALU.subtract).then_inc(hid_lo.sem, 1)

            def body(s):
                for j in range(GB):
                    if s.a:
                        po.wait_ge(*rec_ok.at(s.ag, j + 1))
                        q = prob[j % 2][:, :, :]
                        p.tensor_tensor(q, q, row_rec[:, :].unsqueeze(2).to_broadcast([NP, H, NP]), ALU.mult)\
                            .then_inc(pn_ok.sem, 1)
                    if s.t and j == 0:
                        po.wait_ge(*a_tanh.at(s.tg, 2))
                        p.tensor_tensor(tanh_sb[:, :, :], tanh_sb[:, :, :],
                                        v_row[:, :].unsqueeze(1).to_broadcast([S, GB, D]), ALU.mult).then_inc(av.sem, 1)
                    if s.f:
                        po.wait_ge(*v_ok.at(s.fg, j + 1))
                        po.wait_ge(*cw_ok.at(s.fg, j + 1))
                        a = act[j % 2][:, :, :]
                        p.tensor_tensor(a, a, cw_sb[:, :, :], ALU.mult).then_inc(w_ok.sem, 1)
                        hidden_lo(s, j)
                if s.f:
                    hidden_lo(s, HP)
                if s.t:
                    inv_sqrt(s.tg, ve1_ok, ve1, rs1, rs1_ok)
                    po.wait_ge(*xn_hi_ok.at(s.tg, 1))
                    if s.key >= 0:
                        po.wait_ge(*xc_moved.at(s.tg - 1, 96))
                    p.tensor_tensor(xn_half[1][:, :, :], xn1[:, :, :], xn_half[0][:, :, :].bitcast(FP32), ALU.subtract)\
                        .then_inc(xn_lo_ok.sem, 1)
                if s.a:
                    inv_sqrt(s.ag, ve2_ok, ve2, rs2, rs2_ok)

            sections(po, body)


def kernel(x, L0_tok_W_w, L0_tok_W_b, L0_tok_b, L0_tok_V_w, L0_tok_V_b, L0_tok_P_w, L0_tok_P_b, L0_attn_w_q,
           L0_attn_w_k, L0_attn_w_v, L0_attn_w_o, L0_attn_rel_emb, L0_ffn_gate_weight, L0_ffn_gate_bias, L0_ffn_w1,
           L0_ffn_w2, L0_ffn_w3, L0_ffn_sw1, L0_ffn_sw2, L0_ffn_sw3):
    import numpy as np
    import concourse.bacc as bacc
    from concourse.bass_utils import run_bass_kernel_spmd

    def put(a):
        return np.ascontiguousarray(np.asarray(a))

    x = put(x)
    n = np.arange
    ident = np.eye(128, dtype=np.float32)
    off = n(S)[:, None] - 2 * n(NP)[None, :]
    band = np.where((off >= 0) & (off < 4), 0.0, -1e30).astype(np.float32)
    diag = np.repeat(np.eye(GB, dtype=np.float32)[:, :, None], NP, axis=2)
    flip = np.zeros((KS, NP), np.float32)
    flip[n(NP), NP - 1 - n(NP)] = 1.0
    flip[LO + n(NP), NP - 1 - n(NP)] = 1.0
    pick = np.zeros((40, E, 128), np.float32)
    pick[n(E), n(E), :] = 1.0
    pick[32 + n(E), n(E), :] = 1.0
    below = lambda m: (n(m)[None, :] < n(m)[:, None]).astype(np.float32).reshape(-1)
    arrays = {
        "x": x, "xT": put(x.reshape(B * S, D).T),
        "tok_wT": put(np.asarray(L0_tok_W_w).T), "tok_bias": put(np.stack([np.asarray(L0_tok_W_b), np.asarray(L0_tok_b)])),
        "tok_v": put(np.asarray(L0_tok_V_w).reshape(D)), "tok_vb": put(L0_tok_V_b),
        "tok_pT": put(np.asarray(L0_tok_P_w).T), "tok_pb": put(L0_tok_P_b),
        "wqT": put(np.asarray(L0_attn_w_q).transpose(2, 0, 1)), "wkT": put(np.asarray(L0_attn_w_k).transpose(2, 0, 1)),
        "wvT": put(np.asarray(L0_attn_w_v).transpose(2, 0, 1)), "wo": put(np.asarray(L0_attn_w_o).transpose(1, 0, 2)),
        "rel": put(np.asarray(L0_attn_rel_emb)[:, 100 - NP:100 + NP - 1, :, 0].transpose(1, 0, 2)),
        "gate_w": put(np.asarray(L0_ffn_gate_weight).T), "gate_b": put(L0_ffn_gate_bias),
        "w1T": put(np.asarray(L0_ffn_w1).transpose(2, 0, 1)), "w3T": put(np.asarray(L0_ffn_w3).transpose(2, 0, 1)),
        "w2T": put(np.asarray(L0_ffn_w2).transpose(2, 0, 1)),
        "sw1T": put(np.asarray(L0_ffn_sw1).T), "sw3T": put(np.asarray(L0_ffn_sw3).T), "sw2T": put(np.asarray(L0_ffn_sw2).T),
        "c_ident": ident, "c_band": put(np.tile(band, (1, GB))), "c_diag": put(diag), "c_flip": flip, "c_pick": pick,
        "c_lt4": put(below(4)), "c_lt8": put(below(8)),
    }
    nc = bacc.Bacc("TRN2", target_bir_lowering=False, num_devices=1)
    feeds, args = {}, []
    for name, a in arrays.items():
        feeds[f"in_{name}"] = a
        args.append(nc.dram_tensor(f"in_{name}", a.shape, mybir.dt.from_np(a.dtype), kind="ExternalInput").ap())
    out = nc.dram_tensor("out", (B, NP, D), FP32, kind="ExternalOutput").ap()
    audio_tower_kernel(nc, *args, out)
    return run_bass_kernel_spmd(nc, [feeds], core_ids=[0]).results[0]["out"]
```

```python
import concourse.bass as bass
from concourse import mybir
from contextlib import ExitStack

FP32 = mybir.dt.float32
F32R = mybir.dt.float32r
ALU = mybir.AluOpType
ACT = mybir.ActivationFunctionType
AX = mybir.AxisListType.X

B, S, D = 64, 125, 192
NP = (S - 4) // 2 + 1
H, DH = 8, 96
E, INTER = 8, 128
GB = 4
NG = B // GB
PAIRS = GB // 2
TT = 2 * NP
GT = GB * NP
DA, DB = 128, D - 128
LO = 64
KS = LO + NP
HP = H // 2
LN_EPS = 1e-5
BIG = 1.5e38


class Signal:

    def __init__(self, sem, per_group):
        self.sem, self.n = sem, per_group

    def at(self, g, k):
        return self.sem, g * self.n + k


def split_product(pe, out, xa_hi, xa_lo, xb2, xb_lo, wa_hi, wa_lo, wb):
    pe.matmul(out, xa_hi, wa_hi, start=True, stop=False)
    pe.matmul(out, xa_hi, wa_lo, start=False, stop=False)
    pe.matmul(out, xa_lo, wa_hi, start=False, stop=False)
    pe.matmul(out, xb2, wb, start=False, stop=False)
    return pe.matmul(out, xb_lo, wb[0:DB], start=False, stop=True)


def audio_tower_kernel(nc, x, xT, tok_wT, tok_bias, tok_v, tok_vb, tok_pT, tok_pb, wqT, wkT, wvT, wo, rel, gate_w,
                       gate_b, w1T, w3T, w2T, sw1T, sw3T, sw2T, c_ident, c_band, c_diag, c_flip, c_pick, c_lt4,
                       c_lt8, out):
    scratch = nc.dram_tensor("bias_sums", [H, 2 * NP], FP32, kind="Internal")

    ctx = ExitStack()
    with ctx:
        def sb(name, shape, dt=FP32, where=ctx):
            return where.enter_context(nc.sbuf_tensor(name, shape, dt))

        def sem(name):
            return ctx.enter_context(nc.semaphore(name))

        def signal(name, per_group):
            return Signal(sem(name), per_group)

        qk_a = [sb(f"qk_a{n}", [DA, HP, 3, 128], F32R) for n in range(2)]
        qk_b = sb("qk_b", [2 * DB, HP, 3, 128], F32R)
        vo_a = [sb(f"vo_a{n}", [DA, H, D], F32R) for n in range(2)]
        vo_b = [sb(f"vo_b{n}", [2 * DB, HP, D], F32R) for n in range(2)]
        up_a = [sb(f"up_a{n}", [DA, E + 1, 2, INTER], F32R) for n in range(2)]
        up_b = sb("up_b", [2 * DB, E + 1, 2, INTER], F32R)
        down = [sb(f"down{n}", [INTER, E + 1, D], F32R) for n in range(2)]
        gw_a = [sb(f"gw_a{n}", [DA, E], F32R) for n in range(2)]
        gw_b = sb("gw_b", [2 * DB, E], F32R)
        bias = sb("bias", [KS, H, NP], F32R)
        tw_a, tw_b = sb("tw_a", [DA, D]), sb("tw_b", [DB + 2, D])
        tp_a, tp_b = sb("tp_a", [DA, D]), sb("tp_b", [DB, D])
        v_row, vb_col = sb("v_row", [S, D]), sb("vb_col", [S, 1])
        pb_row, gb_row = sb("pb_row", [TT, D]), sb("gb_row", [TT, E])
        ident = sb("ident", [128, 128])
        ident_r = sb("ident_r", [S, S], F32R)
        band_raw, band_mask = sb("band_raw", [S, GB * NP]), sb("band_mask", [S, GB * NP], F32R)
        diag_mask = sb("diag_mask", [GB, GB, NP])
        flip_raw, flip = sb("flip_raw", [KS, NP]), sb("flip", [KS, NP], F32R)
        pick_raw, pick = sb("pick_raw", [40, E, 128]), sb("pick", [40, E, 128], F32R)
        lt4, lt8 = sb("lt4", [TT, 16]), sb("lt8", [TT, 64])
        ones = sb("ones", [128, 128])
        minus_half = sb("minus_half", [TT, PAIRS])
        wait_cell = sb("wait_cell", [TT, 1])
        xin_a, xin_b = sb("xin_a", [DA, GB * S]), sb("xin_b", [DB + 2, GB * S])
        xin = sb("xin", [S, GB, D])
        tanh_sb = sb("tanh_sb", [S, GB, D])
        score_raw, score = sb("score_raw", [S, GB]), sb("score", [S, GB])
        neg_max, max_diag = sb("neg_max", [GB, NP]), sb("max_diag", [GB, GB, NP])
        band = sb("band", [S, GB, NP])
        mix_a, mix_b = sb("mix_a", [DA, GT]), sb("mix_b", [DB, GT])
        band_rden = sb("band_rden", [TT, PAIRS])
        h1, h1_res = sb("h1", [TT, PAIRS, D]), sb("h1_res", [TT, PAIRS, D])
        st1, mv1, ve1, rs1 = (sb("st1", [TT, PAIRS, 6]), sb("mv1", [TT, PAIRS, 2]), sb("ve1", [TT, PAIRS]),
                              sb("rs1", [TT, PAIRS]))
        xn1 = sb("xn1", [TT, PAIRS, D])
        xn_half = [sb(f"xn_half{n}", [TT, PAIRS, D], F32R) for n in range(2)]
        xc_hi = sb("xc_hi", [KS, GB, D], F32R)
        xc_lo = sb("xc_lo", [NP, GB, D], F32R)
        x1_a = [sb(f"x1_a{n}", [DA, GT], F32R) for n in range(2)]
        x1_b2, x1_blo = sb("x1_b2", [2 * DB, GT], F32R), sb("x1_blo", [DB, GT], F32R)
        prob = [sb(f"prob{n}", [NP, H, NP]) for n in range(2)]
        row_max, row_sum, row_rec = (sb("row_max", [NP, H]), sb("row_sum", [NP, H]), sb("row_rec", [NP, H]))
        probT = sb("probT", [KS, H * NP], F32R)
        h2, h2_res = sb("h2", [TT, PAIRS, D]), sb("h2_res", [TT, PAIRS, D])
        st2, mv2, ve2, rs2 = (sb("st2", [TT, PAIRS, 6]), sb("mv2", [TT, PAIRS, 2]), sb("ve2", [TT, PAIRS]),
                              sb("rs2", [TT, PAIRS]))
        xn2 = sb("xn2", [TT, PAIRS, D])
        x2_a = [sb(f"x2_a{n}", [DA, GT], F32R) for n in range(2)]
        x2_b2, x2_blo = sb("x2_b2", [2 * DB, GT], F32R), sb("x2_blo", [DB, GT], F32R)
        g_tanh, g_sig, g_sb = (sb("g_tanh", [TT, PAIRS * E]), sb("g_sig", [TT, PAIRS, E]), sb("g_sb", [TT, PAIRS, E]))
        g_grp, g_rank4, g_sel4 = (sb("g_grp", [TT, PAIRS, 4]), sb("g_rank4", [TT, PAIRS, 4]), sb("g_sel4", [TT, PAIRS, 4]))
        g_cmp4, g_eq4 = sb("g_cmp4", [TT, PAIRS, 16]), sb("g_eq4", [TT, PAIRS, 16])
        g_msk = sb("g_msk", [TT, PAIRS, E])
        g_cmp8, g_eq8 = sb("g_cmp8", [TT, PAIRS, 64]), sb("g_eq8", [TT, PAIRS, 64])
        g_rank8, g_w = sb("g_rank8", [TT, PAIRS, E]), sb("g_w", [TT, PAIRS, E])
        g_sum, g_rec = sb("g_sum", [TT, PAIRS]), sb("g_rec", [TT, PAIRS])
        g_cw = sb("g_cw", [TT, PAIRS, E])
        cwT = sb("cwT", [40, GT], F32R)
        act = [sb(f"act{n}", [INTER, 2, GT]) for n in range(2)]
        out_sb = sb("out_sb", [TT, PAIRS, D])

        raw = ExitStack()
        rq, rk, rv, ro = (sb(f"raw_{n}", [DH, H, D], FP32, raw) for n in "qkvo")
        r_up_a, r_up_b = (sb(f"raw_up{n}", [p, E + 1, 2, INTER], FP32, raw) for n, p in (("a", DA), ("b", DB)))
        r_down = sb("raw_down", [INTER, E + 1, D], FP32, raw)
        raw.close()
        z_a = [sb(f"z_a{n}", [DA, GB, H, NP], F32R) for n in range(2)]
        z_b = sb("z_b", [2 * DB, GB, H, NP], F32R)
        c_a = [sb(f"c_a{n}", [DA, H, 2, NP], F32R) for n in range(2)]
        c_b = [sb(f"c_b{n}", [2 * DB, HP, 2, NP], F32R) for n in range(2)]
        hid = [sb(f"hid{n}", [INTER, E + 1, GT], F32R) for n in range(2)]
        rel_raw = tanh_sb[0:2 * NP - 1, :, :].rearrange("p b d -> p (b d)").rearrange("p (h e) -> p h e", h=H)
        rel_sum, rel_sumT = sb("rel_sum", [2 * NP - 1, H]), sb("rel_sumT", [H, 2 * NP])
        bias_raw = sb("bias_raw", [NP, H, NP])
        gw_raw_a, gw_raw_b = sb("gw_raw_a", [DA, E]), sb("gw_raw_b", [DB, E])

        bank = {n: ctx.enter_context(nc.psum_tensor(f"bank_{n}", [128, 512], FP32))
                for n in ("logit", "probT", "ca", "cb", "up", "gate_up", "s0", "s1")}

        d_tok, d_small, d_qk, d_vo, d_up, d_down, d_rel, d_bias = (
            sem(n) for n in ("d_tok", "d_small", "d_qk", "d_vo", "d_up", "d_down", "d_rel", "d_bias"))
        p_fill, p_const, p_mm, p_hi, p_lo, p_rel, p_relT, p_relc, d_relw = (
            sem(n) for n in ("p_fill", "p_const", "p_mm", "p_hi", "p_lo", "p_rel", "p_relT", "p_relc", "d_relw"))

        x_loaded = signal("x_loaded", 48)
        a_mm, a_tanh = signal("a_mm", 2), signal("a_tanh", 2)
        av, sc_raw, sc, scT = signal("av", 1), signal("sc_raw", 1), signal("sc", 1), signal("scT", 1)
        nm, nmd, band_mm, band_in, band_e = (signal(n, 1) for n in ("nm", "nmd", "band_mm", "band_in", "band_e"))
        mix_mm, mix_sb, rden, p_mm2, h1_ok = (signal("mix_mm", 1), signal("mix_sb", 2), signal("rden", 1),
                                              signal("proj_mm", 1), signal("h1_ok", 2))
        st1_ok, mv1_ok, ve1_ok, rs1_ok, xn1_ok = (signal("st1_ok", 2), signal("mv1_ok", 2), signal("ve1_ok", 1),
                                                  signal("rs1_ok", 1), signal("xn1_ok", 2))
        xn_hi_ok, xn_lo_ok, xc_moved, h1_kept = (signal("xn_hi_ok", 1), signal("xn_lo_ok", 1), signal("xc_moved", 96),
                                                 signal("h1_kept", 1))
        x1_mm, x1_hi, x1_lo = signal("x1_mm", 1), signal("x1_hi", 3), signal("x1_lo", 2)
        z_mm, z_hi, z_lo = signal("z_mm", 6), signal("z_hi", 8), signal("z_lo", 8)
        l_mm, mx_ok, sub_ok, exp_ok, sum_ok, rec_ok, pn_ok = (
            signal(n, GB) for n in ("l_mm", "mx_ok", "sub_ok", "exp_ok", "sum_ok", "rec_ok", "pn_ok"))
        pt_mm, pt_hi, pt_lo, ca_mm, ca_hi, ca_lo, cb_mm = (
            signal(n, GB) for n in ("pt_mm", "pt_hi", "pt_lo", "ca_mm", "ca_hi", "ca_lo", "cb_mm"))
        cb_hi, cb_lo = signal("cb_hi", 2 * GB), signal("cb_lo", 2 * GB)
        o_mm, h2_ok, st2_ok, mv2_ok, ve2_ok, rs2_ok, xn2_ok, h2_kept = (
            signal("o_mm", 2), signal("h2_ok", 2), signal("st2_ok", 2), signal("mv2_ok", 2), signal("ve2_ok", 1),
            signal("rs2_ok", 1), signal("xn2_ok", 2), signal("h2_kept", 1))
        x2_mm, x2_hi, x2_lo = signal("x2_mm", 1), signal("x2_hi", 3), signal("x2_lo", 2)
        g_mm, g_th = signal("g_mm", 1), signal("g_th", 1)
        GATE_STEPS = 21
        g_step = signal("g_step", GATE_STEPS)
        cwt_mm, cwt_hi, cwt_lo = signal("cwt_mm", 1), signal("cwt_hi", 1), signal("cwt_lo", 1)
        cw_mm, w_ok = signal("cw_mm", HP), signal("w_ok", HP)
        up_mm, tanh_ok, u_ok, v_ok, hid_hi, hid_lo = (
            signal(n, HP + 1) for n in ("up_mm", "tanh_ok", "u_ok", "v_ok", "hid_hi", "hid_lo"))
        y_mm, out_ok, out_sent = signal("y_mm", 2), signal("out_ok", 2), signal("out_sent", 16)

        def unit(u):
            return (1, slice(E, E + 1)) if u == 0 else (2, slice(2 * u - 2, 2 * u))

        class Section:

            def __init__(self, i, key):
                self.i, self.key = i, key
                self.t, self.a, self.f, self.y = key < NG - 1, 0 <= key < NG, 1 <= key <= NG, key >= 2
                self.tg, self.ag, self.fg, self.yg = i + 1, i, i - 1, i - 2

            def has(self, stage):
                return {"t": self.t, "a": self.a, "f": self.f, "y": self.y}[stage]

            def group(self, stage):
                return {"t": self.tg, "a": self.ag, "f": self.fg, "y": self.yg}[stage]

        LOOP = 3

        def sections(eng, body):
            for i in range(-1, LOOP):
                body(Section(i, i))
            with eng.Fori(LOOP, NG - 2) as i:
                body(Section(i, LOOP))
            for i in range(NG - 2, NG + 2):
                body(Section(i, i))

        UNITS = HP + 1
        USES = {}
        for j in range(GB):
            USES["logit", j] = ("logit", "a", sub_ok, j + 1)
            USES["probT", j] = ("probT", "a", pt_lo, j + 1)
            USES["ca", j] = ("ca", "a", ca_lo, j + 1)
            USES["cb", j] = ("cb", "a", cb_lo, 2 * (j + 1))
        USES["up", 0] = ("gate_up", "f", v_ok, 1)
        for u in range(1, UNITS):
            USES["up", u] = ("logit" if u == 3 else "up", "f", u_ok, u + 1)
            USES["gate_up", u] = ("gate_up", "f", v_ok, u + 1)
        USES["o", 1] = ("probT", "a", h2_ok, 2)
        for n, (b, k) in enumerate([("logit", 1), ("ca", 2), ("probT", 4), ("cb", 5), ("gate_up", 6), ("up", 8)]):
            USES["z", n] = (b, "t", z_lo, k)
        for name, b, stage, sig, k in [
                (("score", 0), "s0", "t", a_tanh, 1), (("score", 1), "s1", "t", a_tanh, 2),
                (("y", 0), "s0", "y", out_ok, 1), (("x2", 0), "s1", "f", x2_lo, 2), (("gate", 0), "s1", "f", g_th, 1),
                (("scT", 0), "s0", "t", nm, 1), (("y", 1), "s0", "y", out_ok, 2), (("band", 0), "s1", "t", band_in, 1),
                (("o", 0), "s0", "a", h2_ok, 1), (("mix", 0), "s1", "t", rden, 1), (("cwT", 0), "s0", "f", cwt_lo, 1),
                (("cw", 0), "s0", "f", w_ok, 1), (("proj", 0), "s1", "t", h1_ok, 2), (("cw", 1), "s0", "f", w_ok, 2),
                (("x1", 0), "s1", "t", x1_lo, 2), (("cw", 2), "s0", "f", w_ok, 3),
                (("cw", 3), "s1", "f", w_ok, 4)]:
            USES[name] = (b, stage, sig, k)

        def free(pe, sec, name):
            order = [u for u in USES if USES[u][0] == USES[name][0]]
            here = [(sec, u) for u in order[:order.index(name)]]
            before = [(Section(sec.i - 1, sec.key - 1), u) for u in order] if sec.key >= 0 else []
            for where, u in reversed(before + here):
                _, stage, sig, k = USES[u]
                if where.has(stage):
                    pe.wait_ge(*sig.at(where.group(stage), k))
                    return

        def at(name):
            return bank[USES[name][0]]

        UP_CHUNKS = 3
        SMALL_LOADS = 13
        block = ctx.enter_context(nc.Block())

        @block.sync
        def _(sp):
            def load_x(g):
                sp.dma_start(xin_a[:, :], xT[0:DA, bass.ds(g * (GB * S), GB * S)]).then_inc(x_loaded.sem, 16)
                sp.dma_start(xin_b[0:DB, :], xT[DA:D, bass.ds(g * (GB * S), GB * S)]).then_inc(x_loaded.sem, 16)
                sp.dma_start(xin[:, :, :], x[bass.ds(g * GB, GB), :, :].rearrange("b s d -> s b d"))\
                    .then_inc(x_loaded.sem, 16)

            load_x(0)
            sp.dma_start(tw_a[:, :], tok_wT[0:DA, :]).then_inc(d_tok, 16)
            sp.dma_start(tw_b[0:DB, :], tok_wT[DA:D, :]).then_inc(d_tok, 16)
            sp.dma_start(tw_b[DB:DB + 2, :], tok_bias).then_inc(d_tok, 16)
            sp.dma_start(tp_a[:, :], tok_pT[0:DA, :]).then_inc(d_tok, 16)
            sp.dma_start(tp_b[:, :], tok_pT[DA:D, :]).then_inc(d_tok, 16)
            sp.dma_start(r_up_a[:, 0:E, 0, :], w1T[0:DA]).then_inc(d_up, 16)
            sp.dma_start(r_up_a[:, 0:E, 1, :], w3T[0:DA]).then_inc(d_up, 16)
            sp.dma_start(r_up_a[:, E, 0, :], sw1T[0:DA]).then_inc(d_up, 16)
            sp.dma_start(r_up_a[:, E, 1, :], sw3T[0:DA]).then_inc(d_up, 16)
            sp.dma_start(r_up_b[:, 0:E, 0, :], w1T[DA:D]).then_inc(d_up, 16)
            sp.dma_start(r_up_b[:, 0:E, 1, :], w3T[DA:D]).then_inc(d_up, 16)
            sp.dma_start(r_up_b[:, E, 0, :], sw1T[DA:D]).then_inc(d_up, 16)
            sp.dma_start(r_up_b[:, E, 1, :], sw3T[DA:D]).then_inc(d_up, 16)
            sp.wait_ge(p_relc, 1)
            sp.dma_start(scratch[:, 0:2 * NP - 1], rel_sumT[:, 0:2 * NP - 1]).then_inc(d_relw, 16)
            sp.wait_ge(d_relw, 16)
            sp.dma_start(bias_raw[:, :, :], bass.AP(scratch, 0, [[1, NP], [2 * NP, H], [1, NP]])).then_inc(d_bias, 16)

            def body(s):
                if s.y:
                    sp.wait_ge(*out_ok.at(s.yg, 2))
                    dst = out[bass.ds(s.yg * GB, GB), :, :].rearrange("(t b) p d -> (b p) t d", b=2)
                    sp.dma_start(dst, out_sb[:, :, :]).then_inc(out_sent.sem, 16)
                if s.t and s.key < NG - 2:
                    sp.wait_ge(*mix_mm.at(s.tg, 1))
                    load_x(s.tg + 1)
                if s.t:
                    sp.wait_ge(*xn_hi_ok.at(s.tg, 1))
                    sp.wait_ge(*xn_lo_ok.at(s.tg, 1))
                    if s.a:
                        sp.wait_ge(*cb_mm.at(s.ag, GB))
                    else:
                        sp.wait_ge(p_fill, 6)
                    for par in range(2):
                        src = slice(par * NP, (par + 1) * NP)
                        for dst, n in ((xc_hi[0:NP], 0), (xc_hi[LO:KS], 0), (xc_lo[:, :, :], 1)):
                            sp.dma_start(dst[:, par::2, :].bitcast(FP32), xn_half[n][src, :, :].bitcast(FP32))\
                                .then_inc(xc_moved.sem, 16)

            sections(sp, body)
            sp.wait_ge(out_sent.sem, 16 * NG)

        @block.tensor
        def _(pe):
            mm = nc.tensor.matmul

            pe.wait_ge(p_rel, 1)
            pe.wait_ge(d_small, 16 * SMALL_LOADS)
            nc.tensor.transpose(bank["s0"][0:H, 0:2 * NP - 1], rel_sum[:, :], ident[0:2 * NP - 1, 0:2 * NP - 1])\
                .then_inc(p_relT, 1)
            order = ["logit", "probT", "ca", "cb", "up", "gate_up"]
            n = 0
            for k, (left, right, loaded) in enumerate(((rk, rq, d_qk), (rv, ro, d_vo))):
                pe.wait_ge(loaded, 32)
                for hp in range(HP):
                    for c0, cn in ((0, DA), (DA, DB)):
                        dst = bank[order[n % 6]]
                        if n >= 6:
                            pe.wait_ge(p_lo, n - 5)
                        for par in range(2):
                            last = mm(dst[0:cn, par * D:(par + 1) * D], left[:, 2 * hp + par, c0:c0 + cn],
                                      right[:, 2 * hp + par, :], start=True, stop=True)
                        last.then_inc(p_mm, 1)
                        n += 1

            def hidden(ex, n, kind, dst):
                for e in range(n):
                    o = dst[:, e * GT:(e + 1) * GT]
                    wa, wl, wb = (w[:, ex + e, kind, :] for w in (up_a[0], up_a[1], up_b))
                    mm(o, wa, x2_a[0][:, :], start=True, stop=False)
                    mm(o, wa, x2_a[1][:, :], start=False, stop=False)
                    mm(o, wl, x2_a[0][:, :], start=False, stop=False)
                    mm(o, wb, x2_b2[:, :], start=False, stop=False)
                    last = mm(o, wb[0:DB], x2_blo[:, :], start=False, stop=True)
                return last

            def out_proj(s, t):
                free(pe, s, ("o", t))
                g = s.ag
                pe.wait_ge(*ca_lo.at(g, 2 * t + 2))
                pe.wait_ge(*cb_lo.at(g, 4 * t + 4))
                o = at(("o", t))[0:TT, 0:D]
                for hh in range(H):
                    ch, cl = (c[:, hh, :, :].rearrange("p b q -> p (b q)") for c in c_a)
                    mm(o, ch, vo_a[0][:, hh, :], start=hh == 0, stop=False)
                    mm(o, ch, vo_a[1][:, hh, :], start=False, stop=False)
                    mm(o, cl, vo_a[0][:, hh, :], start=False, stop=False)
                for hp in range(HP):
                    ch, cl = (c[:, hp, :, :].rearrange("p b q -> p (b q)") for c in c_b)
                    mm(o, ch, vo_b[0][:, hp, :], start=False, stop=False)
                    mm(o, ch, vo_b[1][:, hp, :], start=False, stop=False)
                    last = mm(o, cl, vo_b[0][:, hp, :], start=False, stop=hp == HP - 1)
                last.then_inc(o_mm.sem, 1)

            def logits(s, j):
                free(pe, s, ("logit", j))
                if j == 0:
                    pe.wait_ge(*z_lo.at(s.ag, 8))
                q = slice(j * NP, (j + 1) * NP)
                o = bank["logit"][0:NP, 0:H * NP]
                mm(o, flip[:, :], bias[:, :, :].rearrange("p h k -> p (h k)"), start=True, stop=False)
                zh, zl, zb = (z[:, j, :, :].rearrange("p h k -> p (h k)") for z in (z_a[0], z_a[1], z_b))
                mm(o, x1_a[0][:, q], zh, start=False, stop=False)
                mm(o, x1_a[0][:, q], zl, start=False, stop=False)
                mm(o, x1_a[1][:, q], zh, start=False, stop=False)
                mm(o, x1_b2[:, q], zb, start=False, stop=False)
                mm(o, x1_blo[:, q], zb[0:DB], start=False, stop=True).then_inc(l_mm.sem, 1)

            def prob_transpose(s, j):
                free(pe, s, ("probT", j))
                pe.wait_ge(*pn_ok.at(s.ag, j + 1))
                mm(bank["probT"][0:NP, 0:2], flip[:, :], ident_r[:, 0:2], start=True, stop=True)
                for hh in range(H):
                    last = nc.tensor.transpose(bank["probT"][0:NP, hh * NP:(hh + 1) * NP], prob[j % 2][:, hh, :],
                                               ident[0:NP, 0:NP])
                last.then_inc(pt_mm.sem, 1)

            def context(s, j):
                if j == 0:
                    pe.wait_ge(*xc_moved.at(s.ag, 96))
                pe.wait_ge(*pt_lo.at(s.ag, j + 1))
                for name, sig, c0, cn in (("ca", ca_mm, 0, DA), ("cb", cb_mm, DA, DB)):
                    free(pe, s, (name, j))
                    o = bank[name][0:cn, 0:H * NP]
                    mm(o, xc_hi[:, j, c0:c0 + cn], probT[:, :], start=True, stop=False)
                    mm(o, xc_lo[:, j, c0:c0 + cn], probT[0:NP, :], start=False, stop=True).then_inc(sig.sem, 1)

            def token_scores(s, m):
                free(pe, s, ("score", m))
                if m == 0:
                    pe.wait_ge(*x_loaded.at(s.tg, 48))
                    if s.key < 0:
                        pe.wait_ge(d_tok, 80)
                        pe.wait_ge(p_fill, 6)
                for e in range(2):
                    o = at(("score", m))[0:S, e * D:(e + 1) * D]
                    p = slice((2 * m + e) * S, (2 * m + e + 1) * S)
                    mm(o, xin_a[:, p], tw_a[:, :], start=True, stop=False)
                    last = mm(o, xin_b[:, p], tw_b[:, :], start=False, stop=True)
                last.then_inc(a_mm.sem, 1)

            def experts(s, u, kind):
                if u == 0:
                    if kind == 0:
                        pe.wait_ge(*x2_lo.at(s.fg, 2))
                        free(pe, s, ("up", 0))
                    last = hidden(E, 1, kind, at(("up", 0))[:, kind * GT:(kind + 1) * GT])
                else:
                    name = (("up", u), ("gate_up", u))[kind]
                    free(pe, s, name)
                    last = hidden(2 * u - 2, 2, kind, at(name))
                if kind:
                    last.then_inc(up_mm.sem, 1)

            def spread_weights(s, j):
                free(pe, s, ("cw", j))
                b = at(("cw", j))
                if j == 0:
                    pe.wait_ge(*cwt_lo.at(s.fg, 1))
                for e in range(2):
                    last = mm(b[:, e * GT:(e + 1) * GT], pick[:, 2 * j + e, :], cwT[:, :], start=True, stop=True)
                last.then_inc(cw_mm.sem, 1)

            def down_proj(s, t):
                free(pe, s, ("y", t))
                if t == 0:
                    pe.wait_ge(*hid_lo.at(s.yg, UNITS - 1))
                o = at(("y", t))[0:TT, 0:D]
                q = slice(t * TT, (t + 1) * TT)
                order = [E, *range(E)]
                for n, e in enumerate(order):
                    if t == 0 and n == E - 1:
                        pe.wait_ge(*hid_lo.at(s.yg, UNITS))
                    mm(o, hid[0][:, e, q], down[0][:, e, :], start=n == 0, stop=False)
                    mm(o, hid[0][:, e, q], down[1][:, e, :], start=False, stop=False)
                    last = mm(o, hid[1][:, e, q], down[0][:, e, :], start=False, stop=n == E)
                last.then_inc(y_mm.sem, 1)

            def x_transpose(s, name, src, sig, g, ready):
                free(pe, s, (name, 0))
                pe.wait_ge(*ready.at(g, 2))
                o = at((name, 0))
                for t in range(PAIRS):
                    nc.tensor.transpose(o[0:DA, t * TT:(t + 1) * TT], src[:, t, 0:DA], ident[0:TT, 0:TT])
                for t in range(PAIRS):
                    last = nc.tensor.transpose(o[0:DB, GT + t * TT:GT + (t + 1) * TT], src[:, t, DA:D],
                                               ident[0:TT, 0:TT])
                last.then_inc(sig.sem, 1)

            def z_tiles(s, n):
                if n == 0:
                    pe.wait_ge(*x1_lo.at(s.tg, 2))
                    if s.key < 0:
                        pe.wait_ge(p_lo, 27)
                free(pe, s, ("z", n))
                dst = at(("z", n))
                half, kind = n // 3, n % 3
                for e in range(2):
                    hp, tile = (2 * half + kind, e) if kind < 2 else (2 * half + e, 2)
                    w = [q[:, hp, tile, :] for q in (qk_a[0], qk_a[1], qk_b)]
                    o = dst[:, e * GT:(e + 1) * GT]
                    mm(o, w[0], x1_a[0][:, :], start=True, stop=False)
                    mm(o, w[0], x1_a[1][:, :], start=False, stop=False)
                    mm(o, w[1], x1_a[0][:, :], start=False, stop=False)
                    mm(o, w[2], x1_b2[:, :], start=False, stop=False)
                    last = mm(o, w[2][0:DB], x1_blo[:, :], start=False, stop=True)
                last.then_inc(z_mm.sem, 1)

            def weights_transpose(s):
                free(pe, s, ("cwT", 0))
                pe.wait_ge(*g_step.at(s.fg, GATE_STEPS))
                for t in range(PAIRS):
                    last = nc.tensor.transpose(at(("cwT", 0))[0:E, t * TT:(t + 1) * TT], g_cw[:, t, :], ident[0:TT, 0:TT])
                last.then_inc(cwt_mm.sem, 1)

            def score_transpose(s):
                free(pe, s, ("scT", 0))
                pe.wait_ge(*sc.at(s.tg, 1))
                nc.tensor.transpose(at(("scT", 0))[0:GB, 0:S], score[:, :], ident[0:S, 0:S]).then_inc(scT.sem, 1)

            def spread_maxima(s):
                free(pe, s, ("band", 0))
                pe.wait_ge(*nmd.at(s.tg, 1))
                o = at(("band", 0))[0:S, 0:GT]
                mm(o, ident_r[:, :], band_mask[:, :], start=True, stop=False)
                mm(o, ones[0:GB, 0:S], max_diag[:, :, :].rearrange("p b q -> p (b q)"), start=False, stop=True)\
                    .then_inc(band_mm.sem, 1)

            def mix_windows(s):
                free(pe, s, ("mix", 0))
                pe.wait_ge(*band_e.at(s.tg, 1))
                for c0, cn, o0 in ((0, DA, 0), (DA, DB, GT)):
                    for b in range(GB):
                        mm(at(("mix", 0))[0:cn, o0 + b * NP:o0 + (b + 1) * NP], xin[:, b, c0:c0 + cn], band[:, b, :],
                           start=True, stop=True)
                for t in range(PAIRS):
                    last = mm(at(("mix", 0))[0:TT, 2 * GT + t:2 * GT + t + 1],
                              band[:, 2 * t:2 * t + 2, :].rearrange("p b q -> p (b q)"), ones[0:S, 0:1],
                              start=True, stop=True)
                last.then_inc(mix_mm.sem, 1)

            def token_proj(s):
                free(pe, s, ("proj", 0))
                pe.wait_ge(*mix_sb.at(s.tg, 2))
                for t in range(PAIRS):
                    o, q = at(("proj", 0))[0:TT, t * D:(t + 1) * D], slice(t * TT, (t + 1) * TT)
                    mm(o, mix_a[:, q], tp_a[:, :], start=True, stop=False)
                    last = mm(o, mix_b[:, q], tp_b[:, :], start=False, stop=True)
                last.then_inc(p_mm2.sem, 1)

            def gate_logits(s):
                free(pe, s, ("gate", 0))
                pe.wait_ge(*x2_lo.at(s.fg, 2))
                for t in range(PAIRS):
                    q = slice(t * TT, (t + 1) * TT)
                    last = split_product(nc.tensor, at(("gate", 0))[0:TT, t * E:(t + 1) * E], x2_a[0][:, q],
                                         x2_a[1][:, q], x2_b2[:, q], x2_blo[:, q], gw_a[0][:, :], gw_a[1][:, :],
                                         gw_b[:, :])
                last.then_inc(g_mm.sem, 1)

            def body(s):
                if s.t:
                    token_scores(s, 0)
                if s.a:
                    logits(s, 0)
                if s.t:
                    token_scores(s, 1)
                if s.f:
                    x_transpose(s, "x2", xn2, x2_mm, s.fg, xn2_ok)
                if s.y:
                    down_proj(s, 0)
                if s.a:
                    prob_transpose(s, 0)
                    logits(s, 1)
                if s.f:
                    gate_logits(s)
                if s.a:
                    context(s, 0)
                if s.f:
                    experts(s, 0, 0)
                    experts(s, 0, 1)
                    experts(s, 1, 0)
                if s.t:
                    score_transpose(s)
                if s.a:
                    prob_transpose(s, 1)
                    logits(s, 2)
                if s.f:
                    experts(s, 1, 1)
                if s.a:
                    context(s, 1)
                if s.y:
                    down_proj(s, 1)
                if s.t:
                    spread_maxima(s)
                if s.a:
                    prob_transpose(s, 2)
                    out_proj(s, 0)
                    logits(s, 3)
                if s.t:
                    mix_windows(s)
                if s.f:
                    weights_transpose(s)
                if s.a:
                    context(s, 2)
                if s.t:
                    token_proj(s)
                if s.f:
                    experts(s, 2, 0)
                    experts(s, 2, 1)
                if s.a:
                    prob_transpose(s, 3)
                if s.f:
                    spread_weights(s, 0)
                if s.a:
                    context(s, 3)
                if s.f:
                    experts(s, 3, 0)
                    experts(s, 3, 1)
                    spread_weights(s, 1)
                if s.t:
                    x_transpose(s, "x1", xn1, x1_mm, s.tg, xn1_ok)
                if s.a:
                    out_proj(s, 1)
                if s.f:
                    spread_weights(s, 2)
                if s.t:
                    z_tiles(s, 0)
                    z_tiles(s, 1)
                if s.f:
                    experts(s, 4, 0)
                    experts(s, 4, 1)
                    spread_weights(s, 3)
                if s.t:
                    for n in range(2, 6):
                        z_tiles(s, n)

            sections(pe, body)

        @block.scalar
        def _(ac):
            def copy(out_, in_, scale=1.0):
                return nc.scalar.activation(out_, in_, ACT.Copy, scale=scale)

            ac.dma_start(rk[:, :, :], wkT).then_inc(d_qk, 16)
            ac.dma_start(rq[:, :, :], wqT).then_inc(d_qk, 16)
            ac.dma_start(rv[:, :, :], wvT).then_inc(d_vo, 16)
            ac.dma_start(ro[:, :, :], wo).then_inc(d_vo, 16)
            ac.dma_start(r_down[:, 0:E, :], w2T).then_inc(d_down, 16)
            ac.dma_start(r_down[:, E, :], sw2T).then_inc(d_down, 16)
            ac.wait_ge(p_relT, 1)
            copy(rel_sumT[:, 0:2 * NP - 1], bank["s0"][0:H, 0:2 * NP - 1]).then_inc(p_relc, 1)
            order = ["logit", "probT", "ca", "cb", "up", "gate_up"]
            n = 0
            for k in range(2):
                for hp in range(HP):
                    for c0, cn in ((0, DA), (DA, DB)):
                        src = bank[order[n % 6]][0:cn, 0:2 * D].rearrange("p (h e) -> p h e", h=2)
                        ac.wait_ge(p_mm, n + 1)
                        hs = slice(2 * hp, 2 * hp + 2)
                        if k == 0:
                            dst = (qk_a[0][:, hp] if c0 == 0 else qk_b[0:DB, hp])
                            copy(dst[:, 0:2, :], src[:, :, 0:DA], DH ** -0.5)
                            copy(dst[:, 2, :].rearrange("p (h e) -> p h e", h=2), src[:, :, DA:D], DH ** -0.5)\
                                .then_inc(p_hi, 1)
                        elif c0 == 0:
                            copy(vo_a[0][:, hs, :], src).then_inc(p_hi, 1)
                        else:
                            copy(vo_b[0][0:DB, hp, :], src[:, 0, :])
                            copy(vo_b[0][DB:2 * DB, hp, :], src[:, 1, :]).then_inc(p_hi, 1)
                        n += 1
            ac.wait_ge(d_small, 16 * SMALL_LOADS)
            copy(gw_a[0][:, :], gw_raw_a[:, :])
            copy(gw_b[0:DB, :], gw_raw_b[:, :]).then_inc(p_hi, 1)
            ac.wait_ge(d_up, 128)
            for c in range(UP_CHUNKS):
                es = slice(3 * c, 3 * c + 3)
                copy(up_a[0][:, es], r_up_a[:, es]).then_inc(p_hi, 1)
                copy(up_b[0:DB, es], r_up_b[:, es]).then_inc(p_hi, 1)
            ac.wait_ge(d_down, 32)
            for c in range(UP_CHUNKS):
                es = slice(3 * c, 3 * c + 3)
                copy(down[0][:, es], r_down[:, es]).then_inc(p_hi, 1)
            ac.wait_ge(d_bias, 16)
            copy(bias[0:NP, :, :], bias_raw[:, :, :]).then_inc(p_hi, 1)

            def prob_hi(s, j):
                ac.wait_ge(*pt_mm.at(s.ag, j + 1))
                if j:
                    ac.wait_ge(*cb_mm.at(s.ag, j))
                elif s.key > 0:
                    ac.wait_ge(*cb_mm.at(s.ag - 1, GB))
                else:
                    ac.wait_ge(p_fill, 6)
                copy(probT[0:NP, :], bank["probT"][0:NP, 0:H * NP]).then_inc(pt_hi.sem, 1)

            def context_hi(s, j):
                pb = j % 2
                if pb == 0:
                    if j == 2:
                        ac.wait_ge(*o_mm.at(s.ag, j // 2))
                    elif s.key > 0:
                        ac.wait_ge(*o_mm.at(s.ag - 1, 2))
                ac.wait_ge(*ca_mm.at(s.ag, j + 1))
                copy(c_a[0][:, :, pb, :], bank["ca"][:, 0:H * NP].rearrange("p (h q) -> p h q", h=H))\
                    .then_inc(ca_hi.sem, 1)
                ac.wait_ge(*cb_mm.at(s.ag, j + 1))
                src = bank["cb"][0:DB, 0:H * NP].rearrange("p (h two q) -> p h two q", h=HP, two=2)
                for par in range(2):
                    copy(c_b[0][par * DB:(par + 1) * DB, :, pb, :], src[:, :, par, :]).then_inc(cb_hi.sem, 1)

            def hidden_hi(s, j):
                if j:
                    ac.wait_ge(*w_ok.at(s.fg, j))
                else:
                    ac.wait_ge(*v_ok.at(s.fg, 1))
                n, es = unit(j)
                copy(hid[0][:, es, :], act[j % 2][:, 0:n, :]).then_inc(hid_hi.sem, 1)

            def gate_tanh(s, j):
                n = unit(j)[0]
                ac.wait_ge(*up_mm.at(s.fg, j + 1))
                if j >= 2:
                    ac.wait_ge(*hid_lo.at(s.fg, j - 1))
                elif s.key > 1:
                    ac.wait_ge(*hid_lo.at(s.fg - 1, UNITS - j))
                nc.scalar.activation(act[j % 2][:, 0:n, :], at(("up", j))[:, 0:n * GT].rearrange("p (e t) -> p e t", e=n),
                                     ACT.Tanh, scale=0.5).then_inc(tanh_ok.sem, 1)

            def score_tanh(s, m):
                ac.wait_ge(*a_mm.at(s.tg, m + 1))
                if s.key < 0:
                    ac.wait_ge(p_rel, 1)
                elif m == 0:
                    ac.wait_ge(*sc_raw.at(s.tg - 1, 1))
                nc.scalar.activation(tanh_sb[:, 2 * m:2 * m + 2, :],
                                     at(("score", m))[0:S, 0:2 * D].rearrange("p (e d) -> p e d", e=2),
                                     ACT.Tanh)\
                    .then_inc(a_tanh.sem, 1)

            def x_hi(b, sig_mm, sig, g, xa, xb2):
                ac.wait_ge(*sig_mm.at(g, 1))
                copy(xa[0][:, :], b[:, 0:GT]).then_inc(sig.sem, 1)
                copy(xb2[0:DB, :], b[0:DB, GT:2 * GT]).then_inc(sig.sem, 1)
                copy(xb2[DB:2 * DB, :], b[0:DB, GT:2 * GT]).then_inc(sig.sem, 1)

            def z_high(s, n):
                half, kind = n // 3, n % 3
                ac.wait_ge(*z_mm.at(s.tg, n + 1))
                src = at(("z", n))
                if kind < 2:
                    h0 = 4 * half + 2 * kind
                    copy(z_a[0][:, :, h0:h0 + 2, :].rearrange("p b h k -> p h b k"),
                         src[:, 0:2 * GT].rearrange("p (h b k) -> p h b k", h=2, b=GB)).then_inc(z_hi.sem, 1)
                else:
                    for par in range(2):
                        copy(z_b[0:DB, :, 4 * half + par:4 * half + 4:2, :].rearrange("p b h k -> p h b k"),
                             src[par * DB:(par + 1) * DB, 0:2 * GT].rearrange("p (h b k) -> p h b k", h=2, b=GB))\
                            .then_inc(z_hi.sem, 1)

            def prob_exp(s, j):
                ac.wait_ge(*sub_ok.at(s.ag, j + 1))
                nc.scalar.activation(prob[j % 2][:, :, :], prob[j % 2][:, :, :], ACT.Exp).then_inc(exp_ok.sem, 1)

            def norm_halves(s):
                ac.wait_ge(*xn1_ok.at(s.tg, 2))
                if s.key >= 0:
                    ac.wait_ge(*xc_moved.at(s.tg - 1, 96))
                copy(xn_half[0][:, :, :], xn1[:, :, :]).then_inc(xn_hi_ok.sem, 1)

            def body(s):
                if s.t:
                    score_tanh(s, 0)
                if s.a:
                    prob_exp(s, 0)
                if s.t:
                    score_tanh(s, 1)
                if s.a:
                    if s.f:
                        ac.wait_ge(*h2_ok.at(s.fg, 2))
                    ac.wait_ge(*h1_ok.at(s.ag, 2))
                    copy(h1_res[:, :, :], h1[:, :, :]).then_inc(h1_kept.sem, 1)
                if s.f:
                    x_hi(at(("x2", 0)), x2_mm, x2_hi, s.fg, x2_a, x2_b2)
                if s.a:
                    prob_hi(s, 0)
                    prob_exp(s, 1)
                    context_hi(s, 0)
                if s.f:
                    ac.wait_ge(*g_mm.at(s.fg, 1))
                    if s.key > 1:
                        ac.wait_ge(*g_step.at(s.fg - 1, 1))
                    nc.scalar.activation(g_tanh[:, :], at(("gate", 0))[0:TT, 0:PAIRS * E], ACT.Tanh, scale=0.5)\
                        .then_inc(g_th.sem, 1)
                    gate_tanh(s, 0)
                if s.a:
                    prob_hi(s, 1)
                    prob_exp(s, 2)
                if s.f:
                    gate_tanh(s, 1)
                if s.a:
                    context_hi(s, 1)
                if s.f:
                    if s.y:
                        ac.wait_ge(*y_mm.at(s.yg, 2))
                    hidden_hi(s, 0)
                    if s.y:
                        ac.wait_ge(*out_ok.at(s.yg, 2))
                    else:
                        ac.wait_ge(*h2_ok.at(s.fg, 2))
                    copy(h2_res[:, :, :], h2[:, :, :]).then_inc(h2_kept.sem, 1)
                if s.a:
                    prob_hi(s, 2)
                if s.t:
                    ac.wait_ge(*band_in.at(s.tg, 1))
                    nc.scalar.activation(band[:, :, :], band[:, :, :], ACT.Exp).then_inc(band_e.sem, 1)
                if s.t:
                    ac.wait_ge(*mix_mm.at(s.tg, 1))
                    if s.key >= 0:
                        ac.wait_ge(*p_mm2.at(s.tg - 1, 1))
                    copy(mix_a[:, :], at(("mix", 0))[:, 0:GT]).then_inc(mix_sb.sem, 1)
                    copy(mix_b[:, :], at(("mix", 0))[0:DB, GT:2 * GT]).then_inc(mix_sb.sem, 1)
                if s.a:
                    prob_exp(s, 3)
                    context_hi(s, 2)
                if s.f:
                    ac.wait_ge(*cwt_mm.at(s.fg, 1))
                    if s.key > 1:
                        ac.wait_ge(*cw_mm.at(s.fg - 1, HP))
                    else:
                        ac.wait_ge(p_fill, 6)
                    copy(cwT[0:E, :], at(("cwT", 0))[0:E, 0:GT]).then_inc(cwt_hi.sem, 1)
                if s.a:
                    prob_hi(s, 3)
                if s.f:
                    gate_tanh(s, 2)
                    hidden_hi(s, 1)
                if s.a:
                    context_hi(s, 3)
                if s.f:
                    gate_tanh(s, 3)
                    hidden_hi(s, 2)
                if s.t:
                    x_hi(at(("x1", 0)), x1_mm, x1_hi, s.tg, x1_a, x1_b2)
                    norm_halves(s)
                    if s.key < 0:
                        ac.wait_ge(p_lo, 27)
                    z_high(s, 0)
                if s.f:
                    hidden_hi(s, 3)
                if s.t:
                    z_high(s, 1)
                if s.f:
                    gate_tanh(s, 4)
                if s.t:
                    for n in range(2, 6):
                        z_high(s, n)
                if s.f:
                    hidden_hi(s, 4)

            sections(ac, body)

        @block.vector
        def _(ve):
            v = nc.vector

            def low(out_, src, hi):
                return v.tensor_tensor(out_, src, hi.bitcast(FP32), ALU.subtract)

            v.memset(ones[:, :], 1.0).then_inc(p_fill, 1)
            v.memset(minus_half[:, :], -0.5).then_inc(p_fill, 1)
            v.memset(xin_b[DB:DB + 2, :], 1.0).then_inc(p_fill, 1)
            v.memset(probT[32:LO, :].bitcast(FP32), 0.0).then_inc(p_fill, 1)
            v.memset(xc_hi[32:LO, :, :].bitcast(FP32), 0.0)
            v.memset(bias[32:LO, :, :].bitcast(FP32), 0.0).then_inc(p_fill, 1)
            v.memset(cwT[:, :].bitcast(FP32), 0.0).then_inc(p_fill, 1)
            ve.wait_ge(d_rel, 16)
            v.tensor_reduce(rel_sum[:, :], rel_raw, axis=AX, op=ALU.add).then_inc(p_rel, 1)
            ve.wait_ge(d_small, 16 * SMALL_LOADS)
            v.tensor_copy(ident_r[:, :], ident[0:S, 0:S])
            v.tensor_copy(band_mask[:, :], band_raw[:, :])
            v.tensor_copy(flip[:, :], flip_raw[:, :])
            v.tensor_copy(pick[:, :, :], pick_raw[:, :, :]).then_inc(p_const, 1)
            order = ["logit", "probT", "ca", "cb", "up", "gate_up"]
            n = 0
            for k in range(2):
                for hp in range(HP):
                    for c0, cn in ((0, DA), (DA, DB)):
                        src = bank[order[n % 6]][0:cn, 0:2 * D].rearrange("p (h e) -> p h e", h=2)
                        ve.wait_ge(p_hi, n + 1)
                        hs = slice(2 * hp, 2 * hp + 2)
                        if k == 0:
                            hi, lo = ((qk_a[0][:, hp], qk_a[1][:, hp]) if c0 == 0 else
                                      (qk_b[0:DB, hp], qk_b[DB:2 * DB, hp]))
                            for o_, i_, h_ in ((lo[:, 0:2, :], src[:, :, 0:DA], hi[:, 0:2, :]),
                                               (lo[:, 2, :].rearrange("p (h e) -> p h e", h=2), src[:, :, DA:D],
                                                hi[:, 2, :].rearrange("p (h e) -> p h e", h=2))):
                                last = v.scalar_tensor_tensor(out=o_, in0=i_, scalar=DH ** -0.5, in1=h_.bitcast(FP32),
                                                              op0=ALU.mult, op1=ALU.subtract)
                            last.then_inc(p_lo, 1)
                        elif c0 == 0:
                            low(vo_a[1][:, hs, :], src, vo_a[0][:, hs, :]).then_inc(p_lo, 1)
                        else:
                            low(vo_b[1][0:DB, hp, :], src[:, 0, :], vo_b[0][0:DB, hp, :])
                            low(vo_b[1][DB:2 * DB, hp, :], src[:, 1, :], vo_b[0][DB:2 * DB, hp, :]).then_inc(p_lo, 1)
                        n += 1
            ve.wait_ge(p_hi, 17)
            low(gw_a[1][:, :], gw_raw_a[:, :], gw_a[0][:, :])
            low(gw_b[DB:2 * DB, :], gw_raw_b[:, :], gw_b[0:DB, :]).then_inc(p_lo, 1)
            for c in range(UP_CHUNKS):
                es = slice(3 * c, 3 * c + 3)
                ve.wait_ge(p_hi, 18 + 2 * c)
                low(up_a[1][:, es], r_up_a[:, es], up_a[0][:, es]).then_inc(p_lo, 1)
                ve.wait_ge(p_hi, 19 + 2 * c)
                low(up_b[DB:2 * DB, es], r_up_b[:, es], up_b[0:DB, es]).then_inc(p_lo, 1)
            for c in range(UP_CHUNKS):
                es = slice(3 * c, 3 * c + 3)
                ve.wait_ge(p_hi, 24 + c)
                low(down[1][:, es], r_down[:, es], down[0][:, es]).then_inc(p_lo, 1)
            ve.wait_ge(p_hi, 27)
            ve.wait_ge(p_fill, 6)
            low(bias[LO:KS, :, :], bias_raw[:, :, :], bias[0:NP, :, :]).then_inc(p_lo, 1)

            def norm_stats(s, g, t, src, st, mv, src_ok, st_ok, mv_ok):
                ve.wait_ge(*src_ok.at(g, t + 1))
                v.bn_stats(st[:, t, :], src[:, t, :]).then_inc(st_ok.sem, 1)
                ve.wait_ge(*st_ok.at(g, t + 1))
                v.memset(wait_cell[:, :], 0.0)
                v.bn_aggr(mv[:, t, :], st[:, t, :]).then_inc(mv_ok.sem, 1)

            def norm_eps(s, g, mv, veps, mv_ok, ve_ok):
                ve.wait_ge(*mv_ok.at(g, 2))
                v.tensor_scalar(veps[:, :], mv[:, :, 1], LN_EPS, None, ALU.add).then_inc(ve_ok.sem, 1)

            def norm_apply(s, g, src, mv, rs, dst, rs_ok, ok):
                ve.wait_ge(*rs_ok.at(g, 1))
                for t in range(PAIRS):
                    v.tensor_scalar(dst[:, t, :], src[:, t, :], mv[:, t, 0:1], rs[:, t:t + 1], ALU.subtract, ALU.mult)\
                        .then_inc(ok.sem, 1)

            def prob_lo(s, j):
                ve.wait_ge(*pt_hi.at(s.ag, j + 1))
                low(probT[LO:KS, :], bank["probT"][0:NP, 0:H * NP], probT[0:NP, :]).then_inc(pt_lo.sem, 1)

            def context_lo(s, j):
                pb = j % 2
                ve.wait_ge(*ca_hi.at(s.ag, j + 1))
                low(c_a[1][:, :, pb, :], bank["ca"][:, 0:H * NP].rearrange("p (h q) -> p h q", h=H),
                    c_a[0][:, :, pb, :]).then_inc(ca_lo.sem, 1)
                ve.wait_ge(*cb_hi.at(s.ag, 2 * j + 2))
                src = bank["cb"][0:DB, 0:H * NP].rearrange("p (h two q) -> p h two q", h=HP, two=2)
                for par in range(2):
                    p = slice(par * DB, (par + 1) * DB)
                    low(c_b[1][p, :, pb, :], src[:, :, par, :], c_b[0][p, :, pb, :]).then_inc(cb_lo.sem, 1)

            def gate_product(s, j):
                n = unit(j)[0]
                a = act[j % 2][:, 0:n, :].rearrange("p e t -> p (e t)")
                ve.wait_ge(*tanh_ok.at(s.fg, j + 1))
                v.scalar_tensor_tensor(out=a, in0=a, scalar=1.0, in1=at(("up", j))[:, 0:n * GT], op0=ALU.add,
                                       op1=ALU.mult).then_inc(u_ok.sem, 1)
                ve.wait_ge(*u_ok.at(s.fg, j + 1))
                other = bank["gate_up"][:, 0:n * GT] if n == 2 else bank["gate_up"][:, GT:2 * GT]
                v.scalar_tensor_tensor(out=a, in0=a, scalar=0.5, in1=other, op0=ALU.mult, op1=ALU.mult)\
                    .then_inc(v_ok.sem, 1)

            def weigh(s, u):
                a = act[u % 2][:, :, :].rearrange("p e t -> p (e t)")
                ve.wait_ge(*v_ok.at(s.fg, u + 1))
                ve.wait_ge(*cw_mm.at(s.fg, u))
                v.tensor_tensor(a, a, at(("cw", u - 1))[:, 0:2 * GT], ALU.mult).then_inc(w_ok.sem, 1)

            def residual(s, t):
                g = s.ag
                ve.wait_ge(*o_mm.at(g, t + 1))
                if t == 0:
                    ve.wait_ge(*h1_kept.at(g, 1))
                    if s.key > 0:
                        ve.wait_ge(*h2_kept.at(g - 1, 1))
                v.tensor_tensor(h2[:, t, :], at(("o", t))[0:TT, 0:D], h1_res[:, t, :], ALU.add).then_inc(h2_ok.sem, 1)
                norm_stats(s, g, t, h2, st2, mv2, h2_ok, st2_ok, mv2_ok)

            def emit(s, t):
                ve.wait_ge(*y_mm.at(s.yg, t + 1))
                if t == 0:
                    ve.wait_ge(*h2_kept.at(s.yg, 1))
                    if s.key > 2:
                        ve.wait_ge(*out_sent.at(s.yg - 1, 16))
                v.tensor_tensor(out_sb[:, t, :], at(("y", t))[0:TT, 0:D], h2_res[:, t, :], ALU.add)\
                    .then_inc(out_ok.sem, 1)

            def x_low(b, sig_hi, sig, g, xa, xb2, xblo):
                ve.wait_ge(*sig_hi.at(g, 3))
                low(xa[1][:, :], b[:, 0:GT], xa[0][:, :]).then_inc(sig.sem, 1)
                low(xblo[:, :], b[0:DB, GT:2 * GT], xb2[0:DB, :]).then_inc(sig.sem, 1)

            def z_low(s, n):
                half, kind = n // 3, n % 3
                src = at(("z", n))
                done = 4 * half + (kind + 1 if kind < 2 else 4)
                ve.wait_ge(*z_hi.at(s.tg, done))
                if kind < 2:
                    h0 = 4 * half + 2 * kind
                    low(z_a[1][:, :, h0:h0 + 2, :].rearrange("p b h k -> p h b k"),
                        src[:, 0:2 * GT].rearrange("p (h b k) -> p h b k", h=2, b=GB),
                        z_a[0][:, :, h0:h0 + 2, :].rearrange("p b h k -> p h b k")).then_inc(z_lo.sem, 1)
                else:
                    for par in range(2):
                        hs = slice(4 * half + par, 4 * half + 4, 2)
                        low(z_b[DB:2 * DB, :, hs, :].rearrange("p b h k -> p h b k"),
                            src[par * DB:(par + 1) * DB, 0:2 * GT].rearrange("p (h b k) -> p h b k", h=2, b=GB),
                            z_b[0:DB, :, hs, :].rearrange("p b h k -> p h b k")).then_inc(z_lo.sem, 1)

            def choose_steps(s):
                g = s.fg
                pairs = g_sb[:, :, :].rearrange("p t (g two) -> p t g two", two=2)
                masked = g_msk[:, :, :].rearrange("p t (g two) -> p t g two", two=2)

                def rank(val, cmp, eq, below, res, m):
                    vj = val[:, :, :].unsqueeze(2).to_broadcast([TT, PAIRS, m, m])
                    vi = val[:, :, :].unsqueeze(3).to_broadcast([TT, PAIRS, m, m])
                    c4, e4 = (q[:, :, :].rearrange("p t (i j) -> p t i j", i=m) for q in (cmp, eq))
                    lo = below[:, :].unsqueeze(1).to_broadcast([TT, PAIRS, m * m])
                    yield lambda: v.tensor_tensor(c4, vj, vi, ALU.is_gt)
                    yield lambda: v.tensor_tensor(e4, vj, vi, ALU.is_equal)
                    yield lambda: v.tensor_tensor(eq[:, :, :], eq[:, :, :], lo, ALU.mult)
                    yield lambda: v.tensor_tensor(cmp[:, :, :], cmp[:, :, :], eq[:, :, :], ALU.add)
                    yield lambda: v.tensor_reduce(res[:, :, :], c4, axis=AX, op=ALU.add)

                def all_steps():
                    yield lambda: v.tensor_scalar(g_sig[:, :, :].rearrange("p t e -> p (t e)"), g_tanh[:, :], 0.5, 0.5,
                                                  ALU.mult, ALU.add)
                    yield lambda: v.tensor_tensor(g_sb[:, :, :], g_sig[:, :, :],
                                                  gb_row[:, :].unsqueeze(1).to_broadcast([TT, PAIRS, E]), ALU.add)
                    yield lambda: v.tensor_tensor(g_grp[:, :, :], pairs[:, :, :, 0], pairs[:, :, :, 1], ALU.add)
                    yield from rank(g_grp, g_cmp4, g_eq4, lt4, g_rank4, 4)
                    yield lambda: v.tensor_scalar(g_sel4[:, :, :], g_rank4[:, :, :], 2.0, 2 * BIG, ALU.is_lt, ALU.mult)
                    yield lambda: v.tensor_scalar(g_sel4[:, :, :], g_sel4[:, :, :], BIG, None, ALU.subtract)
                    yield lambda: v.tensor_tensor(masked, pairs,
                                                  g_sel4[:, :, :].unsqueeze(3).to_broadcast([TT, PAIRS, 4, 2]), ALU.min)
                    yield from rank(g_msk, g_cmp8, g_eq8, lt8, g_rank8, 8)
                    yield lambda: v.scalar_tensor_tensor(out=g_w[:, :, :], in0=g_rank8[:, :, :], scalar=2.0,
                                                         in1=g_sig[:, :, :], op0=ALU.is_lt, op1=ALU.mult)
                    yield lambda: v.tensor_reduce(g_sum[:, :], g_w[:, :, :], axis=AX, op=ALU.add)
                    yield lambda: v.tensor_scalar(g_sum[:, :], g_sum[:, :], 1e-6, None, ALU.add)
                    yield lambda: v.reciprocal(g_rec[:, :], g_sum[:, :])
                    yield lambda: v.tensor_tensor(g_cw[:, :, :], g_w[:, :, :],
                                                  g_rec[:, :].unsqueeze(2).to_broadcast([TT, PAIRS, E]), ALU.mult)

                for n, step in enumerate(all_steps()):
                    if n == 0:
                        ve.wait_ge(*g_th.at(g, 1))
                    else:
                        ve.wait_ge(*g_step.at(g, n))
                    if n == GATE_STEPS - 1 and s.key > 1:
                        ve.wait_ge(*cwt_mm.at(g - 1, 1))
                    step().then_inc(g_step.sem, 1)
                    yield

            def logit_max(s, j):
                lg = bank["logit"][0:NP, 0:H * NP].rearrange("p (h k) -> p h k", h=H)
                ve.wait_ge(*l_mm.at(s.ag, j + 1))
                v.tensor_reduce(row_max[:, :], lg, axis=AX, op=ALU.max).then_inc(mx_ok.sem, 1)
                ve.wait_ge(*mx_ok.at(s.ag, j + 1))
                if j >= 2:
                    ve.wait_ge(*pt_mm.at(s.ag, j - 1))
                elif s.key > 0:
                    ve.wait_ge(*pt_mm.at(s.ag - 1, j + 3))
                v.tensor_tensor(prob[j % 2][:, :, :], lg, row_max[:, :].unsqueeze(2).to_broadcast([NP, H, NP]),
                                ALU.subtract).then_inc(sub_ok.sem, 1)

            def prob_sum(s, j):
                ve.wait_ge(*exp_ok.at(s.ag, j + 1))
                v.tensor_reduce(row_sum[:, :], prob[j % 2][:, :, :], axis=AX, op=ALU.add).then_inc(sum_ok.sem, 1)
                ve.wait_ge(*sum_ok.at(s.ag, j + 1))
                if j:
                    ve.wait_ge(*pn_ok.at(s.ag, j))
                elif s.key > 0:
                    ve.wait_ge(*pn_ok.at(s.ag - 1, GB))
                v.reciprocal(row_rec[:, :], row_sum[:, :]).then_inc(rec_ok.sem, 1)

            def score_sum(s):
                ve.wait_ge(*av.at(s.tg, 1))
                v.tensor_reduce(score_raw[:, :], tanh_sb[:, :, :], axis=AX, op=ALU.add).then_inc(sc_raw.sem, 1)
                ve.wait_ge(*sc_raw.at(s.tg, 1))
                v.tensor_scalar(score[:, :], score_raw[:, :], vb_col[:, 0:1], None, ALU.add).then_inc(sc.sem, 1)

            def window_max(s):
                ve.wait_ge(*scT.at(s.tg, 1))
                win = bass.AP(at(("scT", 0)), 0, [[512, GB], [2, NP], [1, 4]])
                v.tensor_reduce(neg_max[:, :], win, axis=AX, op=ALU.max, negate=True).then_inc(nm.sem, 1)
                ve.wait_ge(*nm.at(s.tg, 1))
                v.tensor_tensor(max_diag[:, :, :], diag_mask[:, :, :],
                                neg_max[:, :].unsqueeze(1).to_broadcast([GB, GB, NP]), ALU.mult).then_inc(nmd.sem, 1)

            def band_exponent(s):
                ve.wait_ge(*band_mm.at(s.tg, 1))
                v.tensor_tensor(band[:, :, :], at(("band", 0))[0:S, 0:GT].rearrange("p (b q) -> p b q", b=GB),
                                score[:, :].unsqueeze(2).to_broadcast([S, GB, NP]), ALU.add).then_inc(band_in.sem, 1)

            def body(s):
                steps = choose_steps(s) if s.f else iter(())

                def gate(n):
                    for _ in range(n):
                        next(steps, None)

                if s.f:
                    norm_apply(s, s.fg, h2, mv2, rs2, xn2, rs2_ok, xn2_ok)
                if s.a:
                    logit_max(s, 0)
                if s.a:
                    prob_sum(s, 0)
                if s.y:
                    emit(s, 0)
                if s.f:
                    x_low(at(("x2", 0)), x2_hi, x2_lo, s.fg, x2_a, x2_b2, x2_blo)
                if s.a:
                    prob_lo(s, 0)
                    logit_max(s, 1)
                if s.t:
                    score_sum(s)
                if s.a:
                    prob_sum(s, 1)
                if s.a:
                    context_lo(s, 0)
                if s.f:
                    gate_product(s, 0)
                gate(1)
                if s.a:
                    prob_lo(s, 1)
                gate(1)
                if s.a:
                    logit_max(s, 2)
                gate(2)
                if s.t:
                    window_max(s)
                gate(1)
                if s.a:
                    prob_sum(s, 2)
                gate(2)
                if s.f:
                    gate_product(s, 1)
                gate(1)
                if s.a:
                    context_lo(s, 1)
                if s.y:
                    emit(s, 1)
                gate(3)
                if s.a:
                    prob_lo(s, 2)
                gate(2)
                if s.t:
                    band_exponent(s)
                gate(GATE_STEPS)
                if s.a:
                    residual(s, 0)
                if s.a:
                    logit_max(s, 3)
                if s.t:
                    ve.wait_ge(*mix_sb.at(s.tg, 2))
                    v.reciprocal(band_rden[:, :], at(("mix", 0))[0:TT, 2 * GT:2 * GT + PAIRS]).then_inc(rden.sem, 1)
                if s.a:
                    prob_sum(s, 3)
                    context_lo(s, 2)
                if s.f:
                    ve.wait_ge(*cwt_hi.at(s.fg, 1))
                    low(cwT[32:32 + E, :], at(("cwT", 0))[0:E, 0:GT], cwT[0:E, :]).then_inc(cwt_lo.sem, 1)
                if s.t:
                    ve.wait_ge(*p_mm2.at(s.tg, 1))
                    ve.wait_ge(*rden.at(s.tg, 1))
                    if s.key >= 0:
                        ve.wait_ge(*h1_kept.at(s.tg - 1, 1))
                    for t in range(PAIRS):
                        v.scalar_tensor_tensor(out=h1[:, t, :], in0=at(("proj", 0))[0:TT, t * D:(t + 1) * D],
                                               scalar=band_rden[:, t:t + 1], in1=pb_row[:, :], op0=ALU.mult,
                                               op1=ALU.add).then_inc(h1_ok.sem, 1)
                if s.t:
                    for t in range(PAIRS):
                        norm_stats(s, s.tg, t, h1, st1, mv1, h1_ok, st1_ok, mv1_ok)
                    norm_eps(s, s.tg, mv1, ve1, mv1_ok, ve1_ok)
                if s.a:
                    prob_lo(s, 3)
                if s.f:
                    gate_product(s, 2)
                if s.t:
                    if s.key >= 0:
                        ve.wait_ge(*xn_lo_ok.at(s.tg - 1, 1))
                        ve.wait_ge(*xn_hi_ok.at(s.tg - 1, 1))
                    norm_apply(s, s.tg, h1, mv1, rs1, xn1, rs1_ok, xn1_ok)
                if s.f:
                    weigh(s, 1)
                if s.a:
                    context_lo(s, 3)
                if s.f:
                    weigh(s, 2)
                    gate_product(s, 3)
                if s.t:
                    x_low(at(("x1", 0)), x1_hi, x1_lo, s.tg, x1_a, x1_b2, x1_blo)
                if s.a:
                    residual(s, 1)
                    norm_eps(s, s.ag, mv2, ve2, mv2_ok, ve2_ok)
                if s.f:
                    weigh(s, 3)
                if s.t:
                    z_low(s, 0)
                    z_low(s, 1)
                if s.f:
                    gate_product(s, 4)
                    weigh(s, 4)
                if s.t:
                    for n in range(2, 6):
                        z_low(s, n)

            sections(ve, body)

        @block.gpsimd
        def _(po):
            p = nc.gpsimd
            po.dma_start(rel_raw, rel).then_inc(d_rel, 16)
            for dst, src in ((ident[:, :], c_ident), (band_raw[:, :], c_band), (diag_mask[:, :, :], c_diag),
                             (flip_raw[:, :], c_flip), (pick_raw[:, :, :], c_pick),
                             (lt4[:, :], c_lt4.partition_broadcast(TT)), (lt8[:, :], c_lt8.partition_broadcast(TT)),
                             (v_row[:, :], tok_v.partition_broadcast(S)), (vb_col[:, :], tok_vb.partition_broadcast(S)),
                             (pb_row[:, :], tok_pb.partition_broadcast(TT)),
                             (gb_row[:, :], gate_b.partition_broadcast(TT)),
                             (gw_raw_a[:, :], gate_w[0:DA, :]), (gw_raw_b[:, :], gate_w[DA:D, :])):
                po.dma_start(dst, src).then_inc(d_small, 16)
            po.wait_ge(d_small, 16 * SMALL_LOADS)

            def inv_sqrt(g, ve_ok, veps, rs, ok):
                po.wait_ge(*ve_ok.at(g, 1))
                p.tensor_tensor(rs[:, :], veps[:, :], minus_half[:, :], ALU.pow).then_inc(ok.sem, 1)

            def hidden_lo(s, j):
                n, es = unit(j)
                po.wait_ge(*hid_hi.at(s.fg, j + 1))
                p.tensor_tensor(hid[1][:, es, :], act[j % 2][:, 0:n, :], hid[0][:, es, :].bitcast(FP32),
                                ALU.subtract).then_inc(hid_lo.sem, 1)

            def body(s):
                for j in range(GB):
                    if s.a:
                        po.wait_ge(*rec_ok.at(s.ag, j + 1))
                        q = prob[j % 2][:, :, :]
                        p.tensor_tensor(q, q, row_rec[:, :].unsqueeze(2).to_broadcast([NP, H, NP]), ALU.mult)\
                            .then_inc(pn_ok.sem, 1)
                    if s.t and j == 0:
                        po.wait_ge(*a_tanh.at(s.tg, 2))
                        p.tensor_tensor(tanh_sb[:, :, :], tanh_sb[:, :, :],
                                        v_row[:, :].unsqueeze(1).to_broadcast([S, GB, D]), ALU.mult).then_inc(av.sem, 1)
                    if s.f and j == 2:
                        hidden_lo(s, 0)
                if s.t:
                    inv_sqrt(s.tg, ve1_ok, ve1, rs1, rs1_ok)
                if s.f:
                    hidden_lo(s, 1)
                    hidden_lo(s, 2)
                if s.a:
                    inv_sqrt(s.ag, ve2_ok, ve2, rs2, rs2_ok)
                if s.t:
                    po.wait_ge(*xn_hi_ok.at(s.tg, 1))
                    if s.key >= 0:
                        po.wait_ge(*xc_moved.at(s.tg - 1, 96))
                    p.tensor_tensor(xn_half[1][:, :, :], xn1[:, :, :], xn_half[0][:, :, :].bitcast(FP32), ALU.subtract)\
                        .then_inc(xn_lo_ok.sem, 1)
                if s.f:
                    hidden_lo(s, 3)
                    hidden_lo(s, 4)

            sections(po, body)


def kernel(x, L0_tok_W_w, L0_tok_W_b, L0_tok_b, L0_tok_V_w, L0_tok_V_b, L0_tok_P_w, L0_tok_P_b, L0_attn_w_q,
           L0_attn_w_k, L0_attn_w_v, L0_attn_w_o, L0_attn_rel_emb, L0_ffn_gate_weight, L0_ffn_gate_bias, L0_ffn_w1,
           L0_ffn_w2, L0_ffn_w3, L0_ffn_sw1, L0_ffn_sw2, L0_ffn_sw3):
    import numpy as np
    import concourse.bacc as bacc
    from concourse.bass_utils import run_bass_kernel_spmd

    def put(a):
        return np.ascontiguousarray(np.asarray(a))

    x = put(x)
    n = np.arange
    ident = np.eye(128, dtype=np.float32)
    off = n(S)[:, None] - 2 * n(NP)[None, :]
    band = np.where((off >= 0) & (off < 4), 0.0, -1e30).astype(np.float32)
    diag = np.repeat(np.eye(GB, dtype=np.float32)[:, :, None], NP, axis=2)
    flip = np.zeros((KS, NP), np.float32)
    flip[n(NP), NP - 1 - n(NP)] = 1.0
    flip[LO + n(NP), NP - 1 - n(NP)] = 1.0
    pick = np.zeros((40, E, 128), np.float32)
    pick[n(E), n(E), :] = 1.0
    pick[32 + n(E), n(E), :] = 1.0
    below = lambda m: (n(m)[None, :] < n(m)[:, None]).astype(np.float32).reshape(-1)
    arrays = {
        "x": x, "xT": put(x.reshape(B * S, D).T),
        "tok_wT": put(np.asarray(L0_tok_W_w).T), "tok_bias": put(np.stack([np.asarray(L0_tok_W_b), np.asarray(L0_tok_b)])),
        "tok_v": put(np.asarray(L0_tok_V_w).reshape(D)), "tok_vb": put(L0_tok_V_b),
        "tok_pT": put(np.asarray(L0_tok_P_w).T), "tok_pb": put(L0_tok_P_b),
        "wqT": put(np.asarray(L0_attn_w_q).transpose(2, 0, 1)), "wkT": put(np.asarray(L0_attn_w_k).transpose(2, 0, 1)),
        "wvT": put(np.asarray(L0_attn_w_v).transpose(2, 0, 1)), "wo": put(np.asarray(L0_attn_w_o).transpose(1, 0, 2)),
        "rel": put(np.asarray(L0_attn_rel_emb)[:, 100 - NP:100 + NP - 1, :, 0].transpose(1, 0, 2)),
        "gate_w": put(np.asarray(L0_ffn_gate_weight).T), "gate_b": put(L0_ffn_gate_bias),
        "w1T": put(np.asarray(L0_ffn_w1).transpose(2, 0, 1)), "w3T": put(np.asarray(L0_ffn_w3).transpose(2, 0, 1)),
        "w2T": put(np.asarray(L0_ffn_w2).transpose(2, 0, 1)),
        "sw1T": put(np.asarray(L0_ffn_sw1).T), "sw3T": put(np.asarray(L0_ffn_sw3).T), "sw2T": put(np.asarray(L0_ffn_sw2).T),
        "c_ident": ident, "c_band": put(np.tile(band, (1, GB))), "c_diag": put(diag), "c_flip": flip, "c_pick": pick,
        "c_lt4": put(below(4)), "c_lt8": put(below(8)),
    }
    nc = bacc.Bacc("TRN2", target_bir_lowering=False, num_devices=1)
    feeds, args = {}, []
    for name, a in arrays.items():
        feeds[f"in_{name}"] = a
        args.append(nc.dram_tensor(f"in_{name}", a.shape, mybir.dt.from_np(a.dtype), kind="ExternalInput").ap())
    out = nc.dram_tensor("out", (B, NP, D), FP32, kind="ExternalOutput").ap()
    audio_tower_kernel(nc, *args, out)
    return run_bass_kernel_spmd(nc, [feeds], core_ids=[0]).results[0]["out"]
```

```python
import concourse.bass as bass
from concourse import mybir
from contextlib import ExitStack

FP32 = mybir.dt.float32
F32R = mybir.dt.float32r
ALU = mybir.AluOpType
ACT = mybir.ActivationFunctionType
AX = mybir.AxisListType.X

B, S, D = 64, 125, 192
NP = (S - 4) // 2 + 1
H, DH = 8, 96
E, INTER = 8, 128
GB = 4
NG = B // GB
PAIRS = GB // 2
TT = 2 * NP
GT = GB * NP
DA, DB = 128, D - 128
LO = 64
KS = LO + NP
HP = H // 2
LN_EPS = 1e-5
BIG = 1.5e38


class Signal:

    def __init__(self, sem, per_group):
        self.sem, self.n = sem, per_group

    def at(self, g, k):
        return self.sem, g * self.n + k


def split_product(pe, out, xa_hi, xa_lo, xb2, xb_lo, wa_hi, wa_lo, wb):
    pe.matmul(out, xa_hi, wa_hi, start=True, stop=False)
    pe.matmul(out, xa_hi, wa_lo, start=False, stop=False)
    pe.matmul(out, xa_lo, wa_hi, start=False, stop=False)
    pe.matmul(out, xb2, wb, start=False, stop=False)
    return pe.matmul(out, xb_lo, wb[0:DB], start=False, stop=True)


def audio_tower_kernel(nc, x, xT, tok_wT, tok_bias, tok_v, tok_vb, tok_pT, tok_pb, wqT, wkT, wvT, wo, rel, gate_w,
                       gate_b, w1T, w3T, w2T, sw1T, sw3T, sw2T, c_ident, c_band, c_diag, c_flip, c_pick, c_lt4,
                       c_lt8, out):
    scratch = nc.dram_tensor("bias_sums", [H, 2 * NP], FP32, kind="Internal")

    ctx = ExitStack()
    with ctx:
        def sb(name, shape, dt=FP32, where=ctx):
            return where.enter_context(nc.sbuf_tensor(name, shape, dt))

        def sem(name):
            return ctx.enter_context(nc.semaphore(name))

        def signal(name, per_group):
            return Signal(sem(name), per_group)

        qk_a = [sb(f"qk_a{n}", [DA, HP, 3, 128], F32R) for n in range(2)]
        qk_b = sb("qk_b", [2 * DB, HP, 3, 128], F32R)
        vo_a2, vo_b2 = sb("vo_a", [DA, H, 2, D], F32R), sb("vo_b", [2 * DB, HP, 2, D], F32R)
        vo_a, vo_b = ([w[:, :, n, :] for n in range(2)] for w in (vo_a2, vo_b2))
        up_a = [sb(f"up_a{n}", [DA, E + 1, 2, INTER], F32R) for n in range(2)]
        up_b = sb("up_b", [2 * DB, E + 1, 2, INTER], F32R)
        down2 = sb("down", [INTER, E + 1, 2, D], F32R)
        down = [down2[:, :, n, :] for n in range(2)]
        gw_a = [sb(f"gw_a{n}", [DA, E], F32R) for n in range(2)]
        gw_b = sb("gw_b", [2 * DB, E], F32R)
        bias = sb("bias", [KS, H, NP], F32R)
        tw_a, tw_b = sb("tw_a", [DA, D]), sb("tw_b", [DB + 2, D])
        tp_a, tp_b = sb("tp_a", [DA, D]), sb("tp_b", [DB, D])
        v_row, vb_col = sb("v_row", [S, D]), sb("vb_col", [S, 1])
        pb_row, gb_row = sb("pb_row", [TT, D]), sb("gb_row", [TT, E])
        ident = sb("ident", [128, 128])
        ident_r = sb("ident_r", [S, S], F32R)
        band_raw, band_mask = sb("band_raw", [S, GB * NP]), sb("band_mask", [S, GB * NP], F32R)
        diag_mask = sb("diag_mask", [GB, GB, NP])
        flip_raw, flip = sb("flip_raw", [KS, NP]), sb("flip", [KS, NP], F32R)
        pick_raw, pick = sb("pick_raw", [40, E, 128]), sb("pick", [40, E, 128], F32R)
        lt4, lt8 = sb("lt4", [TT, 16]), sb("lt8", [TT, 64])
        ones = sb("ones", [128, 128])
        minus_half = sb("minus_half", [TT, PAIRS])
        wait_cell = sb("wait_cell", [TT, 1])
        xin_a, xin_b = sb("xin_a", [DA, GB * S]), sb("xin_b", [DB + 2, GB * S])
        xin = sb("xin", [S, GB, D])
        tanh_sb = sb("tanh_sb", [S, GB, D])
        score_raw, score = sb("score_raw", [S, GB]), sb("score", [S, GB])
        neg_max, max_diag = sb("neg_max", [GB, NP]), sb("max_diag", [GB, GB, NP])
        band = sb("band", [S, GB, NP])
        mix_a, mix_b = sb("mix_a", [DA, GT]), sb("mix_b", [DB, GT])
        band_rden = sb("band_rden", [TT, PAIRS])
        h1, h1_res = sb("h1", [TT, PAIRS, D]), sb("h1_res", [TT, PAIRS, D])
        st1, mv1, ve1, rs1 = (sb("st1", [TT, PAIRS, 6]), sb("mv1", [TT, PAIRS, 2]), sb("ve1", [TT, PAIRS]),
                              sb("rs1", [TT, PAIRS]))
        xn1 = sb("xn1", [TT, PAIRS, D])
        xn_half = [sb(f"xn_half{n}", [TT, PAIRS, D], F32R) for n in range(2)]
        xc_hi = sb("xc_hi", [KS, GB, D], F32R)
        xc_lo = sb("xc_lo", [NP, GB, D], F32R)
        x1_a = [sb(f"x1_a{n}", [DA, GT], F32R) for n in range(2)]
        x1_b2, x1_blo = sb("x1_b2", [2 * DB, GT], F32R), sb("x1_blo", [DB, GT], F32R)
        prob = [sb(f"prob{n}", [NP, H, NP]) for n in range(2)]
        row_max, row_sum, row_rec = (sb("row_max", [NP, H]), sb("row_sum", [NP, H]), sb("row_rec", [NP, H]))
        probT = sb("probT", [KS, H * NP], F32R)
        h2, h2_res = sb("h2", [TT, PAIRS, D]), sb("h2_res", [TT, PAIRS, D])
        st2, mv2, ve2, rs2 = (sb("st2", [TT, PAIRS, 6]), sb("mv2", [TT, PAIRS, 2]), sb("ve2", [TT, PAIRS]),
                              sb("rs2", [TT, PAIRS]))
        xn2 = sb("xn2", [TT, PAIRS, D])
        x2_a = [sb(f"x2_a{n}", [DA, GT], F32R) for n in range(2)]
        x2_b2, x2_blo = sb("x2_b2", [2 * DB, GT], F32R), sb("x2_blo", [DB, GT], F32R)
        g_tanh, g_sig, g_sb = (sb("g_tanh", [TT, PAIRS * E]), sb("g_sig", [TT, PAIRS, E]), sb("g_sb", [TT, PAIRS, E]))
        g_grp, g_rank4, g_sel4 = (sb("g_grp", [TT, PAIRS, 4]), sb("g_rank4", [TT, PAIRS, 4]), sb("g_sel4", [TT, PAIRS, 4]))
        g_cmp4, g_eq4 = sb("g_cmp4", [TT, PAIRS, 16]), sb("g_eq4", [TT, PAIRS, 16])
        g_msk = sb("g_msk", [TT, PAIRS, E])
        g_cmp8, g_eq8 = sb("g_cmp8", [TT, PAIRS, 64]), sb("g_eq8", [TT, PAIRS, 64])
        g_rank8, g_w = sb("g_rank8", [TT, PAIRS, E]), sb("g_w", [TT, PAIRS, E])
        g_sum, g_rec = sb("g_sum", [TT, PAIRS]), sb("g_rec", [TT, PAIRS])
        g_cw = sb("g_cw", [TT, PAIRS, E])
        cwT = sb("cwT", [40, GT], F32R)
        act = [sb(f"act{n}", [INTER, 2, GT]) for n in range(2)]
        out_sb = sb("out_sb", [TT, PAIRS, D])

        raw = ExitStack()
        rq, rk, rv, ro = (sb(f"raw_{n}", [DH, H, D], FP32, raw) for n in "qkvo")
        r_up_a, r_up_b = (sb(f"raw_up{n}", [p, E + 1, 2, INTER], FP32, raw) for n, p in (("a", DA), ("b", DB)))
        r_down = sb("raw_down", [INTER, E + 1, D], FP32, raw)
        raw.close()
        z_a = [sb(f"z_a{n}", [DA, GB, H, NP], F32R) for n in range(2)]
        z_b = sb("z_b", [2 * DB, GB, H, NP], F32R)
        c_a = [sb(f"c_a{n}", [DA, H, 2, NP], F32R) for n in range(2)]
        c_b = [sb(f"c_b{n}", [2 * DB, HP, 2, NP], F32R) for n in range(2)]
        hid = [sb(f"hid{n}", [INTER, E + 1, GT], F32R) for n in range(2)]
        rel_raw = tanh_sb[0:2 * NP - 1, :, :].rearrange("p b d -> p (b d)").rearrange("p (h e) -> p h e", h=H)
        rel_sum, rel_sumT = sb("rel_sum", [2 * NP - 1, H]), sb("rel_sumT", [H, 2 * NP])
        bias_raw = sb("bias_raw", [NP, H, NP])
        gw_raw_a, gw_raw_b = sb("gw_raw_a", [DA, E]), sb("gw_raw_b", [DB, E])

        bank = {n: ctx.enter_context(nc.psum_tensor(f"bank_{n}", [128, 512], FP32))
                for n in ("logit", "probT", "ca", "cb", "up", "gate_up", "s0", "s1")}

        d_tok, d_proj, d_ident, d_small, d_late, d_qk, d_vo, d_up, d_down, d_rel, d_bias = (
            sem(n) for n in ("d_tok", "d_proj", "d_ident", "d_small", "d_late", "d_qk", "d_vo", "d_up", "d_down", "d_rel", "d_bias"))
        p_fill, p_const, p_mm, p_hi, p_lo, p_rel, p_relT, p_relc, d_relw = (
            sem(n) for n in ("p_fill", "p_const", "p_mm", "p_hi", "p_lo", "p_rel", "p_relT", "p_relc", "d_relw"))

        x_loaded = signal("x_loaded", 48)
        a_mm, a_tanh = signal("a_mm", 2), signal("a_tanh", 2)
        av, sc_raw, sc, scT = signal("av", 1), signal("sc_raw", 1), signal("sc", 1), signal("scT", 1)
        nm, nmd, band_mm, band_in, band_e = (signal(n, 1) for n in ("nm", "nmd", "band_mm", "band_in", "band_e"))
        mix_mm, mix_sb, rden, p_mm2, h1_ok = (signal("mix_mm", 1), signal("mix_sb", 2), signal("rden", 1),
                                              signal("proj_mm", 1), signal("h1_ok", 2))
        st1_ok, mv1_ok, ve1_ok, rs1_ok, xn1_ok = (signal("st1_ok", 2), signal("mv1_ok", 2), signal("ve1_ok", 1),
                                                  signal("rs1_ok", 1), signal("xn1_ok", 2))
        xn_hi_ok, xn_lo_ok, xc_moved, h1_kept = (signal("xn_hi_ok", 1), signal("xn_lo_ok", 1), signal("xc_moved", 96),
                                                 signal("h1_kept", 1))
        x1_mm, x1_hi, x1_lo = signal("x1_mm", 1), signal("x1_hi", 3), signal("x1_lo", 2)
        z_mm, z_hi, z_lo = signal("z_mm", 6), signal("z_hi", 8), signal("z_lo", 8)
        l_mm, mx_ok, sub_ok, exp_ok, sum_ok, rec_ok, pn_ok = (
            signal(n, GB) for n in ("l_mm", "mx_ok", "sub_ok", "exp_ok", "sum_ok", "rec_ok", "pn_ok"))
        pt_mm, pt_hi, pt_lo, ca_mm, ca_hi, ca_lo, cb_mm = (
            signal(n, GB) for n in ("pt_mm", "pt_hi", "pt_lo", "ca_mm", "ca_hi", "ca_lo", "cb_mm"))
        cb_hi, cb_lo = signal("cb_hi", 2 * GB), signal("cb_lo", 2 * GB)
        o_mm, h2_ok, st2_ok, mv2_ok, ve2_ok, rs2_ok, xn2_ok, h2_kept = (
            signal("o_mm", 2), signal("h2_ok", 2), signal("st2_ok", 2), signal("mv2_ok", 2), signal("ve2_ok", 1),
            signal("rs2_ok", 1), signal("xn2_ok", 2), signal("h2_kept", 1))
        x2_mm, x2_hi, x2_lo = signal("x2_mm", 1), signal("x2_hi", 3), signal("x2_lo", 2)
        g_mm, g_th = signal("g_mm", 1), signal("g_th", 1)
        GATE_STEPS = 21
        g_step = signal("g_step", GATE_STEPS)
        cwt_mm, cwt_hi, cwt_lo = signal("cwt_mm", 1), signal("cwt_hi", 1), signal("cwt_lo", 1)
        cw_mm, w_ok = signal("cw_mm", HP), signal("w_ok", HP)
        up_mm, tanh_ok, u_ok, v_ok, hid_hi, hid_lo = (
            signal(n, HP + 1) for n in ("up_mm", "tanh_ok", "u_ok", "v_ok", "hid_hi", "hid_lo"))
        h2_part, out_part = signal("h2_part", 2), signal("out_part", 2)
        y_mm, out_ok, out_sent = signal("y_mm", 2), signal("out_ok", 2), signal("out_sent", 16)

        def unit(u):
            return (1, slice(E, E + 1)) if u == 0 else (2, slice(2 * u - 2, 2 * u))

        class Section:

            def __init__(self, i, key):
                self.i, self.key = i, key
                self.t, self.a, self.f, self.y = key < NG - 1, 0 <= key < NG, 1 <= key <= NG, key >= 2
                self.tg, self.ag, self.fg, self.yg = i + 1, i, i - 1, i - 2

            def has(self, stage):
                return {"t": self.t, "a": self.a, "f": self.f, "y": self.y}[stage]

            def group(self, stage):
                return {"t": self.tg, "a": self.ag, "f": self.fg, "y": self.yg}[stage]

        LOOP = 3

        def sections(eng, body):
            for i in range(-1, LOOP):
                body(Section(i, i))
            with eng.Fori(LOOP, NG - 2) as i:
                body(Section(i, LOOP))
            for i in range(NG - 2, NG + 2):
                body(Section(i, i))

        Z_TILES = [(0, 0), (0, 1), (0, 2), (1, 2), (1, 0), (1, 1)]
        NORM_ON_VECTOR = (0, 1)
        UNITS = HP + 1
        USES = {}
        for j in range(GB):
            USES["logit", j] = ("logit", "a", sub_ok, j + 1)
            USES["probT", j] = ("probT", "a", pt_lo, j + 1)
            USES["ca", j] = ("ca", "a", ca_lo, j + 1)
            USES["cb", j] = ("cb", "a", cb_lo, 2 * (j + 1))
            if j == 1:
                USES["o", 0] = ("cb", "a", h2_ok, 1)
        USES["up", 0] = ("gate_up", "f", v_ok, 1)
        for u in range(1, UNITS):
            USES["up", u] = ("logit" if u == 3 else "up", "f", u_ok, u + 1)
            USES["gate_up", u] = ("gate_up", "f", v_ok, u + 1)
        USES["o", 1] = ("probT", "a", h2_ok, 2)
        for n, (b, k) in enumerate([("logit", 1), ("ca", 2), ("probT", 4), ("cb", 6), ("gate_up", 7), ("up", 8)]):
            USES["z", n] = (b, "t", z_lo, k)
        for name, b, stage, sig, k in [
                (("score", 0), "s0", "t", a_tanh, 1), (("x2", 0), "s1", "f", x2_lo, 2),
                (("score", 1), "s1", "t", a_tanh, 2), (("y", 0), "s0", "y", out_ok, 1), (("gate", 0), "s1", "f", g_th, 1),
                (("scT", 0), "s0", "t", nm, 1), (("y", 1), "s1", "y", out_ok, 2), (("band", 0), "s0", "t", band_in, 1),
                (("mix", 0), "s1", "t", rden, 1), (("cwT", 0), "s0", "f", cwt_lo, 1), (("cw", 0), "s0", "f", w_ok, 1),
                (("proj", 0), "s1", "t", h1_ok, 2), (("cw", 1), "s0", "f", w_ok, 2), (("x1", 0), "s1", "t", x1_lo, 2),
                (("cw", 2), "s1", "f", w_ok, 3), (("cw", 3), "s0", "f", w_ok, 4)]:
            USES[name] = (b, stage, sig, k)

        def free(pe, sec, name):
            order = [u for u in USES if USES[u][0] == USES[name][0]]
            here = [(sec, u) for u in order[:order.index(name)]]
            before = [(Section(sec.i - 1, sec.key - 1), u) for u in order] if sec.key >= 0 else []
            for where, u in reversed(before + here):
                _, stage, sig, k = USES[u]
                if where.has(stage):
                    pe.wait_ge(*sig.at(where.group(stage), k))
                    return

        def at(name):
            return bank[USES[name][0]]

        UP_CHUNKS = 3
        SMALL_LOADS, LATE_LOADS = 5, 7
        PRODUCTS = [(k, hp, c0, cn) for k in range(2) for hp in range(HP) for c0, cn in ((0, DA), (DA, DB))]
        PREP_BANKS = ["logit", "probT", "ca", "cb", "up", "gate_up"]
        block = ctx.enter_context(nc.Block())

        @block.sync
        def _(sp):
            def load_x(g):
                sp.dma_start(xin_a[:, :], xT[0:DA, bass.ds(g * (GB * S), GB * S)]).then_inc(x_loaded.sem, 16)
                sp.dma_start(xin_b[0:DB, :], xT[DA:D, bass.ds(g * (GB * S), GB * S)]).then_inc(x_loaded.sem, 16)
                sp.dma_start(xin[:, :, :], x[bass.ds(g * GB, GB), :, :].rearrange("b s d -> s b d"))\
                    .then_inc(x_loaded.sem, 16)

            sp.dma_start(ident[:, :], c_ident).then_inc(d_ident, 16)
            load_x(0)
            for dst, src in ((v_row[:, :], tok_v.partition_broadcast(S)), (vb_col[:, :], tok_vb.partition_broadcast(S)),
                             (band_raw[:, :], c_band), (diag_mask[:, :, :], c_diag),
                             (pb_row[:, :], tok_pb.partition_broadcast(TT))):
                sp.dma_start(dst, src).then_inc(d_small, 16)
            sp.dma_start(tp_a[:, :], tok_pT[0:DA, :]).then_inc(d_proj, 16)
            sp.dma_start(tp_b[:, :], tok_pT[DA:D, :]).then_inc(d_proj, 16)
            sp.dma_start(rv[:, :, :], wvT).then_inc(d_vo, 16)
            sp.dma_start(ro[:, :, :], wo).then_inc(d_vo, 16)
            sp.dma_start(r_up_a[:, 0:E, 0, :], w1T[0:DA]).then_inc(d_up, 16)
            sp.dma_start(r_up_a[:, 0:E, 1, :], w3T[0:DA]).then_inc(d_up, 16)
            sp.dma_start(r_up_a[:, E, 0, :], sw1T[0:DA]).then_inc(d_up, 16)
            sp.dma_start(r_up_a[:, E, 1, :], sw3T[0:DA]).then_inc(d_up, 16)
            sp.dma_start(r_up_b[:, 0:E, 0, :], w1T[DA:D]).then_inc(d_up, 16)
            sp.dma_start(r_up_b[:, 0:E, 1, :], w3T[DA:D]).then_inc(d_up, 16)
            sp.dma_start(r_up_b[:, E, 0, :], sw1T[DA:D]).then_inc(d_up, 16)
            sp.dma_start(r_up_b[:, E, 1, :], sw3T[DA:D]).then_inc(d_up, 16)
            sp.dma_start(r_down[:, 0:E, :], w2T).then_inc(d_down, 16)
            sp.dma_start(r_down[:, E, :], sw2T).then_inc(d_down, 16)
            sp.wait_ge(p_relc, 1)
            sp.dma_start(scratch[:, 0:2 * NP - 1], rel_sumT[:, 0:2 * NP - 1]).then_inc(d_relw, 16)
            sp.wait_ge(d_relw, 16)
            sp.dma_start(bias_raw[:, :, :], bass.AP(scratch, 0, [[1, NP], [2 * NP, H], [1, NP]])).then_inc(d_bias, 16)

            def body(s):
                if s.y:
                    sp.wait_ge(*out_ok.at(s.yg, 2))
                    dst = out[bass.ds(s.yg * GB, GB), :, :].rearrange("(t b) p d -> (b p) t d", b=2)
                    sp.dma_start(dst, out_sb[:, :, :]).then_inc(out_sent.sem, 16)
                if s.t and s.key < NG - 2:
                    sp.wait_ge(*mix_mm.at(s.tg, 1))
                    load_x(s.tg + 1)
                if s.t:
                    sp.wait_ge(*xn_hi_ok.at(s.tg, 1))
                    sp.wait_ge(*xn_lo_ok.at(s.tg, 1))
                    if s.a:
                        sp.wait_ge(*cb_mm.at(s.ag, GB))
                    else:
                        sp.wait_ge(p_fill, 6)
                    for par in range(2):
                        src = slice(par * NP, (par + 1) * NP)
                        for dst, n in ((xc_hi[0:NP], 0), (xc_hi[LO:KS], 0), (xc_lo[:, :, :], 1)):
                            sp.dma_start(dst[:, par::2, :].bitcast(FP32), xn_half[n][src, :, :].bitcast(FP32))\
                                .then_inc(xc_moved.sem, 16)

            sections(sp, body)
            sp.wait_ge(out_sent.sem, 16 * NG)

        @block.tensor
        def _(pe):
            mm = nc.tensor.matmul

            pe.wait_ge(p_rel, 1)
            pe.wait_ge(d_ident, 16)
            nc.tensor.transpose(bank["s0"][0:H, 0:2 * NP - 1], rel_sum[:, :], ident[0:2 * NP - 1, 0:2 * NP - 1])\
                .then_inc(p_relT, 1)

            def products(first, end):
                for n in range(first, end):
                    k, hp, c0, cn = PRODUCTS[n]
                    left, right, loaded = ((rk, rq, d_qk), (rv, ro, d_vo))[k]
                    pe.wait_ge(loaded, 32)
                    dst = bank[PREP_BANKS[n % 6]]
                    if n >= 6:
                        pe.wait_ge(p_lo, n - 5)
                    for par in range(2):
                        last = mm(dst[0:cn, par * D:(par + 1) * D], left[:, 2 * hp + par, c0:c0 + cn],
                                  right[:, 2 * hp + par, :], start=True, stop=True)
                    last.then_inc(p_mm, 1)

            def hidden(ex, n, kind, dst):
                for e in range(n):
                    o = dst[:, e * GT:(e + 1) * GT]
                    wa, wl, wb = (w[:, ex + e, kind, :] for w in (up_a[0], up_a[1], up_b))
                    mm(o, wa, x2_a[0][:, :], start=True, stop=False)
                    mm(o, wa, x2_a[1][:, :], start=False, stop=False)
                    mm(o, wl, x2_a[0][:, :], start=False, stop=False)
                    mm(o, wb, x2_b2[:, :], start=False, stop=False)
                    last = mm(o, wb[0:DB], x2_blo[:, :], start=False, stop=True)
                return last

            def out_proj(s, t):
                free(pe, s, ("o", t))
                g = s.ag
                pe.wait_ge(*ca_lo.at(g, 2 * t + 2))
                pe.wait_ge(*cb_lo.at(g, 4 * t + 4))
                both, o = at(("o", t))[0:TT, 0:2 * D], at(("o", t))[0:TT, 0:D]
                for hh in range(H):
                    ch, cl = (c[:, hh, :, :].rearrange("p b q -> p (b q)") for c in c_a)
                    mm(both, ch, vo_a2[:, hh, :, :].rearrange("p n d -> p (n d)"), start=hh == 0, stop=False)
                    mm(o, cl, vo_a[0][:, hh, :], start=False, stop=False)
                for hp in range(HP):
                    ch, cl = (c[:, hp, :, :].rearrange("p b q -> p (b q)") for c in c_b)
                    mm(o, cl, vo_b[0][:, hp, :], start=False, stop=False)
                    last = mm(both, ch, vo_b2[:, hp, :, :].rearrange("p n d -> p (n d)"), start=False, stop=hp == HP - 1)
                last.then_inc(o_mm.sem, 1)

            def logits(s, j):
                free(pe, s, ("logit", j))
                if j == 0:
                    pe.wait_ge(*z_hi.at(s.ag, 8))
                    if s.key == 0:
                        pe.wait_ge(p_lo, 17)
                        pe.wait_ge(p_const, 2)
                q = slice(j * NP, (j + 1) * NP)
                o = bank["logit"][0:NP, 0:H * NP]
                mm(o, flip[:, :], bias[:, :, :].rearrange("p h k -> p (h k)"), start=True, stop=False)
                zh, zl, zb = (z[:, j, :, :].rearrange("p h k -> p (h k)") for z in (z_a[0], z_a[1], z_b))
                mm(o, x1_a[0][:, q], zh, start=False, stop=False)
                mm(o, x1_a[1][:, q], zh, start=False, stop=False)
                if j == 0:
                    pe.wait_ge(*z_lo.at(s.ag, 6))
                mm(o, x1_b2[:, q], zb, start=False, stop=False)
                mm(o, x1_blo[:, q], zb[0:DB], start=False, stop=False)
                if j == 0:
                    pe.wait_ge(*z_lo.at(s.ag, 8))
                mm(o, x1_a[0][:, q], zl, start=False, stop=True).then_inc(l_mm.sem, 1)

            def prob_transpose(s, j):
                free(pe, s, ("probT", j))
                pe.wait_ge(*pn_ok.at(s.ag, j + 1))
                mm(bank["probT"][0:NP, 0:2], flip[:, :], ident_r[:, 0:2], start=True, stop=True)
                for hh in range(H):
                    last = nc.tensor.transpose(bank["probT"][0:NP, hh * NP:(hh + 1) * NP], prob[j % 2][:, hh, :],
                                               ident[0:NP, 0:NP])
                last.then_inc(pt_mm.sem, 1)

            def context(s, j):
                if j == 0:
                    pe.wait_ge(*xc_moved.at(s.ag, 96))
                pe.wait_ge(*pt_hi.at(s.ag, j + 1))
                parts = (("ca", ca_mm, 0, DA), ("cb", cb_mm, DA, DB))
                free(pe, s, ("ca", j))
                free(pe, s, ("cb", j))
                for name, _, c0, cn in parts:
                    mm(bank[name][0:cn, 0:H * NP], xc_lo[:, j, c0:c0 + cn], probT[0:NP, :], start=True, stop=False)
                pe.wait_ge(*pt_lo.at(s.ag, j + 1))
                for name, sig, c0, cn in parts:
                    mm(bank[name][0:cn, 0:H * NP], xc_hi[:, j, c0:c0 + cn], probT[:, :], start=False, stop=True)\
                        .then_inc(sig.sem, 1)

            def token_scores(s, m):
                free(pe, s, ("score", m))
                if m == 0:
                    pe.wait_ge(*x_loaded.at(s.tg, 48))
                    if s.key < 0:
                        pe.wait_ge(d_tok, 48)
                        pe.wait_ge(p_fill, 3)
                        pe.wait_ge(p_relc, 1)
                for e in range(2):
                    o = at(("score", m))[0:S, e * D:(e + 1) * D]
                    p = slice((2 * m + e) * S, (2 * m + e + 1) * S)
                    mm(o, xin_a[:, p], tw_a[:, :], start=True, stop=False)
                    last = mm(o, xin_b[:, p], tw_b[:, :], start=False, stop=True)
                last.then_inc(a_mm.sem, 1)

            def experts(s, u, kind):
                if u == 0:
                    if kind == 0:
                        pe.wait_ge(*x2_lo.at(s.fg, 2))
                        free(pe, s, ("up", 0))
                    last = hidden(E, 1, kind, at(("up", 0))[:, kind * GT:(kind + 1) * GT])
                else:
                    name = (("up", u), ("gate_up", u))[kind]
                    free(pe, s, name)
                    last = hidden(2 * u - 2, 2, kind, at(name))
                if kind:
                    last.then_inc(up_mm.sem, 1)

            def spread_weights(s, j):
                free(pe, s, ("cw", j))
                b = at(("cw", j))
                if j == 0:
                    pe.wait_ge(*cwt_lo.at(s.fg, 1))
                for e in range(2):
                    last = mm(b[:, e * GT:(e + 1) * GT], pick[:, 2 * j + e, :], cwT[:, :], start=True, stop=True)
                last.then_inc(cw_mm.sem, 1)

            def down_proj(s, t):
                free(pe, s, ("y", t))
                if t == 0:
                    pe.wait_ge(*hid_lo.at(s.yg, UNITS - 1))
                both, o = at(("y", t))[0:TT, 0:2 * D], at(("y", t))[0:TT, 0:D]
                q = slice(t * TT, (t + 1) * TT)
                order = [E, *range(E)]
                for n, e in enumerate(order):
                    if t == 0 and n == E - 1:
                        pe.wait_ge(*hid_lo.at(s.yg, UNITS))
                    if n:
                        mm(o, hid[1][:, e, q], down[0][:, e, :], start=False, stop=False)
                    last = mm(both, hid[0][:, e, q], down2[:, e, :, :].rearrange("p n d -> p (n d)"), start=n == 0,
                              stop=n == E)
                    if n == 0:
                        mm(o, hid[1][:, e, q], down[0][:, e, :], start=False, stop=False)
                last.then_inc(y_mm.sem, 1)

            def x_transpose(s, name, src, sig, g, ready):
                free(pe, s, (name, 0))
                pe.wait_ge(*ready.at(g, 2))
                o = at((name, 0))
                for t in range(PAIRS):
                    nc.tensor.transpose(o[0:DA, t * TT:(t + 1) * TT], src[:, t, 0:DA], ident[0:TT, 0:TT])
                for t in range(PAIRS):
                    last = nc.tensor.transpose(o[0:DB, GT + t * TT:GT + (t + 1) * TT], src[:, t, DA:D],
                                               ident[0:TT, 0:TT])
                last.then_inc(sig.sem, 1)

            def z_tiles(s, n):
                if n == 0:
                    pe.wait_ge(*x1_lo.at(s.tg, 2))
                    if s.key < 0:
                        pe.wait_ge(p_lo, 16)
                free(pe, s, ("z", n))
                dst = at(("z", n))
                half, kind = Z_TILES[n]
                for e in range(2):
                    hp, tile = (2 * half + kind, e) if kind < 2 else (2 * half + e, 2)
                    w = [q[:, hp, tile, :] for q in (qk_a[0], qk_a[1], qk_b)]
                    o = dst[:, e * GT:(e + 1) * GT]
                    mm(o, w[0], x1_a[0][:, :], start=True, stop=False)
                    mm(o, w[0], x1_a[1][:, :], start=False, stop=False)
                    mm(o, w[1], x1_a[0][:, :], start=False, stop=False)
                    mm(o, w[2], x1_b2[:, :], start=False, stop=False)
                    last = mm(o, w[2][0:DB], x1_blo[:, :], start=False, stop=True)
                last.then_inc(z_mm.sem, 1)

            def weights_transpose(s):
                free(pe, s, ("cwT", 0))
                pe.wait_ge(*g_step.at(s.fg, GATE_STEPS))
                for t in range(PAIRS):
                    last = nc.tensor.transpose(at(("cwT", 0))[0:E, t * TT:(t + 1) * TT], g_cw[:, t, :], ident[0:TT, 0:TT])
                last.then_inc(cwt_mm.sem, 1)

            def score_transpose(s):
                free(pe, s, ("scT", 0))
                pe.wait_ge(*sc.at(s.tg, 1))
                nc.tensor.transpose(at(("scT", 0))[0:GB, 0:S], score[:, :], ident[0:S, 0:S]).then_inc(scT.sem, 1)

            def spread_maxima(s):
                if s.key < 0:
                    pe.wait_ge(p_const, 1)
                free(pe, s, ("band", 0))
                pe.wait_ge(*nmd.at(s.tg, 1))
                o = at(("band", 0))[0:S, 0:GT]
                mm(o, ident_r[:, :], band_mask[:, :], start=True, stop=False)
                mm(o, ones[0:GB, 0:S], max_diag[:, :, :].rearrange("p b q -> p (b q)"), start=False, stop=True)\
                    .then_inc(band_mm.sem, 1)

            def mix_windows(s):
                free(pe, s, ("mix", 0))
                pe.wait_ge(*band_e.at(s.tg, 1))
                for c0, cn, o0 in ((0, DA, 0), (DA, DB, GT)):
                    for b in range(GB):
                        mm(at(("mix", 0))[0:cn, o0 + b * NP:o0 + (b + 1) * NP], xin[:, b, c0:c0 + cn], band[:, b, :],
                           start=True, stop=True)
                for t in range(PAIRS):
                    last = mm(at(("mix", 0))[0:TT, 2 * GT + t:2 * GT + t + 1],
                              band[:, 2 * t:2 * t + 2, :].rearrange("p b q -> p (b q)"), ones[0:S, 0:1],
                              start=True, stop=True)
                last.then_inc(mix_mm.sem, 1)

            def token_proj(s):
                free(pe, s, ("proj", 0))
                pe.wait_ge(*mix_sb.at(s.tg, 2))
                if s.key < 0:
                    pe.wait_ge(d_proj, 32)
                for t in range(PAIRS):
                    o, q = at(("proj", 0))[0:TT, t * D:(t + 1) * D], slice(t * TT, (t + 1) * TT)
                    mm(o, mix_a[:, q], tp_a[:, :], start=True, stop=False)
                    last = mm(o, mix_b[:, q], tp_b[:, :], start=False, stop=True)
                last.then_inc(p_mm2.sem, 1)

            def gate_logits(s):
                free(pe, s, ("gate", 0))
                pe.wait_ge(*x2_lo.at(s.fg, 2))
                if s.key == 1:
                    pe.wait_ge(p_lo, 27)
                for t in range(PAIRS):
                    q = slice(t * TT, (t + 1) * TT)
                    last = split_product(nc.tensor, at(("gate", 0))[0:TT, t * E:(t + 1) * E], x2_a[0][:, q],
                                         x2_a[1][:, q], x2_b2[:, q], x2_blo[:, q], gw_a[0][:, :], gw_a[1][:, :],
                                         gw_b[:, :])
                last.then_inc(g_mm.sem, 1)

            def body(s):
                if s.t:
                    token_scores(s, 0)
                if s.f:
                    x_transpose(s, "x2", xn2, x2_mm, s.fg, xn2_ok)
                if s.a:
                    logits(s, 0)
                if s.y:
                    down_proj(s, 0)
                if s.t:
                    token_scores(s, 1)
                if s.key < 0:
                    products(0, 6)
                if s.a:
                    prob_transpose(s, 0)
                    logits(s, 1)
                if s.f:
                    gate_logits(s)
                if s.a:
                    context(s, 0)
                if s.f:
                    experts(s, 0, 0)
                    experts(s, 0, 1)
                    experts(s, 1, 0)
                if s.t:
                    score_transpose(s)
                if s.key < 0:
                    products(6, 8)
                if s.a:
                    prob_transpose(s, 1)
                    logits(s, 2)
                if s.f:
                    experts(s, 1, 1)
                if s.a:
                    context(s, 1)
                if s.y:
                    down_proj(s, 1)
                if s.t:
                    spread_maxima(s)
                if s.key < 0:
                    products(8, 12)
                if s.a:
                    prob_transpose(s, 2)
                    out_proj(s, 0)
                    logits(s, 3)
                if s.t:
                    mix_windows(s)
                if s.f:
                    experts(s, 2, 0)
                if s.a:
                    context(s, 2)
                if s.t:
                    token_proj(s)
                if s.key < 0:
                    products(12, 16)
                if s.f:
                    experts(s, 2, 1)
                if s.a:
                    prob_transpose(s, 3)
                if s.f:
                    weights_transpose(s)
                    experts(s, 3, 0)
                if s.a:
                    context(s, 3)
                if s.f:
                    spread_weights(s, 0)
                    experts(s, 4, 0)
                    experts(s, 3, 1)
                if s.t:
                    x_transpose(s, "x1", xn1, x1_mm, s.tg, xn1_ok)
                if s.f:
                    spread_weights(s, 1)
                if s.a:
                    out_proj(s, 1)
                if s.f:
                    spread_weights(s, 2)
                if s.t:
                    z_tiles(s, 0)
                    z_tiles(s, 1)
                if s.f:
                    experts(s, 4, 1)
                    spread_weights(s, 3)
                if s.t:
                    for n in range(2, 6):
                        z_tiles(s, n)

            sections(pe, body)

        @block.scalar
        def _(ac):
            def copy(out_, in_, scale=1.0):
                return nc.scalar.activation(out_, in_, ACT.Copy, scale=scale)

            ac.dma_start(rel_raw, rel).then_inc(d_rel, 16)
            ac.dma_start(tw_a[:, :], tok_wT[0:DA, :]).then_inc(d_tok, 16)
            ac.dma_start(tw_b[0:DB, :], tok_wT[DA:D, :]).then_inc(d_tok, 16)
            ac.dma_start(tw_b[DB:DB + 2, :], tok_bias).then_inc(d_tok, 16)
            ac.dma_start(rk[:, :, :], wkT).then_inc(d_qk, 16)
            ac.dma_start(rq[:, :, :], wqT).then_inc(d_qk, 16)
            ac.wait_ge(p_relT, 1)
            copy(rel_sumT[:, 0:2 * NP - 1], bank["s0"][0:H, 0:2 * NP - 1]).then_inc(p_relc, 1)

            def product_highs(first, end):
                for n in range(first, end):
                    k, hp, c0, cn = PRODUCTS[n]
                    src = bank[PREP_BANKS[n % 6]][0:cn, 0:2 * D].rearrange("p (h e) -> p h e", h=2)
                    ac.wait_ge(p_mm, n + 1)
                    hs = slice(2 * hp, 2 * hp + 2)
                    if k == 0:
                        dst = (qk_a[0][:, hp] if c0 == 0 else qk_b[0:DB, hp])
                        copy(dst[:, 0:2, :], src[:, :, 0:DA], DH ** -0.5)
                        copy(dst[:, 2, :].rearrange("p (h e) -> p h e", h=2), src[:, :, DA:D], DH ** -0.5)\
                            .then_inc(p_hi, 1)
                    elif c0 == 0:
                        copy(vo_a[0][:, hs, :], src).then_inc(p_hi, 1)
                    else:
                        copy(vo_b[0][0:DB, hp, :], src[:, 0, :])
                        copy(vo_b[0][DB:2 * DB, hp, :], src[:, 1, :]).then_inc(p_hi, 1)

            def bias_high():
                ac.wait_ge(d_bias, 16)
                copy(bias[0:NP, :, :], bias_raw[:, :, :]).then_inc(p_hi, 1)

            def up_highs(first, end):
                ac.wait_ge(d_up, 128)
                for c in range(first, end):
                    es = slice(3 * c, 3 * c + 3)
                    copy(up_a[0][:, es], r_up_a[:, es]).then_inc(p_hi, 1)
                    copy(up_b[0:DB, es], r_up_b[:, es]).then_inc(p_hi, 1)

            def other_highs():
                ac.wait_ge(d_down, 32)
                for c in range(UP_CHUNKS):
                    es = slice(3 * c, 3 * c + 3)
                    copy(down[0][:, es], r_down[:, es]).then_inc(p_hi, 1)
                ac.wait_ge(d_late, 16 * LATE_LOADS)
                copy(gw_a[0][:, :], gw_raw_a[:, :])
                copy(gw_b[0:DB, :], gw_raw_b[:, :]).then_inc(p_hi, 1)

            def prob_hi(s, j):
                ac.wait_ge(*pt_mm.at(s.ag, j + 1))
                if j:
                    ac.wait_ge(*cb_mm.at(s.ag, j))
                elif s.key > 0:
                    ac.wait_ge(*cb_mm.at(s.ag - 1, GB))
                else:
                    ac.wait_ge(p_fill, 6)
                copy(probT[0:NP, :], bank["probT"][0:NP, 0:H * NP]).then_inc(pt_hi.sem, 1)

            def context_hi(s, j):
                pb = j % 2
                if s.key == 0 and j == 0:
                    ac.wait_ge(p_lo, 23)
                if pb == 0:
                    if j == 2:
                        ac.wait_ge(*o_mm.at(s.ag, j // 2))
                    elif s.key > 0:
                        ac.wait_ge(*o_mm.at(s.ag - 1, 2))
                ac.wait_ge(*ca_mm.at(s.ag, j + 1))
                copy(c_a[0][:, :, pb, :], bank["ca"][:, 0:H * NP].rearrange("p (h q) -> p h q", h=H))\
                    .then_inc(ca_hi.sem, 1)
                ac.wait_ge(*cb_mm.at(s.ag, j + 1))
                src = bank["cb"][0:DB, 0:H * NP].rearrange("p (h two q) -> p h two q", h=HP, two=2)
                for par in range(2):
                    copy(c_b[0][par * DB:(par + 1) * DB, :, pb, :], src[:, :, par, :]).then_inc(cb_hi.sem, 1)

            def hidden_hi(s, j):
                if j:
                    ac.wait_ge(*w_ok.at(s.fg, j))
                else:
                    ac.wait_ge(*v_ok.at(s.fg, 1))
                n, es = unit(j)
                if s.key == 1 and j == 0:
                    ac.wait_ge(p_lo, 27)
                copy(hid[0][:, es, :], act[j % 2][:, 0:n, :]).then_inc(hid_hi.sem, 1)

            def gate_tanh(s, j):
                n = unit(j)[0]
                ac.wait_ge(*up_mm.at(s.fg, j + 1))
                if j >= 2:
                    ac.wait_ge(*hid_lo.at(s.fg, j - 1))
                elif s.key > 1:
                    ac.wait_ge(*hid_lo.at(s.fg - 1, UNITS - j))
                nc.scalar.activation(act[j % 2][:, 0:n, :], at(("up", j))[:, 0:n * GT].rearrange("p (e t) -> p e t", e=n),
                                     ACT.Tanh, scale=0.5).then_inc(tanh_ok.sem, 1)

            def score_tanh(s, m):
                ac.wait_ge(*a_mm.at(s.tg, m + 1))
                if s.key < 0:
                    ac.wait_ge(p_rel, 1)
                elif m == 0:
                    ac.wait_ge(*sc_raw.at(s.tg - 1, 1))
                nc.scalar.activation(tanh_sb[:, 2 * m:2 * m + 2, :],
                                     at(("score", m))[0:S, 0:2 * D].rearrange("p (e d) -> p e d", e=2),
                                     ACT.Tanh)\
                    .then_inc(a_tanh.sem, 1)

            def x_hi(b, sig_mm, sig, g, xa, xb2):
                ac.wait_ge(*sig_mm.at(g, 1))
                copy(xa[0][:, :], b[:, 0:GT]).then_inc(sig.sem, 1)
                copy(xb2[0:DB, :], b[0:DB, GT:2 * GT]).then_inc(sig.sem, 1)
                copy(xb2[DB:2 * DB, :], b[0:DB, GT:2 * GT]).then_inc(sig.sem, 1)

            def z_high(s, n):
                half, kind = Z_TILES[n]
                ac.wait_ge(*z_mm.at(s.tg, n + 1))
                src = at(("z", n))
                if kind < 2:
                    h0 = 4 * half + 2 * kind
                    copy(z_a[0][:, :, h0:h0 + 2, :].rearrange("p b h k -> p h b k"),
                         src[:, 0:2 * GT].rearrange("p (h b k) -> p h b k", h=2, b=GB)).then_inc(z_hi.sem, 1)
                else:
                    for par in range(2):
                        copy(z_b[0:DB, :, 4 * half + par:4 * half + 4:2, :].rearrange("p b h k -> p h b k"),
                             src[par * DB:(par + 1) * DB, 0:2 * GT].rearrange("p (h b k) -> p h b k", h=2, b=GB))\
                            .then_inc(z_hi.sem, 1)

            def prob_exp(s, j):
                ac.wait_ge(*sub_ok.at(s.ag, j + 1))
                nc.scalar.activation(prob[j % 2][:, :, :], prob[j % 2][:, :, :], ACT.Exp).then_inc(exp_ok.sem, 1)

            def norm_halves(s):
                ac.wait_ge(*xn1_ok.at(s.tg, 2))
                if s.key >= 0:
                    ac.wait_ge(*xc_moved.at(s.tg - 1, 96))
                copy(xn_half[0][:, :, :], xn1[:, :, :]).then_inc(xn_hi_ok.sem, 1)

            def body(s):
                if s.t:
                    score_tanh(s, 0)
                if s.f:
                    x_hi(at(("x2", 0)), x2_mm, x2_hi, s.fg, x2_a, x2_b2)
                if s.a:
                    prob_exp(s, 0)
                if s.key == 0:
                    up_highs(0, 2)
                if s.t:
                    score_tanh(s, 1)
                if s.key < 0:
                    product_highs(0, 6)
                if s.a:
                    if s.f:
                        ac.wait_ge(*h2_ok.at(s.fg, 2))
                    ac.wait_ge(*h1_ok.at(s.ag, 2))
                    copy(h1_res[:, :, :], h1[:, :, :]).then_inc(h1_kept.sem, 1)
                if s.a:
                    prob_hi(s, 0)
                    prob_exp(s, 1)
                    if s.key == 0:
                        up_highs(2, UP_CHUNKS)
                    context_hi(s, 0)
                if s.f:
                    ac.wait_ge(*g_mm.at(s.fg, 1))
                    if s.key > 1:
                        ac.wait_ge(*g_step.at(s.fg - 1, 1))
                    nc.scalar.activation(g_tanh[:, :], at(("gate", 0))[0:TT, 0:PAIRS * E], ACT.Tanh, scale=0.5)\
                        .then_inc(g_th.sem, 1)
                    gate_tanh(s, 0)
                if s.a:
                    prob_hi(s, 1)
                    prob_exp(s, 2)
                    if s.key == 0:
                        other_highs()
                if s.f:
                    gate_tanh(s, 1)
                if s.a:
                    context_hi(s, 1)
                if s.f:
                    if s.y:
                        ac.wait_ge(*y_mm.at(s.yg, 2))
                    hidden_hi(s, 0)
                    if s.y:
                        ac.wait_ge(*out_ok.at(s.yg, 2))
                    else:
                        ac.wait_ge(*h2_ok.at(s.fg, 2))
                    copy(h2_res[:, :, :], h2[:, :, :]).then_inc(h2_kept.sem, 1)
                if s.a:
                    prob_hi(s, 2)
                if s.key < 0:
                    product_highs(6, 8)
                if s.t:
                    ac.wait_ge(*band_in.at(s.tg, 1))
                    nc.scalar.activation(band[:, :, :], band[:, :, :], ACT.Exp).then_inc(band_e.sem, 1)
                if s.key < 0:
                    product_highs(8, 12)
                if s.a:
                    prob_exp(s, 3)
                if s.t:
                    ac.wait_ge(*mix_mm.at(s.tg, 1))
                    if s.key >= 0:
                        ac.wait_ge(*p_mm2.at(s.tg - 1, 1))
                    copy(mix_a[:, :], at(("mix", 0))[:, 0:GT]).then_inc(mix_sb.sem, 1)
                    copy(mix_b[:, :], at(("mix", 0))[0:DB, GT:2 * GT]).then_inc(mix_sb.sem, 1)
                if s.a:
                    context_hi(s, 2)
                if s.key < 0:
                    product_highs(12, 16)
                    bias_high()
                if s.a:
                    prob_hi(s, 3)
                if s.f:
                    ac.wait_ge(*cwt_mm.at(s.fg, 1))
                    if s.key > 1:
                        ac.wait_ge(*cw_mm.at(s.fg - 1, HP))
                    else:
                        ac.wait_ge(p_fill, 6)
                    copy(cwT[0:E, :], at(("cwT", 0))[0:E, 0:GT]).then_inc(cwt_hi.sem, 1)
                    gate_tanh(s, 2)
                if s.a:
                    context_hi(s, 3)
                if s.f:
                    hidden_hi(s, 1)
                    gate_tanh(s, 3)
                    hidden_hi(s, 2)
                if s.t:
                    x_hi(at(("x1", 0)), x1_mm, x1_hi, s.tg, x1_a, x1_b2)
                    norm_halves(s)
                    if s.key < 0:
                        ac.wait_ge(p_lo, 16)
                    z_high(s, 0)
                if s.f:
                    hidden_hi(s, 3)
                if s.t:
                    z_high(s, 1)
                if s.f:
                    gate_tanh(s, 4)
                if s.t:
                    for n in range(2, 6):
                        z_high(s, n)
                if s.f:
                    hidden_hi(s, 4)

            sections(ac, body)

        @block.vector
        def _(ve):
            v = nc.vector

            def low(out_, src, hi):
                return v.tensor_tensor(out_, src, hi.bitcast(FP32), ALU.subtract)

            v.memset(ones[:, :], 1.0).then_inc(p_fill, 1)
            v.memset(minus_half[:, :], -0.5).then_inc(p_fill, 1)
            v.memset(xin_b[DB:DB + 2, :], 1.0).then_inc(p_fill, 1)
            v.memset(probT[32:LO, :].bitcast(FP32), 0.0).then_inc(p_fill, 1)
            v.memset(xc_hi[32:LO, :, :].bitcast(FP32), 0.0)
            v.memset(bias[32:LO, :, :].bitcast(FP32), 0.0).then_inc(p_fill, 1)
            v.memset(cwT[:, :].bitcast(FP32), 0.0).then_inc(p_fill, 1)
            ve.wait_ge(d_rel, 16)
            v.tensor_reduce(rel_sum[:, :], rel_raw, axis=AX, op=ALU.add).then_inc(p_rel, 1)
            ve.wait_ge(d_ident, 16)
            v.tensor_copy(ident_r[:, :], ident[0:S, 0:S])
            ve.wait_ge(d_small, 16 * SMALL_LOADS)
            v.tensor_copy(band_mask[:, :], band_raw[:, :]).then_inc(p_const, 1)

            def product_lows(first, end):
                for n in range(first, end):
                    k, hp, c0, cn = PRODUCTS[n]
                    src = bank[PREP_BANKS[n % 6]][0:cn, 0:2 * D].rearrange("p (h e) -> p h e", h=2)
                    ve.wait_ge(p_hi, n + 1)
                    hs = slice(2 * hp, 2 * hp + 2)
                    if k == 0:
                        hi, lo = ((qk_a[0][:, hp], qk_a[1][:, hp]) if c0 == 0 else
                                  (qk_b[0:DB, hp], qk_b[DB:2 * DB, hp]))
                        for o_, i_, h_ in ((lo[:, 0:2, :], src[:, :, 0:DA], hi[:, 0:2, :]),
                                           (lo[:, 2, :].rearrange("p (h e) -> p h e", h=2), src[:, :, DA:D],
                                            hi[:, 2, :].rearrange("p (h e) -> p h e", h=2))):
                            last = v.scalar_tensor_tensor(out=o_, in0=i_, scalar=DH ** -0.5, in1=h_.bitcast(FP32),
                                                          op0=ALU.mult, op1=ALU.subtract)
                        last.then_inc(p_lo, 1)
                    elif c0 == 0:
                        low(vo_a[1][:, hs, :], src, vo_a[0][:, hs, :]).then_inc(p_lo, 1)
                    else:
                        low(vo_b[1][0:DB, hp, :], src[:, 0, :], vo_b[0][0:DB, hp, :])
                        low(vo_b[1][DB:2 * DB, hp, :], src[:, 1, :], vo_b[0][DB:2 * DB, hp, :]).then_inc(p_lo, 1)

            def bias_low():
                ve.wait_ge(p_hi, 17)
                low(bias[LO:KS, :, :], bias_raw[:, :, :], bias[0:NP, :, :]).then_inc(p_lo, 1)
                ve.wait_ge(d_late, 16 * LATE_LOADS)
                v.tensor_copy(flip[:, :], flip_raw[:, :])
                v.tensor_copy(pick[:, :, :], pick_raw[:, :, :]).then_inc(p_const, 1)

            def up_lows(first, end):
                for c in range(first, end):
                    es = slice(3 * c, 3 * c + 3)
                    ve.wait_ge(p_hi, 18 + 2 * c)
                    low(up_a[1][:, es], r_up_a[:, es], up_a[0][:, es]).then_inc(p_lo, 1)
                    ve.wait_ge(p_hi, 19 + 2 * c)
                    low(up_b[DB:2 * DB, es], r_up_b[:, es], up_b[0:DB, es]).then_inc(p_lo, 1)

            def other_lows():
                for c in range(UP_CHUNKS):
                    es = slice(3 * c, 3 * c + 3)
                    ve.wait_ge(p_hi, 24 + c)
                    low(down[1][:, es], r_down[:, es], down[0][:, es]).then_inc(p_lo, 1)
                ve.wait_ge(p_hi, 27)
                low(gw_a[1][:, :], gw_raw_a[:, :], gw_a[0][:, :])
                low(gw_b[DB:2 * DB, :], gw_raw_b[:, :], gw_b[0:DB, :]).then_inc(p_lo, 1)

            def norm_stats(s, g, t, src, st, mv, src_ok, st_ok, mv_ok):
                ve.wait_ge(*src_ok.at(g, t + 1))
                v.bn_stats(st[:, t, :], src[:, t, :]).then_inc(st_ok.sem, 1)
                ve.wait_ge(*st_ok.at(g, t + 1))
                v.memset(wait_cell[:, :], 0.0)
                v.bn_aggr(mv[:, t, :], st[:, t, :]).then_inc(mv_ok.sem, 1)

            def norm_eps(s, g, mv, veps, mv_ok, ve_ok):
                ve.wait_ge(*mv_ok.at(g, 2))
                v.tensor_scalar(veps[:, :], mv[:, :, 1], LN_EPS, None, ALU.add).then_inc(ve_ok.sem, 1)

            def norm_apply(s, g, src, mv, rs, dst, rs_ok, ok):
                ve.wait_ge(*rs_ok.at(g, 1))
                for t in range(PAIRS):
                    v.tensor_scalar(dst[:, t, :], src[:, t, :], mv[:, t, 0:1], rs[:, t:t + 1], ALU.subtract, ALU.mult)\
                        .then_inc(ok.sem, 1)

            def prob_lo(s, j):
                ve.wait_ge(*pt_hi.at(s.ag, j + 1))
                low(probT[LO:KS, :], bank["probT"][0:NP, 0:H * NP], probT[0:NP, :]).then_inc(pt_lo.sem, 1)

            def context_lo(s, j):
                pb = j % 2
                ve.wait_ge(*ca_hi.at(s.ag, j + 1))
                low(c_a[1][:, :, pb, :], bank["ca"][:, 0:H * NP].rearrange("p (h q) -> p h q", h=H),
                    c_a[0][:, :, pb, :]).then_inc(ca_lo.sem, 1)
                ve.wait_ge(*cb_hi.at(s.ag, 2 * j + 2))
                src = bank["cb"][0:DB, 0:H * NP].rearrange("p (h two q) -> p h two q", h=HP, two=2)
                for par in range(2):
                    p = slice(par * DB, (par + 1) * DB)
                    low(c_b[1][p, :, pb, :], src[:, :, par, :], c_b[0][p, :, pb, :]).then_inc(cb_lo.sem, 1)

            def gate_product(s, j):
                n = unit(j)[0]
                a = act[j % 2][:, 0:n, :].rearrange("p e t -> p (e t)")
                ve.wait_ge(*tanh_ok.at(s.fg, j + 1))
                v.scalar_tensor_tensor(out=a, in0=a, scalar=1.0, in1=at(("up", j))[:, 0:n * GT], op0=ALU.add,
                                       op1=ALU.mult).then_inc(u_ok.sem, 1)
                ve.wait_ge(*u_ok.at(s.fg, j + 1))
                other = bank["gate_up"][:, 0:n * GT] if n == 2 else bank["gate_up"][:, GT:2 * GT]
                v.scalar_tensor_tensor(out=a, in0=a, scalar=0.5, in1=other, op0=ALU.mult, op1=ALU.mult)\
                    .then_inc(v_ok.sem, 1)

            def weigh(s, u):
                a = act[u % 2][:, :, :].rearrange("p e t -> p (e t)")
                ve.wait_ge(*v_ok.at(s.fg, u + 1))
                ve.wait_ge(*cw_mm.at(s.fg, u))
                v.tensor_tensor(a, a, at(("cw", u - 1))[:, 0:2 * GT], ALU.mult).then_inc(w_ok.sem, 1)

            def residual(s, t):
                g = s.ag
                ve.wait_ge(*o_mm.at(g, t + 1))
                if t == 0:
                    ve.wait_ge(*h1_kept.at(g, 1))
                    if s.key > 0:
                        ve.wait_ge(*h2_kept.at(g - 1, 1))
                v.tensor_tensor(h2[:, t, :], at(("o", t))[0:TT, 0:D], h1_res[:, t, :], ALU.add).then_inc(h2_part.sem, 1)
                ve.wait_ge(*h2_part.at(g, t + 1))
                v.tensor_tensor(h2[:, t, :], at(("o", t))[0:TT, D:2 * D], h2[:, t, :], ALU.add).then_inc(h2_ok.sem, 1)
                norm_stats(s, g, t, h2, st2, mv2, h2_ok, st2_ok, mv2_ok)

            def emit(s, t):
                ve.wait_ge(*y_mm.at(s.yg, t + 1))
                if t == 0:
                    ve.wait_ge(*h2_kept.at(s.yg, 1))
                    if s.key > 2:
                        ve.wait_ge(*out_sent.at(s.yg - 1, 16))
                v.tensor_tensor(out_sb[:, t, :], at(("y", t))[0:TT, 0:D], h2_res[:, t, :], ALU.add)\
                    .then_inc(out_part.sem, 1)
                ve.wait_ge(*out_part.at(s.yg, t + 1))
                v.tensor_tensor(out_sb[:, t, :], at(("y", t))[0:TT, D:2 * D], out_sb[:, t, :], ALU.add)\
                    .then_inc(out_ok.sem, 1)

            def x_low(b, sig_hi, sig, g, xa, xb2, xblo):
                ve.wait_ge(*sig_hi.at(g, 3))
                low(xa[1][:, :], b[:, 0:GT], xa[0][:, :]).then_inc(sig.sem, 1)
                low(xblo[:, :], b[0:DB, GT:2 * GT], xb2[0:DB, :]).then_inc(sig.sem, 1)

            def z_low(s, n):
                half, kind = Z_TILES[n]
                src = at(("z", n))
                ve.wait_ge(*z_hi.at(s.tg, USES["z", n][3]))
                if kind < 2:
                    h0 = 4 * half + 2 * kind
                    low(z_a[1][:, :, h0:h0 + 2, :].rearrange("p b h k -> p h b k"),
                        src[:, 0:2 * GT].rearrange("p (h b k) -> p h b k", h=2, b=GB),
                        z_a[0][:, :, h0:h0 + 2, :].rearrange("p b h k -> p h b k")).then_inc(z_lo.sem, 1)
                else:
                    for par in range(2):
                        hs = slice(4 * half + par, 4 * half + 4, 2)
                        low(z_b[DB:2 * DB, :, hs, :].rearrange("p b h k -> p h b k"),
                            src[par * DB:(par + 1) * DB, 0:2 * GT].rearrange("p (h b k) -> p h b k", h=2, b=GB),
                            z_b[0:DB, :, hs, :].rearrange("p b h k -> p h b k")).then_inc(z_lo.sem, 1)

            def choose_steps(s):
                g = s.fg
                pairs = g_sb[:, :, :].rearrange("p t (g two) -> p t g two", two=2)
                masked = g_msk[:, :, :].rearrange("p t (g two) -> p t g two", two=2)

                def after(k):
                    if k == 0:
                        ve.wait_ge(*g_th.at(g, 1))
                    else:
                        ve.wait_ge(*g_step.at(g, k))

                def rank(k, val, cmp, eq, below, res, m):
                    vj = val[:, :, :].unsqueeze(2).to_broadcast([TT, PAIRS, m, m])
                    vi = val[:, :, :].unsqueeze(3).to_broadcast([TT, PAIRS, m, m])
                    c4, e4 = (q[:, :, :].rearrange("p t (i j) -> p t i j", i=m) for q in (cmp, eq))
                    lo = below[:, :].unsqueeze(1).to_broadcast([TT, PAIRS, m * m])
                    after(k)
                    v.tensor_tensor(c4, vj, vi, ALU.is_gt).then_inc(g_step.sem, 1)
                    yield
                    after(k + 1)
                    v.tensor_tensor(e4, vj, vi, ALU.is_equal).then_inc(g_step.sem, 1)
                    yield
                    after(k + 2)
                    v.tensor_tensor(eq[:, :, :], eq[:, :, :], lo, ALU.mult).then_inc(g_step.sem, 1)
                    yield
                    after(k + 3)
                    v.tensor_tensor(cmp[:, :, :], cmp[:, :, :], eq[:, :, :], ALU.add).then_inc(g_step.sem, 1)
                    yield
                    after(k + 4)
                    v.tensor_reduce(res[:, :, :], c4, axis=AX, op=ALU.add).then_inc(g_step.sem, 1)
                    yield

                after(0)
                v.tensor_scalar(g_sig[:, :, :].rearrange("p t e -> p (t e)"), g_tanh[:, :], 0.5, 0.5, ALU.mult, ALU.add)\
                    .then_inc(g_step.sem, 1)
                yield
                after(1)
                v.tensor_tensor(g_sb[:, :, :], g_sig[:, :, :], gb_row[:, :].unsqueeze(1).to_broadcast([TT, PAIRS, E]),
                                ALU.add).then_inc(g_step.sem, 1)
                yield
                after(2)
                v.tensor_tensor(g_grp[:, :, :], pairs[:, :, :, 0], pairs[:, :, :, 1], ALU.add).then_inc(g_step.sem, 1)
                yield
                yield from rank(3, g_grp, g_cmp4, g_eq4, lt4, g_rank4, 4)
                after(8)
                v.tensor_scalar(g_sel4[:, :, :], g_rank4[:, :, :], 2.0, 2 * BIG, ALU.is_lt, ALU.mult)\
                    .then_inc(g_step.sem, 1)
                yield
                after(9)
                v.tensor_scalar(g_sel4[:, :, :], g_sel4[:, :, :], BIG, None, ALU.subtract).then_inc(g_step.sem, 1)
                yield
                after(10)
                v.tensor_tensor(masked, pairs, g_sel4[:, :, :].unsqueeze(3).to_broadcast([TT, PAIRS, 4, 2]), ALU.min)\
                    .then_inc(g_step.sem, 1)
                yield
                yield from rank(11, g_msk, g_cmp8, g_eq8, lt8, g_rank8, 8)
                after(16)
                v.scalar_tensor_tensor(out=g_w[:, :, :], in0=g_rank8[:, :, :], scalar=2.0, in1=g_sig[:, :, :],
                                       op0=ALU.is_lt, op1=ALU.mult).then_inc(g_step.sem, 1)
                yield
                after(17)
                v.tensor_reduce(g_sum[:, :], g_w[:, :, :], axis=AX, op=ALU.add).then_inc(g_step.sem, 1)
                yield
                after(18)
                v.tensor_scalar(g_sum[:, :], g_sum[:, :], 1e-6, None, ALU.add).then_inc(g_step.sem, 1)
                yield
                after(19)
                v.reciprocal(g_rec[:, :], g_sum[:, :]).then_inc(g_step.sem, 1)
                yield
                after(20)
                if s.key > 1:
                    ve.wait_ge(*cwt_mm.at(g - 1, 1))
                v.tensor_tensor(g_cw[:, :, :], g_w[:, :, :], g_rec[:, :].unsqueeze(2).to_broadcast([TT, PAIRS, E]),
                                ALU.mult).then_inc(g_step.sem, 1)
                yield

            def logit_max(s, j):
                lg = bank["logit"][0:NP, 0:H * NP].rearrange("p (h k) -> p h k", h=H)
                ve.wait_ge(*l_mm.at(s.ag, j + 1))
                v.tensor_reduce(row_max[:, :], lg, axis=AX, op=ALU.max).then_inc(mx_ok.sem, 1)
                ve.wait_ge(*mx_ok.at(s.ag, j + 1))
                if j >= 2:
                    ve.wait_ge(*pt_mm.at(s.ag, j - 1))
                elif s.key > 0:
                    ve.wait_ge(*pt_mm.at(s.ag - 1, j + 3))
                v.tensor_tensor(prob[j % 2][:, :, :], lg, row_max[:, :].unsqueeze(2).to_broadcast([NP, H, NP]),
                                ALU.subtract).then_inc(sub_ok.sem, 1)

            def prob_sum(s, j):
                ve.wait_ge(*exp_ok.at(s.ag, j + 1))
                v.tensor_reduce(row_sum[:, :], prob[j % 2][:, :, :], axis=AX, op=ALU.add).then_inc(sum_ok.sem, 1)
                ve.wait_ge(*sum_ok.at(s.ag, j + 1))
                if j:
                    ve.wait_ge(*pn_ok.at(s.ag, j))
                elif s.key > 0:
                    ve.wait_ge(*pn_ok.at(s.ag - 1, GB))
                v.reciprocal(row_rec[:, :], row_sum[:, :]).then_inc(rec_ok.sem, 1)
                if j in NORM_ON_VECTOR:
                    ve.wait_ge(*rec_ok.at(s.ag, j + 1))
                    q = prob[j % 2][:, :, :]
                    v.tensor_tensor(q, q, row_rec[:, :].unsqueeze(2).to_broadcast([NP, H, NP]), ALU.mult)\
                        .then_inc(pn_ok.sem, 1)

            def score_sum(s):
                ve.wait_ge(*av.at(s.tg, 1))
                v.tensor_reduce(score_raw[:, :], tanh_sb[:, :, :], axis=AX, op=ALU.add).then_inc(sc_raw.sem, 1)
                ve.wait_ge(*sc_raw.at(s.tg, 1))
                v.tensor_scalar(score[:, :], score_raw[:, :], vb_col[:, 0:1], None, ALU.add).then_inc(sc.sem, 1)

            def window_max(s):
                ve.wait_ge(*scT.at(s.tg, 1))
                win = bass.AP(at(("scT", 0)), 0, [[512, GB], [2, NP], [1, 4]])
                v.tensor_reduce(neg_max[:, :], win, axis=AX, op=ALU.max, negate=True).then_inc(nm.sem, 1)
                ve.wait_ge(*nm.at(s.tg, 1))
                v.tensor_tensor(max_diag[:, :, :], diag_mask[:, :, :],
                                neg_max[:, :].unsqueeze(1).to_broadcast([GB, GB, NP]), ALU.mult).then_inc(nmd.sem, 1)

            def band_exponent(s):
                ve.wait_ge(*band_mm.at(s.tg, 1))
                v.tensor_tensor(band[:, :, :], at(("band", 0))[0:S, 0:GT].rearrange("p (b q) -> p b q", b=GB),
                                score[:, :].unsqueeze(2).to_broadcast([S, GB, NP]), ALU.add).then_inc(band_in.sem, 1)

            def body(s):
                steps = choose_steps(s) if s.f else iter(())

                def gate(n):
                    for _ in range(n):
                        next(steps, None)

                if s.f:
                    x_low(at(("x2", 0)), x2_hi, x2_lo, s.fg, x2_a, x2_b2, x2_blo)
                if s.a:
                    logit_max(s, 0)
                if s.a:
                    prob_sum(s, 0)
                if s.key == 0:
                    up_lows(0, 1)
                if s.y:
                    emit(s, 0)
                if s.a:
                    prob_lo(s, 0)
                    logit_max(s, 1)
                if s.key < 0:
                    product_lows(0, 4)
                if s.key == 0:
                    up_lows(1, 2)
                if s.t:
                    score_sum(s)
                if s.key < 0:
                    product_lows(4, 6)
                if s.a:
                    prob_sum(s, 1)
                if s.key == 0:
                    up_lows(2, UP_CHUNKS)
                if s.f:
                    gate_product(s, 0)
                if s.a:
                    context_lo(s, 0)
                gate(1)
                if s.a:
                    prob_lo(s, 1)
                gate(1)
                if s.a:
                    logit_max(s, 2)
                gate(2)
                if s.t:
                    window_max(s)
                if s.key < 0:
                    product_lows(6, 8)
                gate(1)
                if s.a:
                    prob_sum(s, 2)
                gate(2)
                if s.a:
                    context_lo(s, 1)
                if s.f:
                    gate_product(s, 1)
                gate(1)
                if s.y:
                    emit(s, 1)
                if s.key == 0:
                    other_lows()
                gate(2)
                if s.t:
                    band_exponent(s)
                if s.key < 0:
                    product_lows(8, 12)
                gate(2)
                if s.a:
                    prob_lo(s, 2)
                gate(1)
                gate(2)
                if s.a:
                    logit_max(s, 3)
                gate(2)
                if s.a:
                    residual(s, 0)
                if s.t:
                    ve.wait_ge(*mix_sb.at(s.tg, 2))
                    v.reciprocal(band_rden[:, :], at(("mix", 0))[0:TT, 2 * GT:2 * GT + PAIRS]).then_inc(rden.sem, 1)
                if s.a:
                    prob_sum(s, 3)
                gate(2)
                if s.a:
                    context_lo(s, 2)
                gate(GATE_STEPS)
                if s.t:
                    ve.wait_ge(*p_mm2.at(s.tg, 1))
                    ve.wait_ge(*rden.at(s.tg, 1))
                    if s.key >= 0:
                        ve.wait_ge(*h1_kept.at(s.tg - 1, 1))
                    for t in range(PAIRS):
                        v.scalar_tensor_tensor(out=h1[:, t, :], in0=at(("proj", 0))[0:TT, t * D:(t + 1) * D],
                                               scalar=band_rden[:, t:t + 1], in1=pb_row[:, :], op0=ALU.mult,
                                               op1=ALU.add).then_inc(h1_ok.sem, 1)
                if s.t:
                    for t in range(PAIRS):
                        norm_stats(s, s.tg, t, h1, st1, mv1, h1_ok, st1_ok, mv1_ok)
                    norm_eps(s, s.tg, mv1, ve1, mv1_ok, ve1_ok)
                if s.key < 0:
                    product_lows(12, 13)
                if s.a:
                    prob_lo(s, 3)
                if s.f:
                    ve.wait_ge(*cwt_hi.at(s.fg, 1))
                    low(cwT[32:32 + E, :], at(("cwT", 0))[0:E, 0:GT], cwT[0:E, :]).then_inc(cwt_lo.sem, 1)
                    gate_product(s, 2)
                if s.t:
                    if s.key >= 0:
                        ve.wait_ge(*xn_lo_ok.at(s.tg - 1, 1))
                        ve.wait_ge(*xn_hi_ok.at(s.tg - 1, 1))
                    norm_apply(s, s.tg, h1, mv1, rs1, xn1, rs1_ok, xn1_ok)
                if s.key < 0:
                    product_lows(13, 16)
                if s.f:
                    weigh(s, 1)
                if s.a:
                    context_lo(s, 3)
                if s.f:
                    weigh(s, 2)
                    gate_product(s, 3)
                if s.t:
                    x_low(at(("x1", 0)), x1_hi, x1_lo, s.tg, x1_a, x1_b2, x1_blo)
                if s.a:
                    residual(s, 1)
                    norm_eps(s, s.ag, mv2, ve2, mv2_ok, ve2_ok)
                if s.f:
                    weigh(s, 3)
                if s.t:
                    z_low(s, 0)
                    if s.key < 0:
                        bias_low()
                    z_low(s, 1)
                if s.f:
                    gate_product(s, 4)
                    weigh(s, 4)
                if s.t:
                    z_low(s, 2)
                    z_low(s, 3)
                if s.a:
                    norm_apply(s, s.ag, h2, mv2, rs2, xn2, rs2_ok, xn2_ok)
                if s.t:
                    z_low(s, 4)
                    z_low(s, 5)

            sections(ve, body)

        @block.gpsimd
        def _(po):
            p = nc.gpsimd
            for dst, src in ((flip_raw[:, :], c_flip), (pick_raw[:, :, :], c_pick),
                             (lt4[:, :], c_lt4.partition_broadcast(TT)), (lt8[:, :], c_lt8.partition_broadcast(TT)),
                             (gb_row[:, :], gate_b.partition_broadcast(TT)),
                             (gw_raw_a[:, :], gate_w[0:DA, :]), (gw_raw_b[:, :], gate_w[DA:D, :])):
                po.dma_start(dst, src).then_inc(d_late, 16)
            po.wait_ge(d_small, 16 * SMALL_LOADS)

            def inv_sqrt(g, ve_ok, veps, rs, ok):
                po.wait_ge(*ve_ok.at(g, 1))
                p.tensor_tensor(rs[:, :], veps[:, :], minus_half[:, :], ALU.pow).then_inc(ok.sem, 1)

            def hidden_lo(s, j):
                n, es = unit(j)
                po.wait_ge(*hid_hi.at(s.fg, j + 1))
                p.tensor_tensor(hid[1][:, es, :], act[j % 2][:, 0:n, :], hid[0][:, es, :].bitcast(FP32),
                                ALU.subtract).then_inc(hid_lo.sem, 1)

            def body(s):
                for j in range(GB):
                    if s.a and j not in NORM_ON_VECTOR:
                        po.wait_ge(*rec_ok.at(s.ag, j + 1))
                        q = prob[j % 2][:, :, :]
                        p.tensor_tensor(q, q, row_rec[:, :].unsqueeze(2).to_broadcast([NP, H, NP]), ALU.mult)\
                            .then_inc(pn_ok.sem, 1)
                    if s.t and j == 0:
                        po.wait_ge(*a_tanh.at(s.tg, 2))
                        p.tensor_tensor(tanh_sb[:, :, :], tanh_sb[:, :, :],
                                        v_row[:, :].unsqueeze(1).to_broadcast([S, GB, D]), ALU.mult).then_inc(av.sem, 1)
                    if s.f and j == 2:
                        hidden_lo(s, 0)
                if s.t:
                    inv_sqrt(s.tg, ve1_ok, ve1, rs1, rs1_ok)
                if s.f:
                    hidden_lo(s, 1)
                    hidden_lo(s, 2)
                if s.a:
                    inv_sqrt(s.ag, ve2_ok, ve2, rs2, rs2_ok)
                if s.t:
                    po.wait_ge(*xn_hi_ok.at(s.tg, 1))
                    if s.key >= 0:
                        po.wait_ge(*xc_moved.at(s.tg - 1, 96))
                    p.tensor_tensor(xn_half[1][:, :, :], xn1[:, :, :], xn_half[0][:, :, :].bitcast(FP32), ALU.subtract)\
                        .then_inc(xn_lo_ok.sem, 1)
                if s.f:
                    hidden_lo(s, 3)
                    hidden_lo(s, 4)

            sections(po, body)


def kernel(x, L0_tok_W_w, L0_tok_W_b, L0_tok_b, L0_tok_V_w, L0_tok_V_b, L0_tok_P_w, L0_tok_P_b, L0_attn_w_q,
           L0_attn_w_k, L0_attn_w_v, L0_attn_w_o, L0_attn_rel_emb, L0_ffn_gate_weight, L0_ffn_gate_bias, L0_ffn_w1,
           L0_ffn_w2, L0_ffn_w3, L0_ffn_sw1, L0_ffn_sw2, L0_ffn_sw3):
    import numpy as np
    import concourse.bacc as bacc
    from concourse.bass_utils import run_bass_kernel_spmd

    def put(a):
        return np.ascontiguousarray(np.asarray(a))

    x = put(x)
    n = np.arange
    ident = np.eye(128, dtype=np.float32)
    off = n(S)[:, None] - 2 * n(NP)[None, :]
    band = np.where((off >= 0) & (off < 4), 0.0, -1e30).astype(np.float32)
    diag = np.repeat(np.eye(GB, dtype=np.float32)[:, :, None], NP, axis=2)
    flip = np.zeros((KS, NP), np.float32)
    flip[n(NP), NP - 1 - n(NP)] = 1.0
    flip[LO + n(NP), NP - 1 - n(NP)] = 1.0
    pick = np.zeros((40, E, 128), np.float32)
    pick[n(E), n(E), :] = 1.0
    pick[32 + n(E), n(E), :] = 1.0
    below = lambda m: (n(m)[None, :] < n(m)[:, None]).astype(np.float32).reshape(-1)
    arrays = {
        "x": x, "xT": put(x.reshape(B * S, D).T),
        "tok_wT": put(np.asarray(L0_tok_W_w).T), "tok_bias": put(np.stack([np.asarray(L0_tok_W_b), np.asarray(L0_tok_b)])),
        "tok_v": put(np.asarray(L0_tok_V_w).reshape(D)), "tok_vb": put(L0_tok_V_b),
        "tok_pT": put(np.asarray(L0_tok_P_w).T), "tok_pb": put(L0_tok_P_b),
        "wqT": put(np.asarray(L0_attn_w_q).transpose(2, 0, 1)), "wkT": put(np.asarray(L0_attn_w_k).transpose(2, 0, 1)),
        "wvT": put(np.asarray(L0_attn_w_v).transpose(2, 0, 1)), "wo": put(np.asarray(L0_attn_w_o).transpose(1, 0, 2)),
        "rel": put(np.asarray(L0_attn_rel_emb)[:, 100 - NP:100 + NP - 1, :, 0].transpose(1, 0, 2)),
        "gate_w": put(np.asarray(L0_ffn_gate_weight).T), "gate_b": put(L0_ffn_gate_bias),
        "w1T": put(np.asarray(L0_ffn_w1).transpose(2, 0, 1)), "w3T": put(np.asarray(L0_ffn_w3).transpose(2, 0, 1)),
        "w2T": put(np.asarray(L0_ffn_w2).transpose(2, 0, 1)),
        "sw1T": put(np.asarray(L0_ffn_sw1).T), "sw3T": put(np.asarray(L0_ffn_sw3).T), "sw2T": put(np.asarray(L0_ffn_sw2).T),
        "c_ident": ident, "c_band": put(np.tile(band, (1, GB))), "c_diag": put(diag), "c_flip": flip, "c_pick": pick,
        "c_lt4": put(below(4)), "c_lt8": put(below(8)),
    }
    nc = bacc.Bacc("TRN2", target_bir_lowering=False, num_devices=1)
    feeds, args = {}, []
    for name, a in arrays.items():
        feeds[f"in_{name}"] = a
        args.append(nc.dram_tensor(f"in_{name}", a.shape, mybir.dt.from_np(a.dtype), kind="ExternalInput").ap())
    out = nc.dram_tensor("out", (B, NP, D), FP32, kind="ExternalOutput").ap()
    audio_tower_kernel(nc, *args, out)
    return run_bass_kernel_spmd(nc, [feeds], core_ids=[0]).results[0]["out"]
```
